# Optimizing a Trainium2 kernel written in Bass

```python
import numpy as np
import jax
import jax.numpy as jnp

def _softmax(x, axis=-1):
    return jax.nn.softmax(x, axis=axis)

def _gelu(x):
    return jax.nn.gelu(x, approximate=True)

def _silu(x):
    return jax.nn.silu(x)

def _sigmoid(x):
    return jax.nn.sigmoid(x)

def _layernorm(x, axis=-1, eps=1e-05):
    m = jnp.mean(x, axis=axis, keepdims=True)
    v = jnp.var(x, axis=axis, keepdims=True)
    return (x - m) / jnp.sqrt(v + eps)

def _scatter_add(tgt, idx, src, axis=0):
    return tgt.at[idx].add(src)

def _segment_sum(src, seg, n):
    return jax.ops.segment_sum(src, seg, n)
kernel_name = 'mk_perceiver_d2_seqx_r4_979069'

def setup_inputs(seed: int=0):
    np.random.seed(seed)
    _w = jnp.asarray

    def _rec_inputs():
        import jax
        import jax.numpy as jnp
        _rk = jax.random.key(seed)
        x = -0.0003929 + 0.9999 * jax.random.normal(jax.random.fold_in(_rk, 1), (1, 256, 256), jnp.float32)
        _lenS = 256 - jax.random.randint(jax.random.fold_in(_rk, 7), (1,), 0, max(1, 256 // 4) + 1, jnp.int32)
        _lenS2 = 4096 - jax.random.randint(jax.random.fold_in(_rk, 8), (1,), 0, max(1, 4096 // 4) + 1, jnp.int32)
        _ctx_768P = jax.random.normal(jax.random.fold_in(_rk, 11), (1, 16, 192), jnp.float32)
        _ctx_768c = jax.random.dirichlet(jax.random.fold_in(_rk, 511), 0.3 * jnp.ones((16,), jnp.float32), (1, 4096))
        _ctx_768t = jnp.einsum('bsk,bkd->bsd', _ctx_768c, _ctx_768P)
        _ctx_768t = _ctx_768t * jax.lax.rsqrt(jnp.mean(jnp.square(_ctx_768t)) + 1e-12) * 0.953939
        ctx_768 = 0.00095986 + 0.999812 * (_ctx_768t + 0.3 * jax.random.normal(jax.random.fold_in(_rk, 611), (1, 4096, 192), jnp.float32))
        _validS = jnp.arange(256)[None, :] < _lenS[:, None]
        _validS2 = jnp.arange(4096)[None, :] < _lenS2[:, None]
        _causal = jnp.tril(jnp.ones((256, 256), dtype=bool))
        mask_BxS2_bf1 = jnp.ones((1, 4096), dtype=bool)
        mask_BxS_bf1 = jnp.ones((1, 256), dtype=bool)
        return (x, ctx_768, mask_BxS2_bf1, mask_BxS_bf1)
    x, ctx_768, mask_BxS2_bf1, mask_BxS_bf1 = _rec_inputs()

    def _L0_xattn_setup():
        import jax, jax.numpy as jnp
        import numpy as np
        DIM = 256
        CTX_DIM = 192
        HEADS = 16
        key = jax.random.key(seed)
        ks = jax.random.split(key, 7)
        B, N, M = (4, 1024, 64)
        x = jax.random.normal(ks[0], (B, N, DIM), dtype=jnp.float32)
        context = jax.random.normal(ks[1], (B, M, CTX_DIM), dtype=jnp.float32)
        context_mask = jnp.ones((B, M), dtype=bool)
        s_d = 1.0 / np.sqrt(DIM)
        s_c = 1.0 / np.sqrt(CTX_DIM)
        Wq = jax.random.normal(ks[2], (DIM, DIM), dtype=jnp.float32) * s_d
        Wk = jax.random.normal(ks[3], (CTX_DIM, DIM), dtype=jnp.float32) * s_c
        Wv = jax.random.normal(ks[4], (CTX_DIM, DIM), dtype=jnp.float32) * s_c
        Wo = jax.random.normal(ks[5], (DIM, DIM), dtype=jnp.float32) * s_d
        return {'x': x, 'context': context, 'context_mask': context_mask, 'Wq': Wq, 'Wk': Wk, 'Wv': Wv, 'Wo': Wo}
    _L0_xattn_all = _L0_xattn_setup()
    _L0_xattn_in = {k: v for k, v in _L0_xattn_all.items() if k in ('Wq', 'Wk', 'Wv', 'Wo')}
    del _L0_xattn_all

    def _L0_attn_setup():
        import jax, jax.numpy as jnp
        import numpy as np
        D_MODEL = 256
        NUM_HEADS = 16
        D_K = D_MODEL // NUM_HEADS
        key = jax.random.key(seed)
        k1, k2, k3, k4, k5 = jax.random.split(key, 5)
        scale = 1.0 / np.sqrt(D_MODEL)
        x = jax.random.normal(k1, (2, 2048, D_MODEL), dtype=jnp.float32)
        W_qkv = jax.random.normal(k2, (D_MODEL, 3 * D_MODEL), dtype=jnp.float32) * scale
        b_qkv = jax.random.normal(k3, (3 * D_MODEL,), dtype=jnp.float32) * 0.01
        W_out = jax.random.normal(k4, (D_MODEL, D_MODEL), dtype=jnp.float32) * scale
        b_out = jax.random.normal(k5, (D_MODEL,), dtype=jnp.float32) * 0.01
        return {'x': x, 'W_qkv': W_qkv, 'b_qkv': b_qkv, 'W_out': W_out, 'b_out': b_out}
    _L0_attn_all = _L0_attn_setup()
    _L0_attn_in = {k: v for k, v in _L0_attn_all.items() if k in ('W_qkv', 'b_qkv', 'W_out', 'b_out')}
    del _L0_attn_all

    def _L0_ffn_setup():
        import jax, jax.numpy as jnp
        import numpy as np
        QMAX = 127.0

        def _ste_round(v):
            return v + jax.lax.stop_gradient(jnp.round(v) - v)

        def _act_fake_quant(x, clip_factor):
            scale = jax.nn.sigmoid(clip_factor) * jnp.max(jnp.abs(x)) / QMAX
            return jnp.clip(_ste_round(x / scale), -QMAX - 1.0, QMAX) * scale

        def _weight_fake_quant(w):
            scale = jnp.max(jnp.abs(w), axis=1, keepdims=True) / QMAX
            return jnp.clip(_ste_round(w / scale), -QMAX - 1.0, QMAX) * scale
        key = jax.random.key(seed)
        k1, k2, k3, k4 = jax.random.split(key, 4)
        B, S, H, I = (8, 2048, 256, 704)
        return {'x': jax.random.normal(k1, (B, S, H), dtype=jnp.float32), 'clip_x': jnp.full((1,), 4.0, dtype=jnp.float32), 'clip_down': jnp.full((1,), 4.0, dtype=jnp.float32), 'w_gate': jax.random.normal(k2, (I, H), dtype=jnp.float32) * 0.02, 'w_up': jax.random.normal(k3, (I, H), dtype=jnp.float32) * 0.02, 'w_down': jax.random.normal(k4, (H, I), dtype=jnp.float32) * 0.02}
    _L0_ffn_all = _L0_ffn_setup()
    _L0_ffn_in = {k: v for k, v in _L0_ffn_all.items() if k in ('clip_x', 'clip_down', 'w_gate', 'w_up', 'w_down')}
    del _L0_ffn_all

    def _L1_xattn_setup():
        import jax, jax.numpy as jnp
        import numpy as np
        B, T, DT, G, DV = (16, 128, 256, 144, 192)
        H, DH = (4, 32)
        INNER = H * DH
        HID = 4 * DT
        N_STATE = 64
        K_TOP = 32

        def layernorm(x, g, b, eps=1e-05):
            m = x.mean(-1, keepdims=True)
            v = x.var(-1, keepdims=True)
            return (x - m) * jax.lax.rsqrt(v + eps) * g + b

        def s4d(x, log_dt, A_re, A_im, C_re, C_im, D_skip):
            Bb, L, D = x.shape
            dt = jnp.exp(log_dt)
            A = A_re + 1j * A_im
            C = C_re + 1j * C_im
            dtA = dt[:, None] * A
            dC = C * (jnp.exp(dtA) - 1.0) / A
            powers = jnp.exp(dtA[:, :, None] * jnp.arange(L))
            K = 2.0 * jnp.einsum('dn,dnl->dl', dC, powers).real
            n = 2 * L
            Kf = jnp.fft.rfft(K, n=n, axis=-1)
            xf = jnp.fft.rfft(x, n=n, axis=1)
            y = jnp.fft.irfft(xf * Kf.T[None], n=n, axis=1)[:, :L]
            return y + x * D_skip
        key = jax.random.key(seed)
        ks = jax.random.split(key, 16)
        s = 0.02
        inp = {'x_text': jax.random.normal(ks[0], (B, T, DT), jnp.float32), 'x_vision': jax.random.normal(ks[1], (B, G, DV), jnp.float32), 'text_mask': jnp.ones((B, T), bool), 'vision_mask': jnp.ones((B, G), bool), 'Wq': jax.random.normal(ks[2], (DT, INNER), jnp.float32) * s, 'Wk': jax.random.normal(ks[3], (DV, INNER), jnp.float32) * s, 'Wv': jax.random.normal(ks[4], (DV, DT), jnp.float32) * s, 'W_film_in': jax.random.normal(ks[5], (DT, 2 * DT), jnp.float32) * s, 'b_film_in': jnp.zeros((2 * DT,), jnp.float32), 'W_film_out': jax.random.normal(ks[6], (DT, 2 * DT), jnp.float32) * s, 'b_film_out': jnp.zeros((2 * DT,), jnp.float32), 'g_norm_in': jnp.ones((DT,), jnp.float32), 'b_norm_in': jnp.zeros((DT,), jnp.float32), 'g_norm_out': jnp.ones((DT,), jnp.float32), 'b_norm_out': jnp.zeros((DT,), jnp.float32), 'g_ffn': jnp.ones((DT,), jnp.float32), 'b_ffn': jnp.zeros((DT,), jnp.float32), 'W1': jax.random.normal(ks[7], (DT, HID), jnp.float32) * s, 'b1': jnp.zeros((HID,), jnp.float32), 'W2': jax.random.normal(ks[8], (HID, DT), jnp.float32) * s, 'b2': jnp.zeros((DT,), jnp.float32), 'log_dt': jnp.log(0.001) + jax.random.uniform(ks[9], (DT,), jnp.float32) * (jnp.log(0.1) - jnp.log(0.001)), 'A_re': -0.5 * jnp.ones((DT, N_STATE), jnp.float32), 'A_im': jnp.tile(jnp.pi * jnp.arange(N_STATE, dtype=jnp.float32), (DT, 1)), 'C_re': jax.random.normal(ks[10], (DT, N_STATE), jnp.float32) * 0.5 ** 0.5, 'C_im': jax.random.normal(ks[11], (DT, N_STATE), jnp.float32) * 0.5 ** 0.5, 'D_skip': jax.random.normal(ks[12], (DT,), jnp.float32), 'mod_gate': jnp.array(0.5, jnp.float32)}
        return inp
    _L1_xattn_all = _L1_xattn_setup()
    _L1_xattn_in = {k: v for k, v in _L1_xattn_all.items() if k in ('Wq', 'Wk', 'Wv', 'W_film_in', 'b_film_in', 'W_film_out', 'b_film_out', 'g_norm_in', 'b_norm_in', 'g_norm_out', 'b_norm_out', 'g_ffn', 'b_ffn', 'W1', 'b1', 'W2', 'b2', 'log_dt', 'A_re', 'A_im', 'C_re', 'C_im', 'D_skip', 'mod_gate')}
    del _L1_xattn_all

    def _L1_attn_setup():
        import jax, jax.numpy as jnp
        import numpy as np
        B, L, D = (4, 2048, 256)

        def _mingru_scan(gates, candidates):

            def combine(e1, e2):
                a1, b1 = e1
                a2, b2 = e2
                return (a2 * a1, a2 * b1 + b2)
            _, h = jax.lax.associative_scan(combine, (gates, candidates), axis=1)
            return h
        key = jax.random.key(seed)
        kx, kg, kc = jax.random.split(key, 3)
        scale = 1.0 / np.sqrt(D)
        return {'x': jax.random.normal(kx, (B, L, D), dtype=jnp.float32), 'Wg': jax.random.normal(kg, (D, D), dtype=jnp.float32) * scale, 'bg': jnp.ones((D,), dtype=jnp.float32), 'Wc': jax.random.normal(kc, (D, D), dtype=jnp.float32) * scale, 'bc': jnp.zeros((D,), dtype=jnp.float32)}
    _L1_attn_all = _L1_attn_setup()
    _L1_attn_in = {k: v for k, v in _L1_attn_all.items() if k in ('Wg', 'bg', 'Wc', 'bc')}
    del _L1_attn_all

    def _L1_ffn_setup():
        import jax, jax.numpy as jnp
        import numpy as np
        E, K, H, I, SI = (32, 8, 256, 128, 512)
        CAP = 512
        LIMIT = 7.0
        SCALE = 2.5
        B, S = (2, 512)
        key = jax.random.key(seed)
        ks = jax.random.split(key, 8)
        s = 0.02
        return {'hidden_states': jax.random.normal(ks[0], (B, S, H), jnp.float32), 'router_weight': jax.random.normal(ks[1], (E, H), jnp.float32) * s, 'e_score_correction_bias': jnp.zeros((E,), jnp.float32), 'gate_up_proj': jax.random.normal(ks[2], (E, 2 * I, H), jnp.float32) * s, 'down_proj': jax.random.normal(ks[3], (E, H, I), jnp.float32) * s, 'shared_gate': jax.random.normal(ks[4], (SI, H), jnp.float32) * s, 'shared_up': jax.random.normal(ks[5], (SI, H), jnp.float32) * s, 'shared_down': jax.random.normal(ks[6], (H, SI), jnp.float32) * s}
    _L1_ffn_all = _L1_ffn_setup()
    _L1_ffn_in = {k: v for k, v in _L1_ffn_all.items() if k in ('router_weight', 'e_score_correction_bias', 'gate_up_proj', 'down_proj', 'shared_gate', 'shared_up', 'shared_down')}
    del _L1_ffn_all
    return {'x': x, 'ctx_768': ctx_768, 'mask_BxS2_bf1': mask_BxS2_bf1, 'mask_BxS_bf1': mask_BxS_bf1, 'L0_xattn_Wq': _L0_xattn_in['Wq'], 'L0_xattn_Wk': _L0_xattn_in['Wk'], 'L0_xattn_Wv': _L0_xattn_in['Wv'], 'L0_xattn_Wo': _L0_xattn_in['Wo'], 'L0_attn_W_qkv': _L0_attn_in['W_qkv'], 'L0_attn_b_qkv': _L0_attn_in['b_qkv'], 'L0_attn_W_out': _L0_attn_in['W_out'], 'L0_attn_b_out': _L0_attn_in['b_out'], 'L0_ffn_clip_x': _L0_ffn_in['clip_x'], 'L0_ffn_clip_down': _L0_ffn_in['clip_down'], 'L0_ffn_w_gate': _L0_ffn_in['w_gate'], 'L0_ffn_w_up': _L0_ffn_in['w_up'], 'L0_ffn_w_down': _L0_ffn_in['w_down'], 'L1_xattn_Wq': _L1_xattn_in['Wq'], 'L1_xattn_Wk': _L1_xattn_in['Wk'], 'L1_xattn_Wv': _L1_xattn_in['Wv'], 'L1_xattn_W_film_in': _L1_xattn_in['W_film_in'], 'L1_xattn_b_film_in': _L1_xattn_in['b_film_in'], 'L1_xattn_W_film_out': _L1_xattn_in['W_film_out'], 'L1_xattn_b_film_out': _L1_xattn_in['b_film_out'], 'L1_xattn_g_norm_in': _L1_xattn_in['g_norm_in'], 'L1_xattn_b_norm_in': _L1_xattn_in['b_norm_in'], 'L1_xattn_g_norm_out': _L1_xattn_in['g_norm_out'], 'L1_xattn_b_norm_out': _L1_xattn_in['b_norm_out'], 'L1_xattn_g_ffn': _L1_xattn_in['g_ffn'], 'L1_xattn_b_ffn': _L1_xattn_in['b_ffn'], 'L1_xattn_W1': _L1_xattn_in['W1'], 'L1_xattn_b1': _L1_xattn_in['b1'], 'L1_xattn_W2': _L1_xattn_in['W2'], 'L1_xattn_b2': _L1_xattn_in['b2'], 'L1_xattn_log_dt': _L1_xattn_in['log_dt'], 'L1_xattn_A_re': _L1_xattn_in['A_re'], 'L1_xattn_A_im': _L1_xattn_in['A_im'], 'L1_xattn_C_re': _L1_xattn_in['C_re'], 'L1_xattn_C_im': _L1_xattn_in['C_im'], 'L1_xattn_D_skip': _L1_xattn_in['D_skip'], 'L1_xattn_mod_gate': _L1_xattn_in['mod_gate'], 'L1_attn_Wg': _L1_attn_in['Wg'], 'L1_attn_bg': _L1_attn_in['bg'], 'L1_attn_Wc': _L1_attn_in['Wc'], 'L1_attn_bc': _L1_attn_in['bc'], 'L1_ffn_router_weight': _L1_ffn_in['router_weight'], 'L1_ffn_e_score_correction_bias': _L1_ffn_in['e_score_correction_bias'], 'L1_ffn_gate_up_proj': _L1_ffn_in['gate_up_proj'], 'L1_ffn_down_proj': _L1_ffn_in['down_proj'], 'L1_ffn_shared_gate': _L1_ffn_in['shared_gate'], 'L1_ffn_shared_up': _L1_ffn_in['shared_up'], 'L1_ffn_shared_down': _L1_ffn_in['shared_down']}

def reference(x, ctx_768, mask_BxS2_bf1, mask_BxS_bf1, L0_xattn_Wq, L0_xattn_Wk, L0_xattn_Wv, L0_xattn_Wo, L0_attn_W_qkv, L0_attn_b_qkv, L0_attn_W_out, L0_attn_b_out, L0_ffn_clip_x, L0_ffn_clip_down, L0_ffn_w_gate, L0_ffn_w_up, L0_ffn_w_down, L1_xattn_Wq, L1_xattn_Wk, L1_xattn_Wv, L1_xattn_W_film_in, L1_xattn_b_film_in, L1_xattn_W_film_out, L1_xattn_b_film_out, L1_xattn_g_norm_in, L1_xattn_b_norm_in, L1_xattn_g_norm_out, L1_xattn_b_norm_out, L1_xattn_g_ffn, L1_xattn_b_ffn, L1_xattn_W1, L1_xattn_b1, L1_xattn_W2, L1_xattn_b2, L1_xattn_log_dt, L1_xattn_A_re, L1_xattn_A_im, L1_xattn_C_re, L1_xattn_C_im, L1_xattn_D_skip, L1_xattn_mod_gate, L1_attn_Wg, L1_attn_bg, L1_attn_Wc, L1_attn_bc, L1_ffn_router_weight, L1_ffn_e_score_correction_bias, L1_ffn_gate_up_proj, L1_ffn_down_proj, L1_ffn_shared_gate, L1_ffn_shared_up, L1_ffn_shared_down):
    import jax
    import jax.numpy as jnp

    def _L0_xattn_ref(x, context, context_mask, Wq, Wk, Wv, Wo):
        import jax, jax.numpy as jnp
        import numpy as np
        DIM = 256
        CTX_DIM = 192
        HEADS = 16
        B, N, _ = x.shape
        M = context.shape[1]
        hd = DIM // HEADS
        scale = hd ** (-0.5)
        q = (x @ Wq).reshape(B, N, HEADS, hd).transpose(0, 2, 1, 3)
        k = (context @ Wk).reshape(B, M, HEADS, hd).transpose(0, 2, 1, 3)
        v = (context @ Wv).reshape(B, M, HEADS, hd).transpose(0, 2, 1, 3)
        scores = jnp.einsum('bhid,bhjd->bhij', q, k) * scale
        max_neg = -jnp.finfo(scores.dtype).max
        scores = jnp.where(context_mask[:, None, None, :], scores, max_neg)
        attn = jax.nn.softmax(scores, axis=-1)
        out = jnp.einsum('bhij,bhjd->bhid', attn, v)
        out = out.transpose(0, 2, 1, 3).reshape(B, N, DIM)
        return out @ Wo

    def _L0_attn_ref(x, W_qkv, b_qkv, W_out, b_out):
        import jax, jax.numpy as jnp
        import numpy as np
        D_MODEL = 256
        NUM_HEADS = 16
        D_K = D_MODEL // NUM_HEADS
        B, S, _ = x.shape
        qkv = (jnp.einsum('bsd,de->bse', x, W_qkv) + b_qkv).reshape(B, S, NUM_HEADS, 3 * D_K)
        q, k, v = (qkv[..., :D_K], qkv[..., D_K:2 * D_K], qkv[..., 2 * D_K:])
        scores = jnp.einsum('bshd,bsgd->bshg', q, k) / np.sqrt(D_K)
        attn = jax.nn.softmax(scores, axis=-1)
        context = jnp.einsum('bshg,bsgd->bshd', attn, v).reshape(B, S, NUM_HEADS * D_K)
        return jnp.einsum('bsd,de->bse', context, W_out) + b_out

    def _L0_ffn_ref(x, clip_x, clip_down, w_gate, w_up, w_down):
        import jax, jax.numpy as jnp
        import numpy as np
        QMAX = 127.0

        def _ste_round(v):
            return v + jax.lax.stop_gradient(jnp.round(v) - v)

        def _act_fake_quant(x, clip_factor):
            scale = jax.nn.sigmoid(clip_factor) * jnp.max(jnp.abs(x)) / QMAX
            return jnp.clip(_ste_round(x / scale), -QMAX - 1.0, QMAX) * scale

        def _weight_fake_quant(w):
            scale = jnp.max(jnp.abs(w), axis=1, keepdims=True) / QMAX
            return jnp.clip(_ste_round(w / scale), -QMAX - 1.0, QMAX) * scale
        xq = _act_fake_quant(x, clip_x[0])
        gate = jnp.einsum('bsh,ih->bsi', xq, _weight_fake_quant(w_gate))
        up = jnp.einsum('bsh,ih->bsi', xq, _weight_fake_quant(w_up))
        h = _act_fake_quant(jax.nn.silu(gate) * up, clip_down[0])
        return jnp.einsum('bsi,hi->bsh', h, _weight_fake_quant(w_down))

    def _L1_xattn_ref(x_text, x_vision, text_mask, vision_mask, Wq, Wk, Wv, W_film_in, b_film_in, W_film_out, b_film_out, g_norm_in, b_norm_in, g_norm_out, b_norm_out, g_ffn, b_ffn, W1, b1, W2, b2, log_dt, A_re, A_im, C_re, C_im, D_skip, mod_gate):
        import jax, jax.numpy as jnp
        import numpy as np
        B, T, DT, G, DV = (16, 128, 256, 144, 192)
        H, DH = (4, 32)
        INNER = H * DH
        HID = 4 * DT
        N_STATE = 64
        K_TOP = 32

        def layernorm(x, g, b, eps=1e-05):
            m = x.mean(-1, keepdims=True)
            v = x.var(-1, keepdims=True)
            return (x - m) * jax.lax.rsqrt(v + eps) * g + b

        def s4d(x, log_dt, A_re, A_im, C_re, C_im, D_skip):
            Bb, L, D = x.shape
            dt = jnp.exp(log_dt)
            A = A_re + 1j * A_im
            C = C_re + 1j * C_im
            dtA = dt[:, None] * A
            dC = C * (jnp.exp(dtA) - 1.0) / A
            powers = jnp.exp(dtA[:, :, None] * jnp.arange(L))
            K = 2.0 * jnp.einsum('dn,dnl->dl', dC, powers).real
            n = 2 * L
            Kf = jnp.fft.rfft(K, n=n, axis=-1)
            xf = jnp.fft.rfft(x, n=n, axis=1)
            y = jnp.fft.irfft(xf * Kf.T[None], n=n, axis=1)[:, :L]
            return y + x * D_skip
        Bb, Tt, D = x_text.shape
        Gg = x_vision.shape[1]
        Q = (x_text @ Wq).reshape(Bb, Tt, H, DH)
        K = (x_vision @ Wk).reshape(Bb, Gg, H, DH)
        scores = jnp.einsum('bthd,bghd->bhtg', Q, K) / np.sqrt(DH).astype(np.float32)
        scores = jnp.where(vision_mask[:, None, None, :], scores, -jnp.inf)
        topv, topi = jax.lax.top_k(scores, K_TOP)
        probs = jax.nn.softmax(topv, axis=-1)
        bi = jnp.arange(Bb)[:, None, None, None]
        hi = jnp.arange(H)[None, :, None, None]
        ti = jnp.arange(Tt)[None, None, :, None]
        attn = jnp.zeros_like(scores).at[bi, hi, ti, topi].set(probs)
        attn_mean = attn.mean(axis=1)
        V = x_vision @ Wv
        c_t = jnp.einsum('btg,bgd->btd', attn_mean, V)
        c_t = c_t * text_mask[..., None]
        x = layernorm(x_text, g_norm_in, b_norm_in)
        scale_in, shift_in = jnp.split(c_t @ W_film_in + b_film_in, 2, axis=-1)
        x = x * (1.0 + mod_gate * scale_in) + mod_gate * shift_in
        y = s4d(x, log_dt, A_re, A_im, C_re, C_im, D_skip)
        scale_out, shift_out = jnp.split(c_t @ W_film_out + b_film_out, 2, axis=-1)
        y = y * (1.0 + mod_gate * scale_out) + mod_gate * shift_out
        xt = x_text + y
        h = layernorm(xt, g_ffn, b_ffn)
        h = jax.nn.gelu(h @ W1 + b1, approximate=False) @ W2 + b2
        xt = xt + h
        return layernorm(xt, g_norm_out, b_norm_out)

    def _L1_attn_ref(x, Wg, bg, Wc, bc):
        import jax, jax.numpy as jnp
        import numpy as np
        B, L, D = (4, 2048, 256)

        def _mingru_scan(gates, candidates):

            def combine(e1, e2):
                a1, b1 = e1
                a2, b2 = e2
                return (a2 * a1, a2 * b1 + b2)
            _, h = jax.lax.associative_scan(combine, (gates, candidates), axis=1)
            return h
        gates = jax.nn.sigmoid(jnp.einsum('bld,ed->ble', x, Wg) + bg)
        candidates = jnp.tanh(jnp.einsum('bld,ed->ble', x, Wc) + bc)
        return _mingru_scan(gates, candidates)

    def _L1_ffn_ref(hidden_states, router_weight, e_score_correction_bias, gate_up_proj, down_proj, shared_gate, shared_up, shared_down):
        import jax, jax.numpy as jnp
        import numpy as np
        E, K, H, I, SI = (32, 8, 256, 128, 512)
        CAP = 512
        LIMIT = 7.0
        SCALE = 2.5
        B, S = (2, 512)
        b, s, _ = hidden_states.shape
        T = b * s
        x = hidden_states.reshape(T, H)
        logits = x.astype(jnp.float32) @ router_weight.astype(jnp.float32).T
        scores = jax.nn.sigmoid(logits)
        _, idx = jax.lax.top_k(scores + e_score_correction_bias, K)
        w = jnp.take_along_axis(scores, idx, axis=1)
        w = w / (w.sum(-1, keepdims=True) + 1e-20) * SCALE
        e_flat = idx.reshape(-1)
        onehot = jax.nn.one_hot(e_flat, E, dtype=jnp.int32)
        pos = jnp.cumsum(onehot, axis=0) - onehot
        pos = jnp.take_along_axis(pos, e_flat[:, None], axis=1)[:, 0]
        keep = pos < CAP
        slot = jnp.where(keep, e_flat * CAP + pos, E * CAP)
        tok = jnp.arange(T * K) // K
        buf = jnp.zeros((E * CAP + 1, H), x.dtype).at[slot].set(x[tok])
        xe = buf[:E * CAP].reshape(E, CAP, H)
        gu = jnp.einsum('ech,eoh->eco', xe, gate_up_proj)
        g, u = (gu[..., :I], gu[..., I:])
        g = jnp.minimum(g, LIMIT)
        u = jnp.clip(u, -LIMIT, LIMIT)
        h = jax.nn.silu(g) * u
        ye = jnp.einsum('eci,ehi->ech', h, down_proj)
        yp = ye.reshape(E * CAP, H)[jnp.minimum(slot, E * CAP - 1)]
        yp = jnp.where(keep[:, None], yp, 0.0) * w.reshape(-1)[:, None]
        routed = jax.ops.segment_sum(yp, tok, num_segments=T).reshape(b, s, H)
        shared = jax.nn.silu(hidden_states @ shared_gate.T) * (hidden_states @ shared_up.T) @ shared_down.T
        return routed + shared
    x = x + _L0_xattn_ref(_layernorm(x, axis=-1), ctx_768, mask_BxS2_bf1, L0_xattn_Wq, L0_xattn_Wk, L0_xattn_Wv, L0_xattn_Wo)
    x = x + _L0_attn_ref(_layernorm(x, axis=-1), L0_attn_W_qkv, L0_attn_b_qkv, L0_attn_W_out, L0_attn_b_out)
    x = x + _L0_ffn_ref(_layernorm(x, axis=-1), L0_ffn_clip_x, L0_ffn_clip_down, L0_ffn_w_gate, L0_ffn_w_up, L0_ffn_w_down)
    x = x + _L1_xattn_ref(_layernorm(x, axis=-1), ctx_768, mask_BxS_bf1, mask_BxS2_bf1, L1_xattn_Wq, L1_xattn_Wk, L1_xattn_Wv, L1_xattn_W_film_in, L1_xattn_b_film_in, L1_xattn_W_film_out, L1_xattn_b_film_out, L1_xattn_g_norm_in, L1_xattn_b_norm_in, L1_xattn_g_norm_out, L1_xattn_b_norm_out, L1_xattn_g_ffn, L1_xattn_b_ffn, L1_xattn_W1, L1_xattn_b1, L1_xattn_W2, L1_xattn_b2, L1_xattn_log_dt, L1_xattn_A_re, L1_xattn_A_im, L1_xattn_C_re, L1_xattn_C_im, L1_xattn_D_skip, L1_xattn_mod_gate)
    x = x + _L1_attn_ref(_layernorm(x, axis=-1), L1_attn_Wg, L1_attn_bg, L1_attn_Wc, L1_attn_bc)
    x = x + _L1_ffn_ref(_layernorm(x, axis=-1), L1_ffn_router_weight, L1_ffn_e_score_correction_bias, L1_ffn_gate_up_proj, L1_ffn_down_proj, L1_ffn_shared_gate, L1_ffn_shared_up, L1_ffn_shared_down)
    return x

_drawn_inputs = setup_inputs


def setup_inputs(seed=0):
    import zlib

    import numpy as np

    out = dict(_drawn_inputs(seed))
    spreads = {'L1_xattn_b_film_in': (0.0, 0.1),
     'L1_xattn_b_film_out': (0.0, 0.271),
     'L1_xattn_g_norm_in': (1.0, 0.2),
     'L1_xattn_b_norm_in': (0.0, 0.1),
     'L1_xattn_g_norm_out': (1.0, 0.2),
     'L1_xattn_b_norm_out': (0.0, 0.1),
     'L1_xattn_g_ffn': (1.0, 0.6),
     'L1_xattn_b_ffn': (0.0, 0.8),
     'L1_xattn_b1': (0.0, 0.629),
     'L1_xattn_b2': (0.0, 0.1),
     'L1_xattn_A_re': (-0.5, 0.2),
     'L1_attn_bg': (1.0, 0.2),
     'L1_attn_bc': (0.0, 0.1),
     'L1_ffn_e_score_correction_bias': (0.0, 0.8)}
    factors = {'L0_attn_b_qkv': 8.0,
     'L0_attn_b_out': 4.756,
     'L1_xattn_Wq': 4.292,
     'L1_xattn_Wk': 4.571,
     'L1_xattn_W_film_in': 2.846,
     'L1_xattn_W_film_out': 3.83,
     'L1_ffn_router_weight': 8.0,
     'L1_ffn_gate_up_proj': 8.0,
     'L1_ffn_down_proj': 8.0,
     'L1_ffn_shared_gate': 5.438,
     'L1_ffn_shared_up': 5.479,
     'L1_ffn_shared_down': 5.314}
    for name, (base, spread) in spreads.items():
        noise = np.random.default_rng([zlib.crc32(name.encode()), seed]).standard_normal(out[name].shape)
        drawn = base * np.exp(spread * noise) if base else spread * noise
        out[name] = jnp.asarray(drawn.astype(out[name].dtype))
    for name, factor in factors.items():
        out[name] = (out[name] * factor).astype(out[name].dtype)
    return out
```

```python
from contextlib import ExitStack
from math import exp, pi

import concourse.bass as bass
from concourse import mybir
from concourse.alu_op_type import AluOpType as ALU

F32 = mybir.dt.float32
F32R = mybir.dt.float32r
BF16 = mybir.dt.bfloat16
U8 = mybir.dt.uint8
ACT = mybir.ActivationFunctionType
AX = mybir.AxisListType.X
RMAX = bass.bass_isa.ReduceOp.max

P = 128
T = 256
TT = T // P
D = 256
M = 4096
CD = 192
C1 = CD - P
KT = M // P
H = 16
HD = D // H
PAIRS = H // 2
SLOTS = 16
CH = M // 512
NEG = -2.0 ** 127
ROUND = 1.5 * 2.0 ** 23
NS = 64
LA = 16
E = 32
F_ = 704
FR = [min(P, F_ - i * P) for i in range(6)]
LOW = -1e38
SILU7 = 7.0 / (1.0 + exp(-7.0))
QMAX = 127.0
I = 128
SIN_MAX = 3.1415925
TWO_PI = (6.28125, 0.0019350051879882812, 3.0198482e-07)


def perceiver_kernel(nc, A, out):
    ctx = ExitStack()
    with ctx:
        sems = {}

        def S(name):
            if name not in sems:
                sems[name] = ctx.enter_context(nc.semaphore(name))
            return sems[name]

        def sb(name, shape, dt=F32, scope=None):
            return (scope or ctx).enter_context(nc.sbuf_tensor(name, shape, dt))

        def chain(eng, name):
            n = [0]

            def link(ins):
                n[0] += 1
                ins.then_inc(S(name), 1)
                eng.wait_ge(S(name), n[0])
                return ins
            return link

        PS = ctx.enter_context(nc.psum_tensor("PS", [P, 8, 512], F32))

        x = sb("x", [P, TT, D])
        z = sb("z", [P, TT, D])
        zT = sb("zT", [P, 2, T])
        ident = sb("ident", [P, P])
        stats = sb("stats", [P, TT, 6])
        mv = sb("mv", [P, TT, 2])
        sd = sb("sd", [P, TT])
        rs = sb("rs", [P, TT])
        eps = sb("eps", [P, 1])
        rows_scratch = nc.dram_tensor("rows_scratch", [16, M], F32).ap()
        K_scratch = nc.dram_tensor("K_scratch", [LA, LA, D], F32).ap()

        ph1 = ExitStack()
        qst = sb("qst", [P, 4, T], F32R, ph1)
        q_hi = sb("q_hi", [P, 2, T], F32R, ph1)
        q_lo = sb("q_lo", [P, 2, T], F32R, ph1)
        k_hi = sb("k_hi", [P, 2, M], F32R, ph1)
        k_lo = sb("k_lo", [P, 2, M], F32R, ph1)
        vst = sb("vst", [P, KT, H, 2 * HD + 1], F32R, ph1)
        sub = ExitStack()
        ctxT = sb("ctxT", [P, 2, M], F32, sub)
        sub.close()
        kst = sb("kst", [P, 2, M], F32R, ph1)
        prep = ExitStack()
        wv = sb("wv", [P, 2, D], F32, prep)
        s4 = sb("s4", [P, 4, D], F32, prep)
        dtb = sb("dtb", [P, D], F32, prep)
        sw = sb("sw", [P, 5, D], F32, prep)
        fac = sb("fac", [P, 2 * LA], F32, prep)
        phs = sb("phs", [P, 8], F32, prep)
        mku = sb("mku", [P, 32], U8, prep)
        ang = sb("ang", [P, LA, 2 * LA], F32, prep)
        kk = sb("kk", [P, LA, 2 * LA], F32, prep)
        yA = kk
        mag = sb("mag", [P, LA, 2 * LA], F32, prep)
        maskb = mag
        SV = sb("SV", [P, LA, 2 * LA], F32, prep)
        T2 = sb("T2", [P, LA, LA], F32, prep)
        first = ExitStack()
        wq = sb("wq", [P, 2, D], F32, first)
        wk = sb("wk", [P, 2, D], F32, first)
        first.close()
        UV = sb("UV", [P, 2, LA, 2 * LA], F32, prep)
        Kstage = sw[0:LA, 3:5, :]
        prep.close()
        loop = ExitStack()
        prob = sb("prob", [P, 4, 512], F32, loop)
        prob_hi = sb("prob_hi", [P, 4, 512], F32R, loop)
        prob_lo = sb("prob_lo", [P, 4, 512], F32R, loop)
        mxp = sb("mxp", [P, 2, 8], F32, loop)
        mx = sb("mx", [P, 2, TT], F32, loop)
        rows = sb("rows", [P, 2, T], F32, loop)
        mrow = rows[:, :, :].bitcast(F32R)
        ostage = rows[0:2 * HD + 1, :, :]
        oh = sb("oh", [P, 2, T], F32, loop)
        ol, osum = zT, z
        loop.close()
        ph1.close()
        wo = sb("wo", [P, 2, D])
        wqkv = sb("wqkv", [P, 2, 3 * D])
        bqkv = sb("bqkv", [P, 3 * D])
        wout = sb("wout", [P, 2, D])
        bout = sb("bout", [P, D])
        clips = sb("clips", [P, 2])
        wq1 = sb("wq1", [P, 2, P])
        wk1 = sb("wk1", [P, 2, P])
        wv1 = sb("wv1", [P, 2, D])
        wfi = sb("wfi", [P, 2, 2 * D])
        wfo = sb("wfo", [P, 2, 2 * D])
        bfi = sb("bfi", [P, 2 * D])
        bfo = sb("bfo", [P, 2 * D])
        gb = sb("gb", [P, 6, D])
        b1 = sb("b1", [P, 8])
        b2 = sb("b2", [P, D])
        dskip = sb("dskip", [P, D])
        gate = sb("gate", [P, 1])
        tmask_u = sb("tmask_u", [P, TT], U8)
        tmask = sb("tmask", [P, TT])
        dft = sb("dft", [P, 2, 2 * T])
        dftT = sb("dftT", [P, 4, T])
        Kf = sb("Kf", [P, 4, D])
        wgg = sb("wgg", [P, 2, D])
        wgc = sb("wgc", [P, 2, D])
        bgc = sb("bgc", [P, 2, 2])
        router = sb("router", [P, 2, E])
        rbias = sb("rbias", [P, E])
        identb = sb("identb", [P, P], BF16)
        q1 = sb("q1", [P, T])
        cT = sb("cT", [P, 2, T])
        zc = sb("zc", [P, 2, T])
        xt = sb("xt", [P, TT, D])
        y = sb("y", [P, TT, D])
        Kt = y
        small = sb("small", [P, 128])
        big = ExitStack()
        over_ctx = ExitStack()
        ctxT2 = sb("ctxT2", [P, 2, M], F32, over_ctx)
        over_ctx.close()
        EB = sb("EB", [P, 2, M], F32, big)
        k1T = sb("k1T", [P, M], F32, big)
        attn = ExitStack()
        prod = sb("prod", [P, 2, 8 * H * HD], F32, attn)
        qkv = sb("qkv", [P, TT, 3 * D], F32, attn)
        sc = sb("sc", [P, TT, H * H], F32, attn)
        attn.close()
        AM = sb("AM", [P, M], F32, big)
        ctxn = sb("ctxn", [P, KT, CD], F32, big)
        ffn = ExitStack()
        wraw = sb("wraw", [P, 2, 6, D], F32, ffn)
        wdraw = sb("wdraw", [P, 2, F_], F32, ffn)
        wint = sb("wint", [P, 2, 6, D], BF16, ffn)
        wdint = sb("wdint", [P, 2, F_], BF16, ffn)
        guT = sb("guT", [P, 2, 2, F_], BF16, ffn)
        wdT = sb("wdT", [P, 6, D], BF16, ffn)
        xqT = sb("xqT", [P, 2, T], BF16, ffn)
        sg, hf = wraw[:, 0], wraw[:, 1]
        hq = sb("hq", [P, 6, T], BF16, ffn)
        ffn.close()
        maskrow = sb("maskrow", [P, M], F32, big)
        Asc = sb("Asc", [P, 2, M], F32, big)
        AMT = wqkv[:, :, 0:4 * P].rearrange("p n (u t) -> p n u t", u=4)
        m8 = sb("m8", [P, 2, 32], F32, big)
        big.close()
        moe = ExitStack()
        Gh = sb("Gh", [P, 8, T], F32, moe)
        Yf = sb("Yf", [P, 4, D], F32, moe)
        gup = sb("gup", [P, E, 2, 2 * I], F32, moe)
        down = sb("down", [P, E, D], F32, moe)
        sgu = sb("sgu", [P, 2, 2, 512], F32, moe)
        sdn = sb("sdn", [P, 4, D], F32, moe)
        dense = ExitStack()
        w1 = sb("w1", [P, 2, 4 * D], F32, dense)
        w2 = sb("w2", [P, 8, D], F32, dense)
        dense.close()
        esg = sb("esg", [P, 2, T], F32, moe)
        euc = sb("euc", [P, 2, T], F32, moe)
        ehw = sb("ehw", [P, 2, T], F32, moe)
        gt = sb("gt", [P, 2, T], F32, moe)
        cd = sb("cd", [P, 2, T], F32, moe)
        wT = sb("wT", [E, T], F32, moe)
        rt = sb("rt", [P, 4, TT, E], F32, moe)
        moe.close()

        bank = lambda b: PS[:, b, :]
        at = lambda *tags: {tag: n + 1 for n, tag in enumerate(tags)}
        LN = at("ln0", "ln1", "ln2", "ln3", "xin", "ln4", "nout", "ln5", "ln6")
        Z = at("ln0", "ln1", "attn_out", "ln2", "ffn_q", "ln3", "xin", "ln4", "nout", "ln5", "ln6")
        ZT = at("ln0", "ln1", "attn_out", "ffn_q", "ln3", "ln4", "ln5", "ln6")

        def ln_stats(dve, link, tag, src, affine=None):
            for t in range(TT):
                last = nc.vector.bn_stats(stats[:, t, :], src[:, t, :])
            link(last)
            for t in range(TT):
                last = nc.vector.bn_aggr(mv[:, t, :], stats[:, t, :])
            last.then_inc(S("ln_var"), 1)
            dve.wait_ge(S("ln_sd"), LN[tag])
            link(nc.vector.reciprocal(rs[:, :], sd[:, :]))
            for t in range(TT):
                last = nc.vector.tensor_scalar(z[:, t, :], src[:, t, :], mv[:, t, 0:1], rs[:, t:t + 1],
                                               ALU.subtract, ALU.mult)
            if affine is not None:
                link(last)
                g, s = (gb[:, affine + n, :].unsqueeze(1).broadcast_to([P, TT, D]) for n in range(2))
                link(nc.vector.tensor_tensor(z[:, :, :], z[:, :, :], g, ALU.mult))
                last = nc.vector.tensor_tensor(z[:, :, :], z[:, :, :], s, ALU.add)
            last.then_inc(S("z_ready"), 1)
            dve.wait_ge(S("z_ready"), Z[tag])

        def ln_sqrt(act, tag):
            act.wait_ge(S("ln_var"), LN[tag])
            nc.scalar.activation(sd[:, :], mv[:, :, 1], ACT.Sqrt, bias=eps[:, 0:1]).then_inc(S("ln_sd"), 1)

        def to_features(pe, src, b, tag):
            pe.wait_ge(S("z_ready"), Z[tag])
            for m in range(2):
                for t in range(TT):
                    last = nc.tensor.transpose(bank(b)[:, m * T + t * P:m * T + (t + 1) * P],
                                               src[:, t, m * P:(m + 1) * P], ident[:, :])
            last.then_inc(S("zT_full"), 1)

        def keep_features(act, dst, b, tag):
            act.wait_ge(S("zT_full"), ZT[tag])
            nc.scalar.copy(dst[:, :, :], bank(b)).then_inc(S("zT_kept"), 1)

        S_NEXT = {0: 5, 2: 6, 4: 7}
        S_AFTER = {6: 0, 8: 1, 10: 2, 12: 3, 14: 4}
        M_AT = 8
        AHEAD = 4

        block = ctx.enter_context(nc.Block())

        @block.sync
        def _(sp):
            def move(to, rows_, done):
                sp.dma_start(to.bitcast(F32), rows_.bitcast(F32)).then_inc(S(done), 16)

            sp.dma_start(x[:, :, :], A["x"].rearrange("(t p) d -> p t d", p=P)).then_inc(S("x_in"), 16)
            sp.dma_start(wk[:, 0, :], A["L0_xattn_Wk"][0:P, :]).then_inc(S("wk_in"), 16)
            sp.dma_start(wk[0:C1, 1, :], A["L0_xattn_Wk"][P:CD, :]).then_inc(S("wk_in"), 16)
            for c in range(4):
                cs = slice(c * 1024, (c + 1) * 1024)
                sp.dma_start(ctxT[:, 0, cs], A["ctxT"][0:P, cs]).then_inc(S(f"ctxT_in{c}"), 16)
                sp.dma_start(ctxT[0:C1, 1, cs], A["ctxT"][P:CD, cs]).then_inc(S(f"ctxT_in{c}"), 16)
                if c == 0:
                    sp.dma_start(ident[:, :], A["ident"]).then_inc(S("ident_in"), 16)
                    sp.dma_start(wq[:, :, :], A["L0_xattn_Wq"].rearrange("(k p) d -> p k d", p=P)).then_inc(S("wq_in"), 16)
                    sp.dma_start(fac[:, :], A["lfac"]).then_inc(S("s4_in"), 16)
                    sp.dma_start(phs[:, :], A["phase"]).then_inc(S("s4_in"), 16)
                    sp.dma_start(dtb[:, :], A["L1_xattn_log_dt"].partition_broadcast(P)).then_inc(S("s4_in"), 16)
                    for n, name in enumerate(("A_reT", "A_imT", "C_reT", "C_imT")):
                        for half in range(2):
                            sp.dma_start(s4[NS * half:NS * (half + 1), n, :], A[name]).then_inc(S("s4_in"), 16)
                    sp.dma_start(mku[:, :], A["ctx_mask"].rearrange("(p j) -> p j", p=P)).then_inc(S("mku_in"), 16)
                if c == 1:
                    sp.dma_start(wv[:, 0, :], A["L0_xattn_Wv"][0:P, :]).then_inc(S("wv_in"), 16)
                    sp.dma_start(wv[0:C1, 1, :], A["L0_xattn_Wv"][P:CD, :]).then_inc(S("wv_in"), 16)
            sp.wait_ge(S("maskb_ready"), 1)
            sp.dma_start(rows_scratch.rearrange("r (p j) -> p r j", p=P), maskb[:, :, :]).then_inc(S("mask_out"), 16)
            for n in range(16):
                sp.wait_ge(S("K_staged"), n + 2)
                sp.dma_start(K_scratch[:, :, LA * n:LA * (n + 1)],
                             Kstage[:, n % 2, :].rearrange("a (b d) -> a b d", d=LA)).then_inc(S("K_out"), 16)

            sp.wait_ge(S("kv_low"), 4 + 32)
            sp.wait_ge(S("mask_out"), 16)
            for s in range(2):
                for par in range(2):
                    sp.dma_start(kst[64 * par + 48:64 * par + 64, s, :].bitcast(F32), rows_scratch).then_inc(S("kmask_in"), 16)

            def load_stack(p):
                for par in range(2):
                    src = 32 * (p % 4) + HD * par
                    for r, k in enumerate((k_hi, k_hi, k_lo)):
                        b = 64 * par + HD * r
                        move(kst[b:b + HD, p % 2, :], k[src:src + HD, p // 4, :], "kst_in")

            def load_queries(h):
                if h >= 4:
                    sp.wait_ge(S("st_full"), SLOTS * (h - 3))
                b, f = 64 * (h % 2), slice(HD * (h % 8), HD * (h % 8 + 1))
                for r, q in enumerate((q_hi, q_lo, q_hi)):
                    move(qst[b + HD * r:b + HD * (r + 1), h % 4, :], q[f, h // 8, :], f"q_in{h % 4}")
                sp.dma_start(qst[b + 48:b + 62, h % 4, :].bitcast(F32), rows_scratch[2:16, 0:T])\
                    .then_inc(S(f"q_in{h % 4}"), 16)

            def load_max(h):
                sp.wait_ge(S("mrow_ready"), h + 1)
                b = 64 * (h % 2) + 49
                move(qst[b:b + 2, h % 4, :], mrow[96:97, :, :], "m_in")

            def gather_head(h):
                sp.wait_ge(S("o_staged"), h + 3)
                f = slice(HD * (h % 8), HD * (h % 8 + 1))
                st = ostage[:, h % 2, :]
                sp.dma_start(oh[f, h // 8, :], st[0:HD, :]).then_inc(S("o_in"), 16)
                sp.dma_start(ol[f, h // 8, :], st[HD + 1:2 * HD + 1, :]).then_inc(S("o_in"), 16)
                sp.dma_start(osum[f, h // 8, :], st[HD:HD + 1, :].unsqueeze(1).broadcast_to([1, HD, T])).then_inc(S("o_in"), 16)

            load_stack(0)
            load_stack(1)
            sp.wait_ge(S("q_lo_ready"), 2)
            sp.wait_ge(S("stacks_set"), 2)
            for h in range(4):
                load_queries(h)
            load_max(0)
            for p in range(PAIRS):
                load_max(2 * p + 1)
                if p + 2 < PAIRS:
                    load_queries(2 * p + 4)
                gather_head(2 * p)
                if p + 1 < PAIRS:
                    load_max(2 * p + 2)
                    if p + 2 < PAIRS:
                        sp.wait_ge(S("st_full"), 2 * SLOTS * (p + 1))
                        load_stack(p + 2)
                        load_queries(2 * p + 5)
                gather_head(2 * p + 1)
            def load(to, rows_, done):
                sp.dma_start(to, rows_).then_inc(S(done), 16)

            rows2 = lambda a: a.rearrange("(k p) n -> p k n", p=P)
            across = lambda a: a.partition_broadcast(P)
            sp.wait_ge(S("aT"), 1)
            load(wo[:, :, :], rows2(A["L0_xattn_Wo"]), "self_in")
            load(wqkv[:, :, :], rows2(A["L0_attn_W_qkv"]), "self_in")
            load(bqkv[:, :], across(A["L0_attn_b_qkv"]), "self_in")
            load(wout[:, :, :], rows2(A["L0_attn_W_out"]), "self_in")
            load(bout[:, :], across(A["L0_attn_b_out"]), "self_in")
            for n, name in enumerate(("L0_ffn_w_gate", "L0_ffn_w_up")):
                load(wraw[:, n, 0:5, :], A[name][0:5 * P, :].rearrange("(i p) n -> p i n", p=P), "wffn_in")
                load(wraw[0:FR[5], n, 5, :], A[name][5 * P:F_, :], "wffn_in")
            load(wdraw[:, :, :], rows2(A["L0_ffn_w_down"]), "wffn_in")
            load(clips[:, 0:1], across(A["L0_ffn_clip_x"]), "wffn_in")
            load(clips[:, 1:2], across(A["L0_ffn_clip_down"]), "wffn_in")
            load(wk1[:, 0, :], A["L1_xattn_Wk"][0:P, :], "keys2_in")
            load(wk1[0:C1, 1, :], A["L1_xattn_Wk"][P:CD, :], "keys2_in")
            load(ctxT2[:, 0, :], A["ctxT"][0:P, :], "keys2_in")
            load(ctxT2[0:C1, 1, :], A["ctxT"][P:CD, :], "keys2_in")
            load(Kt[:, 0, :], K_scratch[0:8].rearrange("a b d -> (a b) d"), "keys2_in")
            load(Kt[:, 1, :], K_scratch[8:16].rearrange("a b d -> (a b) d"), "keys2_in")
            load(dft[:, :, :], rows2(A["dft"]), "keys2_in")
            load(dftT[:, :, :], rows2(A["dftT"]), "keys2_in")
            load(wq1[:, :, :], rows2(A["L1_xattn_Wq"]), "film_in")
            load(tmask_u[:, :], A["text_mask"], "film_in")
            load(wv1[:, 0, :], A["L1_xattn_Wv"][0:P, :], "film_in")
            load(wv1[0:C1, 1, :], A["L1_xattn_Wv"][P:CD, :], "film_in")
            load(wfi[:, :, :], rows2(A["L1_xattn_W_film_in"]), "film_in")
            load(wfo[:, :, :], rows2(A["L1_xattn_W_film_out"]), "film_in")
            load(bfi[:, :], across(A["L1_xattn_b_film_in"]), "film_in")
            load(bfo[:, :], across(A["L1_xattn_b_film_out"]), "film_in")
            for n, name in enumerate(("g_norm_in", "b_norm_in", "g_ffn", "b_ffn", "g_norm_out", "b_norm_out")):
                load(gb[:, n, :], across(A["L1_xattn_" + name]), "film_in")
            load(b2[:, :], across(A["L1_xattn_b2"]), "film_in")
            load(dskip[:, :], across(A["L1_xattn_D_skip"]), "film_in")
            load(gate[:, :], across(A["L1_xattn_mod_gate"]), "film_in")
            load(b1[:, :], A["b1T"], "film_in")
            load(wgg[:, :, :], rows2(A["WgT"]), "rest_in")
            load(wgc[:, :, :], rows2(A["WcT"]), "rest_in")
            load(bgc[:, 0, :], A["bgT"], "rest_in")
            load(bgc[:, 1, :], A["bcT"], "rest_in")
            load(router[:, :, :], rows2(A["routerT"]), "rest_in")
            load(rbias[:, :], across(A["L1_ffn_e_score_correction_bias"]), "rest_in")
            sp.wait_ge(S("x_new"), 4)
            load(ctxn[:, :, :], A["ctx"].rearrange("(k p) c -> p k c", p=P), "ctxn_in")
            sp.wait_ge(S("hq_used"), 1)
            load(maskrow[:, :], rows_scratch[0:1, :].rearrange("a k -> (a k)").partition_broadcast(P), "maskrow_in")
            sp.wait_ge(S("zc_ready"), 2)
            load(w1[:, :, :], rows2(A["L1_xattn_W1"]), "w12_in")
            load(w2[:, :, :], rows2(A["L1_xattn_W2"]), "w12_in")
            load(sgu[:, :, :, :], A["sguT"].rearrange("p (k g i) -> p k g i", k=2, g=2), "shared_in")
            load(sdn[:, :, :], A["sdnT"].rearrange("p (k n) -> p k n", k=4), "shared_in")
            for g in range(4):
                es = slice(8 * g, 8 * g + 8)
                load(gup[:, es, :, :], A["gupT"][:, es, :, :], f"experts_in{g}")
                load(down[:, es, :], A["downT"][:, es, :], f"experts_in{g}")
            sp.wait_ge(S("x_new"), 12)
            sp.dma_start(out.rearrange("(t p) d -> p t d", p=P), x[:, :, :]).then_inc(S("out_done"), 16)
            sp.wait_ge(S("out_done"), 16)

        @block.tensor
        def _(pe):
            pe.wait_ge(S("wk_in"), 32)

            def fill_k(c, n):
                for j, m in enumerate((0, 1)):
                    b = n + j
                    for k in range(2):
                        r = P if k == 0 else C1
                        last = nc.tensor.matmul(bank(b), wk[0:r, k, m * P:(m + 1) * P],
                                                ctxT[0:r, k, bass.ds(c * 512, 512)], start=(k == 0), stop=(k == 1))
                    last.then_inc(S("fill"), 1)

            for i in range(4):
                pe.wait_ge(S(f"ctxT_in{i}"), 32)
                for u in range(2):
                    pe.wait_ge(S("kv_low"), 4 * i + 2 * u + 2)
                    fill_k(2 * i + u, 2 * u)
            pe.wait_ge(S("ident_in"), 16)
            to_features(pe, z, 4, "ln0")
            pe.wait_ge(S("zT_kept"), ZT["ln0"])
            pe.wait_ge(S("wq_in"), 16)
            for m in range(2):
                for k in range(2):
                    last = nc.tensor.matmul(bank(5)[:, m * T:(m + 1) * T], wq[:, k, m * P:(m + 1) * P], zT[:, k, :],
                                            start=(k == 0), stop=(k == 1))
                last.then_inc(S("q_full"), 1)
            pe.wait_ge(S("wv_in"), 32)
            for i in range(4):
                for j in range(4):
                    pe.wait_ge(S("kv_low"), i * 4 + (16 + j + 1))
                    for u in range(2):
                        for k in range(2):
                            r = P if k == 0 else C1
                            last = nc.tensor.matmul(bank(j)[:, u * D:(u + 1) * D],
                                                    ctxT[0:r, k, bass.ds(i * 1024 + (2 * j + u) * P, P)], wv[0:r, k, :],
                                                    start=(k == 0), stop=(k == 1))
                    last.then_inc(S("fill"), 1)
            with pe.Fori(0, 8) as i:
                for s in range(2):
                    pe.wait_ge(S("uv_ready"), i * 2 + s + 2)
                    pe.wait_ge(S("K_staged"), i * 2 + s + 1)
                    o = bank(6 + s)[0:LA, 0:LA * LA].rearrange("a (b d) -> a d b", d=LA)
                    for d in range(LA):
                        last = nc.tensor.matmul(o[:, d, :], UV[:, s, d, 0:LA], UV[:, s, d, LA:2 * LA],
                                                start=True, stop=True)
                    last.then_inc(S("K_full"), 1)

            def scores(h, s):
                t, c = s // 4, s % 4
                for u in range(2):
                    last = nc.tensor.matmul(bank(2 * (s % 2) + u), qst[:, h % 4, t * P:(t + 1) * P],
                                            kst[:, h // 2 % 2, c * 1024 + u * 512:c * 1024 + (u + 1) * 512],
                                            start=True, stop=True)
                last.then_inc(S("s_full"), 1)

            def scores_t(h, j):
                for u in range(2):
                    last = nc.tensor.matmul(bank(4 + j % 2)[:, u * T:(u + 1) * T],
                                            kst[:, h // 2 % 2, (2 * j + u) * P:(2 * j + u + 1) * P],
                                            qst[:, h % 4, :], start=True, stop=True)
                last.then_inc(S("st_full"), 1)

            def max_row(h):
                for t in range(TT):
                    last = nc.tensor.matmul(bank(7)[96:97, t * P:(t + 1) * P], mx[:, h % 2, t:t + 1], ident[:, :],
                                            start=True, stop=True)
                last.then_inc(S("mrow_full"), 1)

            def weigh(p, par, j):
                for u in range(2):
                    for part in (prob_hi, prob_lo):
                        last = nc.tensor.matmul(bank(6 + par)[0:2 * HD + 1, 0:T],
                                                vst[:, 2 * j + u, p * 2 + par, :],
                                                part[:, j % 4, u * T:(u + 1) * T],
                                                start=(j == 0 and u == 0 and part is prob_hi),
                                                stop=(j == SLOTS - 1 and u == 1 and part is prob_lo))
                last.then_inc(S("pv_done"), 1)

            def pair(p):
                for i in range(2 * SLOTS):
                    par, j = divmod(i, SLOTS)
                    h = 2 * p + par
                    g, s = (h + 1, S_NEXT[j]) if j in S_NEXT else (h + 2, S_AFTER[j]) if j in S_AFTER else (H, 0)
                    if g < H:
                        if g % 2 == 0 and s == 0:
                            pe.wait_ge(S("kst_in"), 96 * (g // 2 + 1))
                        if s == 0:
                            pe.wait_ge(S(f"q_in{g % 4}"), 64 * (g // 4 + 1))
                        pe.wait_ge(S("s_free"), 8 * g + s + 1)
                        scores(g, s)
                    if j == M_AT and h + 1 < H:
                        pe.wait_ge(S("m_ready"), h + 2)
                        pe.wait_ge(S("mrow_ready"), h + 1)
                        max_row(h + 1)
                    n = 2 * SLOTS * p + i + AHEAD
                    if n < SLOTS * H:
                        slot_t(n)
                    if j == 0:
                        pe.wait_ge(S("o_staged"), h + 1)
                    q, r = divmod(i, 4)
                    if r < 3:
                        pe.wait_ge(S("low_pool"), p * 24 + (3 * q + r + 1 + 3))
                    else:
                        pe.wait_ge(S("low_dve"), p * 8 + (q + 1 + 1))
                    weigh(p, par, j)

            def slot_t(n):
                h, j = divmod(n, SLOTS)
                if j == 0:
                    pe.wait_ge(S("m_in"), 16 * (h + 1))
                pe.wait_ge(S("exp_done"), n + 1)
                scores_t(h, j)

            for h in range(2):
                pe.wait_ge(S(f"q_in{h}"), 64)
            pe.wait_ge(S("kmask_in"), 16 * 4)
            pe.wait_ge(S("kst_in"), 192)
            pe.wait_ge(S("stacks_set"), 2)
            pe.wait_ge(S("q_lo_ready"), 2)
            pe.wait_ge(S("kv_low"), 4 + 32)
            for h, n in ((0, 8), (1, 5)):
                for s in range(n):
                    pe.wait_ge(S("s_free"), 8 * h + s + 1)
                    scores(h, s)
                if h == 0:
                    pe.wait_ge(S("m_ready"), 1)
                    pe.wait_ge(S("K_staged"), 17)
                    max_row(0)
            for n in range(AHEAD):
                slot_t(n)
            for p in range(PAIRS):
                pair(p)
            pe.wait_ge(S("self_in"), 16 * 5)
            pe.wait_ge(S("aT"), 1)
            for t in range(TT):
                for k in range(2):
                    last = nc.tensor.matmul(bank(t)[:, 0:D], zT[:, k, t * P:(t + 1) * P], wo[:, k, :],
                                            start=(k == 0), stop=(k == 1))
                last.then_inc(S("projected"), 1)

            def features(tag, b=6, src=z):
                to_features(pe, src, b, tag)
                pe.wait_ge(S("zT_kept"), ZT[tag])

            def project(lhs, w, n, cols, b, done, width=None):
                for t in range(TT):
                    for k in range(2):
                        last = nc.tensor.matmul(bank(b + t)[:, 0:n], lhs[:, k, t * P:(t + 1) * P], w[:, k, cols:cols + n],
                                                start=(k == 0), stop=(k == 1))
                    last.then_inc(S(done), 1)

            def to_tokens(src, b, tag, ready):
                pe.wait_ge(S(ready), 1)
                for t in range(TT):
                    for m in range(2):
                        last = nc.tensor.transpose(bank(b)[:, t * D + m * P:t * D + (m + 1) * P],
                                                   src[:, m, t * P:(t + 1) * P], ident[:, :])
                last.then_inc(S(tag), 1)

            features("ln1")
            pe.wait_ge(S("self_in"), 16 * 5)
            for t in range(TT):
                for c in range(2):
                    for k in range(2):
                        last = nc.tensor.matmul(bank(2 * t + c)[:, 0:384], zT[:, k, t * P:(t + 1) * P],
                                                wqkv[:, k, c * 384:(c + 1) * 384], start=(k == 0), stop=(k == 1))
            last.then_inc(S("qkv_full"), 1)
            pe.wait_ge(S("keys2_in"), 16 * 8)
            for c in range(CH):
                if c >= 2:
                    pe.wait_ge(S("k1_kept"), c - 1)
                for k in range(2):
                    r = P if k == 0 else C1
                    last = nc.tensor.matmul(bank(4 + c % 2), wk1[0:r, k, :], ctxT2[0:r, k, c * 512:(c + 1) * 512],
                                            start=(k == 0), stop=(k == 1))
                last.then_inc(S("k1_full"), 1)

            def spectrum(src, done):
                for f in range(4):
                    for k in range(2):
                        last = nc.tensor.matmul(bank(6 + f // 2)[:, f % 2 * D:(f % 2 + 1) * D],
                                                dft[:, k, f * P:(f + 1) * P], src[:, k, :],
                                                start=(k == 0), stop=(k == 1))
                last.then_inc(S(done), 1)

            pe.wait_ge(S("keys2_in"), 16 * 8)
            spectrum(Kt, "Kf_full")
            pe.wait_ge(S("wints"), 3)
            pe.wait_ge(S("k1_kept"), CH)
            pe.wait_ge(S("Kf_kept"), 2)
            for n in range(2):
                for k in range(2):
                    b = (4 + k if n == 0 else 6 + k)
                    for i, r in enumerate(FR):
                        last = nc.tensor.transpose(bank(b).bitcast(BF16)[:, i * P:i * P + r],
                                                   wint[0:r, n, i, k * P:(k + 1) * P], identb[0:r, 0:r])
                    last.then_inc(S("wT_full"), 1)
            for m in range(2):
                pe.wait_ge(S("wT_kept"), m + 1)
                for i, r in enumerate(FR):
                    last = nc.tensor.transpose(bank(4 + m).bitcast(BF16)[0:r, i * P:(i + 1) * P],
                                               wdint[:, m, i * P:i * P + r], identb[:, :])
                last.then_inc(S("wT_full"), 1)
            pe.wait_ge(S("wT_kept"), 6)
            features("attn_out")
            pe.wait_ge(S("self_in"), 16 * 5)
            project(zT, wout, D, 0, 0, "projected")

            features("ffn_q")
            for i, r in enumerate(FR):
                for n in range(2):
                    for k in range(2):
                        last = nc.tensor.matmul(bank(i)[0:r, n * T:(n + 1) * T], guT[:, n, k, i * P:i * P + r],
                                                xqT[:, k, :], start=(k == 0), stop=(k == 1))
                last.then_inc(S("gu_full"), 1)
            pe.wait_ge(S("hq_ready"), 1)
            for m in range(2):
                for i, r in enumerate(FR):
                    last = nc.tensor.matmul(bank(6)[:, m * T:(m + 1) * T], wdT[0:r, i, m * P:(m + 1) * P],
                                            hq[0:r, i, :], start=(i == 0), stop=(i == 5))
            last.then_inc(S("down_full"), 1)
            to_tokens(zT, 7, "ffn_y", "down_kept")

            features("ln3")
            pe.wait_ge(S("film_in"), 16 * 18)
            for k in range(2):
                last = nc.tensor.matmul(bank(5)[:, 0:T], wq1[:, k, :], zT[:, k, :], start=(k == 0), stop=(k == 1))
            last.then_inc(S("q1_full"), 1)
            pe.wait_ge(S("q1_kept"), 1)

            def weigh_context(t):
                for g in range(8):
                    n = 8 * t + g
                    pe.wait_ge(S("AM_ready"), t + 1)
                    if n >= 2:
                        pe.wait_ge(S("AMT_kept"), n - 1)
                    for u in range(4):
                        last = nc.tensor.transpose(bank(4 + g % 2)[:, u * P:(u + 1) * P],
                                                   AM[:, (4 * g + u) * P:(4 * g + u + 1) * P], ident[:, :])
                    last.then_inc(S("AMT_full"), 1)
                    if g > 0:
                        context_sum(t, g - 1)
                context_sum(t, 7)

            def context_sum(t, g):
                pe.wait_ge(S("AMT_kept"), 8 * t + g + 1)
                pe.wait_ge(S("ctxn_in"), 16)
                for u in range(4):
                    kt = 4 * g + u
                    for c, w in ((0, P), (1, C1)):
                        last = nc.tensor.matmul(bank(6 + c)[0:w, t * P:(t + 1) * P], ctxn[:, kt, c * P:c * P + w],
                                                AMT[:, g % 2, u, :], start=(kt == 0), stop=(kt == KT - 1))
                last.then_inc(S("zc_full"), 1)

            for n in range(8):
                t, h = divmod(n, 4)
                for c in range(CH):
                    m = CH * n + c
                    if m >= 4:
                        pe.wait_ge(S("A_copied"), m - 3)
                    last = nc.tensor.matmul(bank(c % 4), q1[32 * h:32 * h + 32, t * P:(t + 1) * P],
                                            k1T[32 * h:32 * h + 32, c * 512:(c + 1) * 512], start=True, stop=True)
                    last.then_inc(S("A_full"), 1)
                if n == 5:
                    weigh_context(0)
            weigh_context(1)
            pe.wait_ge(S("zc_ready"), 2)
            pe.wait_ge(S("film_in"), 16 * 18)
            for m in range(2):
                for k in range(2):
                    r = P if k == 0 else C1
                    last = nc.tensor.matmul(bank(0)[:, m * T:(m + 1) * T], wv1[0:r, k, m * P:(m + 1) * P], zc[0:r, k, :],
                                            start=(k == 0), stop=(k == 1))
            last.then_inc(S("cT_full"), 1)
            pe.wait_ge(S("cT_ready"), 1)
            project(cT, wfi, 2 * D, 0, 1, "film_in_full")
            project(cT, wfo, 2 * D, 0, 3, "film_out_full")
            pe.wait_ge(S("u_ready"), 1)
            spectrum(z, "U_full")
            pe.wait_ge(S("Y_ready"), 1)
            for t in range(TT):
                for f in range(4):
                    last = nc.tensor.matmul(bank(5)[:, t * D:(t + 1) * D], dftT[:, f, t * P:(t + 1) * P], Yf[:, f, :],
                                            start=(f == 0), stop=(f == 3))
            last.then_inc(S("y_full"), 1)
            features("ln4")
            pe.wait_ge(S("w12_in"), 32)
            for m in range(8):
                for k in range(2):
                    last = nc.tensor.matmul(bank(m // 2)[:, m % 2 * T:(m % 2 + 1) * T], w1[:, k, m * P:(m + 1) * P],
                                            zT[:, k, :], start=(k == 0), stop=(k == 1))
                if m % 2 == 1:
                    last.then_inc(S("h1_full"), 1)
            for m in range(8):
                if m % 2 == 0:
                    pe.wait_ge(S("Gh_ready"), m // 2 + 1)
                for t in range(TT):
                    last = nc.tensor.matmul(bank(4 + t)[:, 0:D], Gh[:, m, t * P:(t + 1) * P], w2[:, m, :],
                                            start=(m == 0), stop=(m == 7))
            last.then_inc(S("h2_full"), 1)

            features("ln5")
            pe.wait_ge(S("rest_in"), 16 * 6)
            for n, w in enumerate((wgg, wgc)):
                for m in range(2):
                    for k in range(2):
                        last = nc.tensor.matmul(bank(n)[:, m * T:(m + 1) * T], w[:, k, m * P:(m + 1) * P], zT[:, k, :],
                                                start=(k == 0), stop=(k == 1))
                last.then_inc(S("gru_full"), 1)
            to_tokens(cT, 2, "gru_y", "gru_done")

            features("ln6")
            pe.wait_ge(S("rest_in"), 16 * 6)
            for t in range(TT):
                for k in range(2):
                    last = nc.tensor.matmul(bank(7)[:, t * E:(t + 1) * E], zT[:, k, t * P:(t + 1) * P], router[:, k, :],
                                            start=(k == 0), stop=(k == 1))
            last.then_inc(S("logits"), 1)

            def expert_in(n):
                if n >= 2:
                    pe.wait_ge(S("unit_read"), n - 1)
                for g in range(2):
                    for k in range(2):
                        w = sgu[:, k, g, n * P:(n + 1) * P] if n < 4 else gup[:, n - 4, k, g * I:(g + 1) * I]
                        last = nc.tensor.matmul(bank(n % 2)[:, g * T:(g + 1) * T], w, zT[:, k, :],
                                                start=(k == 0), stop=(k == 1))
                if n >= 4:
                    e = n - 4
                    last = nc.tensor.matmul(bank(2 + n % 2)[:, 0:T], ident[0:E, e:e + 1].broadcast_to([E, P]), wT[:, :],
                                            start=True, stop=True)
                last.then_inc(S("unit_full"), 1)

            def expert_out(n):
                pe.wait_ge(S("unit_ready"), n + 1)
                w = sdn[:, n, :] if n < 4 else down[:, n - 4, :]
                for t in range(TT):
                    last = nc.tensor.matmul(bank(4 + t)[:, 0:D], ehw[:, n % 2, t * P:(t + 1) * P], w,
                                            start=(n == 0), stop=(n == E + 3))
                last.then_inc(S("unit_done"), 1)

            pe.wait_ge(S("shared_in"), 32)
            for n in range(E + 4):
                if n == 4:
                    pe.wait_ge(S("wtok"), 1)
                    for t in range(TT):
                        last = nc.tensor.transpose(bank(7)[0:E, t * P:(t + 1) * P], rt[:, 2, t, :], ident[:, :])
                    last.then_inc(S("wT_t"), 1)
                    pe.wait_ge(S("wT_ready"), 1)
                if n >= 4 and n % 8 == 4:
                    pe.wait_ge(S(f"experts_in{(n - 4) // 8}"), 32)
                expert_in(n)
                if n >= 1:
                    expert_out(n - 1)
            expert_out(E + 3)

        @block.scalar
        def _(act):
            act.wait_ge(S("eps_set"), 1)
            ln_sqrt(act, "ln0")
            for i in range(4):
                for u in range(4):
                    c, m = 2 * i + u // 2, u % 2
                    act.wait_ge(S("fill"), 4 * i + u + 1)
                    nc.scalar.copy(k_hi[:, m, c * 512:(c + 1) * 512], bank(u)).then_inc(S("kv_high"), 1)
            keep_features(act, zT, 4, "ln0")
            for m in range(2):
                act.wait_ge(S("q_full"), 2)
                nc.scalar.copy(q_hi[:, m, :], bank(5)[:, m * T:(m + 1) * T]).then_inc(S("q_hi_ready"), 1)
            act.wait_ge(S("s4_in"), 16 * 11)
            nc.scalar.activation(dtb[:, :], dtb[:, :], ACT.Exp).then_inc(S("dt_ready"), 1)
            act.wait_ge(S("step_ready"), 1)
            nc.scalar.activation(sw[:, 2, :], sw[:, 0, :], ACT.Tanh, scale=0.5)
            nc.scalar.activation(sw[:, 3, :], sw[:, 4, :], ACT.Sin, scale=0.5)
            nc.scalar.activation(sw[:, 4, :], sw[:, 4, :], ACT.Sin).then_inc(S("step_funcs"), 1)

            with act.Fori(0, 4) as i:
                for j in range(4):
                    act.wait_ge(S("fill"), i * 4 + (16 + j + 1))
                    nc.scalar.copy(vst[:, bass.ds(i * 8 + 2 * j, 2), :, 0:HD],
                                   bank(j).rearrange("p (u h d) -> p u h d", u=2, d=HD)).then_inc(S("kv_high"), 1)

            def waves(n):
                act.wait_ge(S("mag_arg"), n + 1)
                nc.scalar.activation(mag[:, :, :], mag[:, :, :], ACT.Exp).then_inc(S("mag_ready"), 1)
                act.wait_ge(S("ang_ready"), n + 1)
                act.wait_ge(S("uv_ready"), n + 1)
                nc.scalar.activation(SV[:, :, 0:LA], yA[:, :, 0:LA], ACT.Sin, bias=phs[:, 3:4], scale=-1.0)
                nc.scalar.activation(SV[:, :, LA:2 * LA], yA[:, :, LA:2 * LA], ACT.Sin, bias=phs[:, 3:4], scale=phs[:, 0:1])
                nc.scalar.activation(T2[:, :, :], ang[:, :, 0:LA], ACT.Sin, bias=phs[:, 4:5], scale=phs[:, 1:2])\
                    .then_inc(S("sin_ready"), 1)

            def stage(n):
                act.wait_ge(S("K_full"), n + 3)
                act.wait_ge(S("K_out"), n * 16 + 16)
                nc.scalar.copy(Kstage[:, n % 2, :], PS[0:LA, n % 2 + 6, 0:LA * LA]).then_inc(S("K_staged"), 1)

            waves(0)
            with act.Fori(0, 15) as n:
                waves(n + 1)
                stage(n)
            stage(15)
            act.wait_ge(S("K_out"), 17 * 16)

            def keep_turned(act, t, g):
                act.wait_ge(S("AMT_full"), 8 * t + g + 1)
                if 8 * t + g >= 2:
                    act.wait_ge(S("zc_full"), 8 * t + g - 1)
                nc.scalar.copy(AMT[:, g % 2, :, :], bank(4 + g % 2)).then_inc(S("AMT_kept"), 1)

            with act.Fori(0, PAIRS) as p:
                for i in range(2 * SLOTS):
                    q, r = divmod(i, 4)
                    act.wait_ge(S("st_full"), p * 32 + i + 1)
                    if r < 3:
                        act.wait_ge(S("low_pool"), p * 24 + (3 * q + r + 1))
                    else:
                        act.wait_ge(S("low_dve"), p * 8 + (q + 1))
                    nc.scalar.activation(prob[:, r, :], bank(4 + i % 2), ACT.Exp, scale=HD ** -0.5)\
                        .then_inc(S("exp_done"), 1)
                    if r < 3:
                        act.wait_ge(S("exp_done"), p * 32 + (i + 3))
                        act.wait_ge(S("pv_done"), p * 32 + (i + 1))
                        nc.scalar.copy(prob_hi[:, r, :], prob[:, r, :]).then_inc(S("high_act"), 1)

            def copy(to, frm, waits, done):
                for name, v in waits:
                    act.wait_ge(S(name), v)
                nc.scalar.copy(to, frm).then_inc(S(done), 1)

            ln_sqrt(act, "ln1")
            keep_features(act, zT, 6, "ln1")
            for c in range(CH):
                copy(k1T[:, c * 512:(c + 1) * 512], bank(4 + c % 2), [("k1_full", c + 1)], "k1_kept")
            for n in range(2):
                copy(Kf[:, 2 * n:2 * n + 2, :], bank(6 + n), [("Kf_full", 1)], "Kf_kept")
            act.wait_ge(S("sc_ready"), 1)
            nc.scalar.activation(sc[:, :, :], sc[:, :, :], ACT.Exp, scale=HD ** -0.5).then_inc(S("sc_exp"), 1)
            for n in range(2):
                for k in range(2):
                    b = (4 + k if n == 0 else 6 + k)
                    copy(guT[:, n, k, :], bank(b).bitcast(BF16)[:, 0:F_], [("wT_full", 2 * n + k + 1)], "wT_kept")
            for m in range(2):
                act.wait_ge(S("wT_full"), 5 + m)
                nc.scalar.copy(wdT[:, 0:5, m * P:(m + 1) * P],
                               bank(4 + m).bitcast(BF16)[:, 0:5 * P].rearrange("p (i h) -> p i h", i=5))
                nc.scalar.copy(wdT[0:FR[5], 5, m * P:(m + 1) * P], bank(4 + m).bitcast(BF16)[0:FR[5], 5 * P:6 * P])\
                    .then_inc(S("wT_kept"), 1)
            keep_features(act, zT, 6, "attn_out")

            act.wait_ge(S("wffn_in"), 16 * 7)
            nc.scalar.activation(small[:, 32:34], clips[:, :], ACT.Exp, scale=-1.0).then_inc(S("clip_exp"), 1)
            ln_sqrt(act, "ln2")
            act.wait_ge(S("zT_full"), ZT["ffn_q"])
            nc.scalar.copy(xqT[:, :, :], bank(6)).then_inc(S("zT_kept"), 1)
            act.wait_ge(S("comb_ready"), 1)
            for i, r in enumerate(FR):
                act.wait_ge(S("gu_full"), i + 1)
                nc.scalar.activation(sg[0:r, i, :], bank(i)[0:r, 0:T], ACT.Silu, scale=small[0:r, 40 + i:41 + i])\
                    .then_inc(S("sg_ready"), 1)
            act.wait_ge(S("down_full"), 1)
            for m in range(2):
                last = nc.scalar.activation(zT[:, m, :], bank(6)[:, m * T:(m + 1) * T], ACT.Copy,
                                            scale=small[:, 56 + m:57 + m])
            last.then_inc(S("down_kept"), 1)

            ln_sqrt(act, "ln3")
            keep_features(act, zT, 6, "ln3")
            copy(q1[:, :], bank(5)[:, 0:T], [("q1_full", 1)], "q1_kept")

            def keep_scores(n):
                for c in range(CH):
                    act.wait_ge(S("A_full"), CH * n + c + 1)
                    if c == 0 and n >= 2:
                        act.wait_ge(S("top_weighed"), n - 1)
                    nc.scalar.activation(Asc[:, n % 2, c * 512:(c + 1) * 512], bank(c % 4), ACT.Copy, scale=32 ** -0.5)\
                        .then_inc(S("A_copied"), 1)

            act.wait_ge(S("hq_used"), 1)
            act.wait_ge(S("x_new"), 6)
            keep_scores(0)
            for n in range(8):
                t, h = divmod(n, 4)
                if n + 1 < 8:
                    keep_scores(n + 1)
                act.wait_ge(S("top_found"), n + 1)
                nc.scalar.activation(EB[:, n % 2, :], Asc[:, n % 2, :], ACT.Exp, bias=small[:, 64 + n % 2:65 + n % 2])\
                    .then_inc(S("E_ready"), 1)
                act.wait_ge(S("r_ready"), n + 1)
                if h == 0:
                    if t == 1:
                        for g in range(8):
                            keep_turned(act, 0, g)
                    nc.scalar.activation(AM[:, :], EB[:, n % 2, :], ACT.Copy, scale=small[:, 66 + n % 2:67 + n % 2])\
                        .then_inc(S("E_scaled"), 1)
                else:
                    nc.scalar.activation(EB[:, n % 2, :], EB[:, n % 2, :], ACT.Copy, scale=small[:, 66 + n % 2:67 + n % 2])\
                        .then_inc(S("E_scaled"), 1)
            for g in range(8):
                keep_turned(act, 1, g)
            act.wait_ge(S("zc_full"), 16)
            nc.scalar.copy(zc[:, 0, :], bank(6)[:, 0:T]).then_inc(S("zc_ready"), 1)
            nc.scalar.copy(zc[0:C1, 1, :], bank(7)[0:C1, 0:T]).then_inc(S("zc_ready"), 1)
            copy(cT[:, :, :], bank(0), [("cT_full", 1)], "cT_ready")
            ln_sqrt(act, "xin")
            ln_sqrt(act, "ln4")
            keep_features(act, zT, 6, "ln4")
            for m in range(8):
                act.wait_ge(S("h1_full"), m // 2 + 1)
                last = nc.scalar.activation(Gh[:, m, :], bank(m // 2)[:, m % 2 * T:(m % 2 + 1) * T], ACT.Gelu,
                                            bias=b1[:, m:m + 1])
                if m % 2 == 1:
                    last.then_inc(S("Gh_ready"), 1)
            ln_sqrt(act, "nout")

            ln_sqrt(act, "ln5")
            keep_features(act, zT, 6, "ln5")
            for n, (to, f) in enumerate(((gt, ACT.Sigmoid), (cd, ACT.Tanh))):
                act.wait_ge(S("gru_full"), n + 1)
                for m in range(2):
                    last = nc.scalar.activation(to[:, m, :], bank(n)[:, m * T:(m + 1) * T], f, bias=bgc[:, n, m:m + 1])
                last.then_inc(S("gru_act"), 1)

            ln_sqrt(act, "ln6")
            keep_features(act, zT, 6, "ln6")
            act.wait_ge(S("logits"), 1)
            nc.scalar.activation(rt[:, 0, :, :], bank(7)[:, 0:TT * E].rearrange("p (t e) -> p t e", t=TT), ACT.Sigmoid)\
                .then_inc(S("rscores"), 1)
            for n in range(E + 4):
                if n == 4:
                    copy(wT[:, :], bank(7)[0:E, 0:T], [("wT_t", 1)], "wT_ready")
                act.wait_ge(S("unit_full"), n + 1)
                if n >= 2:
                    act.wait_ge(S("unit_ready"), n - 1)
                nc.scalar.activation(esg[:, n % 2, :], bank(n % 2)[:, 0:T], ACT.Silu).then_inc(S("unit_silu"), 1)

        @block.gpsimd
        def _(pool):
            link = chain(pool, "pool_chain")
            nc.gpsimd.memset(eps[:, :], 1e-5).then_inc(S("eps_set"), 1)
            nc.gpsimd.memset(vst[:, :, :, HD:HD + 1].bitcast(F32), 1.0).then_inc(S("stacks_set"), 1)
            pool.wait_ge(S("stacks_set"), 1)
            nc.gpsimd.memset(qst[:, :, :].bitcast(F32), 0.0).then_inc(S("stacks_set"), 1)
            pool.wait_ge(S("stacks_set"), 2)
            pool.wait_ge(S("mku_in"), 16)
            link(nc.gpsimd.memset(maskb[:, 1:3, :], 1.0))
            link(nc.gpsimd.memset(maskb[:, 3:16, :], 0.0))
            link(nc.gpsimd.tensor_copy(maskb[:, 0, :], mku[:, :]))
            nc.gpsimd.tensor_scalar(maskb[:, 0, :], maskb[:, 0, :], -NEG, NEG, ALU.mult, ALU.add).then_inc(S("maskb_ready"), 1)
            bd = lambda v: v.unsqueeze(2).broadcast_to([P, LA, 2 * LA])
            facb = fac[:, :].unsqueeze(1).broadcast_to([P, LA, 2 * LA])
            bh = lambda v: v.unsqueeze(2).broadcast_to([P, LA, LA])
            pool.wait_ge(S("dC_ready"), 1)
            pool.wait_ge(S("mask_out"), 16)
            with pool.Fori(0, 8) as i:
                for s in range(2):
                    ds = bass.ds(i * 32 + s * LA, LA)
                    pool.wait_ge(S("uv_ready"), i * 2 + s + 1)
                    nc.gpsimd.tensor_tensor(mag[:, :, :], bd(sw[:, 0, ds]), facb, ALU.mult).then_inc(S("mag_arg"), 1)
                    pool.wait_ge(S("mag_ready"), i * 2 + s + 1)
                    pool.wait_ge(S("sin_ready"), i * 2 + s + 2)
                    nc.gpsimd.tensor_tensor(T2[:, :, :], T2[:, :, :], mag[:, :, 0:LA], ALU.mult).then_inc(S("t2_a"), 1)
                    pool.wait_ge(S("t2_a"), i * 2 + s + 1)
                    nc.gpsimd.tensor_tensor(T2[:, :, :], T2[:, :, :], bh(s4[:, 3, ds]), ALU.mult).then_inc(S("t2_b"), 1)
                    pool.wait_ge(S("t2_b"), i * 2 + s + 1)
                    pool.wait_ge(S("sv_mag"), i * 2 + s + 1)
                    pool.wait_ge(S("K_full"), i * 2 + s + 1)
                    nc.gpsimd.tensor_tensor(UV[:, s, :, 0:LA], SV[:, :, 0:LA], T2[:, :, :], ALU.subtract)\
                        .then_inc(S("uv_ready"), 1)
            pool.wait_ge(S("K_out"), 17 * 16)
            with pool.Fori(0, PAIRS) as p:
                for i in range(2 * SLOTS):
                    q, r = divmod(i, 4)
                    if r < 3:
                        pool.wait_ge(S("high_act"), p * 24 + (3 * q + r + 1))
                        nc.gpsimd.tensor_tensor(prob_lo[:, r, :], prob[:, r, :], prob_hi[:, r, :].bitcast(F32),
                                                ALU.subtract).then_inc(S("low_pool"), 1)

            link2 = chain(pool, "pool_chain2")
            pool.wait_ge(S("aT"), 1)
            link2(nc.gpsimd.memset(wraw[64:P, :, 5, :], 1.0))
            pool.wait_ge(S("wffn_in"), 16 * 7)
            pool.wait_ge(S("wscales"), 1)
            for n, (w, o, a, g) in enumerate(((wraw[:, 0], wint[:, 0], 0, 6), (wraw[:, 1], wint[:, 1], 6, 6), (wdraw, wdint, 12, 2))):
                k = w.shape[2]
                inv = small[:, 16 + a:16 + a + g].unsqueeze(2).broadcast_to([P, g, k])
                link2(nc.gpsimd.tensor_tensor(w[:, :, :], w[:, :, :], inv, ALU.mult))
                link2(nc.gpsimd.tensor_scalar(w[:, :, :], w[:, :, :], QMAX, -QMAX - 1, ALU.min, ALU.max))
                link2(nc.gpsimd.tensor_scalar(w[:, :, :], w[:, :, :], ROUND, None, ALU.add))
                nc.gpsimd.tensor_scalar(o[:, :, :], w[:, :, :], ROUND, None, ALU.subtract).then_inc(S("wints"), 1)
                pool.wait_ge(S("wints"), n + 1)
            for n in range(2):
                pool.wait_ge(S("absmax_part"), n + 1)
                nc.gpsimd.partition_all_reduce(small[:, 36 + n:37 + n], small[:, 34 + n:35 + n], P, RMAX)\
                    .then_inc(S("absmax_all"), 1)
                pool.wait_ge(S("absmax_all"), n + 1)
            pool.wait_ge(S("maskrow_in"), 16)

            def mask_scores(n):
                pool.wait_ge(S("A_copied"), CH * (n + 1))
                nc.gpsimd.tensor_tensor(Asc[:, n % 2, :], Asc[:, n % 2, :], maskrow[:, :], ALU.add)\
                    .then_inc(S("A_masked"), 1)
                pool.wait_ge(S("A_masked"), n + 1)

            mask_scores(0)
            for n in range(8):
                t, h = divmod(n, 4)
                if n + 1 < 8:
                    mask_scores(n + 1)
                pool.wait_ge(S("E_scaled"), n + 1)
                if h > 0:
                    nc.gpsimd.tensor_tensor(AM[:, :], AM[:, :], EB[:, n % 2, :], ALU.add).then_inc(S("E_added"), 1)
                    pool.wait_ge(S("E_added"), 3 * t + h)
                if h == 3:
                    nc.gpsimd.sem_inc(S("AM_ready"), 1)

        @block.vector
        def _(dve):
            link = chain(dve, "dve_chain")
            nc.vector.sem_inc(S("kv_low"), 4)
            nc.vector.sem_inc(S("s_free"), 2)
            nc.vector.sem_inc(S("exp_done"), 2)
            nc.vector.sem_inc(S("o_staged"), 2)
            nc.vector.sem_inc(S("low_pool"), 3)
            nc.vector.sem_inc(S("low_dve"), 1)
            nc.vector.sem_inc(S("pv_done"), 4)
            nc.vector.sem_inc(S("K_full"), 2)
            for name, n in (("uv_ready", 1), ("sin_ready", 1), ("K_staged", 1), ("K_out", 16), ("o_in", 48)):
                nc.vector.sem_inc(S(name), n)
            dve.wait_ge(S("x_in"), 16)
            ln_stats(dve, link, "ln0", x)
            for i in range(4):
                for u in range(4):
                    c, m = 2 * i + u // 2, u % 2
                    dve.wait_ge(S("kv_high"), 4 * i + u + 1)
                    nc.vector.tensor_tensor(k_lo[:, m, c * 512:(c + 1) * 512], bank(u),
                                            k_hi[:, m, c * 512:(c + 1) * 512].bitcast(F32),
                                            ALU.subtract).then_inc(S("kv_low"), 1)
            for m in range(2):
                dve.wait_ge(S("q_hi_ready"), 2)
                nc.vector.tensor_tensor(q_lo[:, m, :], bank(5)[:, m * T:(m + 1) * T], q_hi[:, m, :].bitcast(F32),
                                        ALU.subtract).then_inc(S("q_lo_ready"), 1)

            tt = nc.vector.tensor_tensor
            stt = nc.vector.scalar_tensor_tensor
            ts = nc.vector.tensor_scalar
            Ar, Ai, Cr, Ci = (s4[:, n, :] for n in range(4))
            a, w1, th, s2, sn = (sw[:, n, :] for n in range(5))

            def reduce_angle(y, k):
                link(ts(k, y, 1 / (2 * pi), ROUND, ALU.mult, ALU.add))
                link(ts(k, k, ROUND, None, ALU.subtract))
                for part in TWO_PI:
                    link(stt(y, k, -part, y, ALU.mult, ALU.add))
                link(ts(y, y, SIN_MAX, -SIN_MAX, ALU.min, ALU.max))

            dve.wait_ge(S("dt_ready"), 1)
            link(tt(sw[:, 0, :], dtb[:, :], Ar, ALU.mult))
            link(tt(dtb[:, :], dtb[:, :], Ai, ALU.mult))
            link(nc.vector.tensor_copy(sn, dtb[:, :]))
            reduce_angle(sn, w1)
            nc.vector.sem_inc(S("step_ready"), 1)
            dve.wait_ge(S("step_funcs"), 1)
            link(ts(w1, th, -1.0, 1.0, ALU.mult, ALU.add))
            link(nc.vector.reciprocal(w1, w1))
            link(stt(th, th, 2.0, w1, ALU.mult, ALU.mult))
            link(tt(s2, s2, s2, ALU.mult))
            link(ts(s2, s2, 2.0, None, ALU.mult))
            link(stt(sn, th, 1.0, sn, ALU.add, ALU.mult))
            link(stt(w1, th, -1.0, s2, ALU.mult, ALU.mult))
            link(tt(w1, w1, th, ALU.add))
            link(tt(th, w1, s2, ALU.subtract))
            link(tt(w1, th, Ar, ALU.mult))
            link(tt(s2, sn, Ai, ALU.mult))
            link(tt(w1, w1, s2, ALU.add))
            link(tt(s2, sn, Ar, ALU.mult))
            link(tt(th, th, Ai, ALU.mult))
            link(tt(s2, s2, th, ALU.subtract))
            link(tt(Ar, Ar, Ar, ALU.mult))
            link(tt(Ai, Ai, Ai, ALU.mult))
            link(tt(Ar, Ar, Ai, ALU.add))
            link(nc.vector.reciprocal(Ar, Ar))
            link(stt(w1, w1, 2.0, Ar, ALU.mult, ALU.mult))
            link(stt(s2, s2, 2.0, Ar, ALU.mult, ALU.mult))
            link(tt(Ar, Cr, w1, ALU.mult))
            link(tt(Ai, Ci, s2, ALU.mult))
            link(tt(th, Ar, Ai, ALU.subtract))
            link(tt(Ar, Cr, s2, ALU.mult))
            link(tt(Ai, Ci, w1, ALU.mult))
            link(tt(Ci, Ar, Ai, ALU.add))
            link(nc.vector.tensor_copy(Cr, th))
            nc.vector.sem_inc(S("dC_ready"), 1)

            with dve.Fori(0, 4) as i:
                for j in range(4):
                    dve.wait_ge(S("kv_high"), i * 4 + (16 + j + 1))
                    v = bank(j).rearrange("p (u h d) -> p u h d", u=2, d=HD)
                    for u in range(2):
                        kt = i * 8 + (2 * j + u)
                        last = tt(vst[:, kt, :, HD + 1:2 * HD + 1], v[:, u], vst[:, kt, :, 0:HD].bitcast(F32),
                                  ALU.subtract)
                    last.then_inc(S("kv_low"), 1)

            bd = lambda v: v.unsqueeze(2).broadcast_to([P, LA, 2 * LA])
            facb = fac[:, :].unsqueeze(1).broadcast_to([P, LA, 2 * LA])
            with dve.Fori(0, 8) as i:
                for s in range(2):
                    ds = bass.ds(i * 32 + s * LA, LA)
                    n = i * 2 + s
                    step = [0]

                    def then(ins):
                        step[0] += 1
                        ins.then_inc(S("angle_step"), 1)
                        dve.wait_ge(S("angle_step"), n * 7 + step[0])
                    dve.wait_ge(S("sin_ready"), n + 1)
                    then(tt(ang[:, :, :], bd(dtb[:, ds]), facb, ALU.mult))
                    then(ts(kk[:, :, :], ang[:, :, :], 1 / (2 * pi), ROUND, ALU.mult, ALU.add))
                    then(ts(kk[:, :, :], kk[:, :, :], ROUND, None, ALU.subtract))
                    f = lambda v: v[:, :, :].rearrange("p d j -> p (d j)")
                    for part in TWO_PI:
                        then(stt(f(ang), f(kk), -part, f(ang), ALU.mult, ALU.add))
                    then(ts(f(ang), f(ang), SIN_MAX, -SIN_MAX, ALU.min, ALU.max))
                    stt(f(yA), f(ang), phs[:, 0:1], f(ang), ALU.mult, ALU.max).then_inc(S("ya_done"), 1)
                    dve.wait_ge(S("ya_done"), n + 1)
                    stt(ang[:, :, 0:LA], ang[:, :, 0:LA], phs[:, 1:2], ang[:, :, 0:LA], ALU.mult, ALU.max)\
                        .then_inc(S("ang_ready"), 1)
                    dve.wait_ge(S("mag_ready"), n + 1)
                    dve.wait_ge(S("sin_ready"), n + 2)
                    dve.wait_ge(S("K_full"), n + 1)
                    tt(UV[:, s, :, LA:2 * LA], SV[:, :, LA:2 * LA], mag[:, :, LA:2 * LA], ALU.mult).then_inc(S("sv_1"), 1)
                    tt(SV[:, :, 0:LA], SV[:, :, 0:LA], mag[:, :, 0:LA], ALU.mult).then_inc(S("sv_1"), 1)
                    dve.wait_ge(S("sv_1"), n * 2 + 2)
                    tt(SV[:, :, 0:LA], SV[:, :, 0:LA], bd(s4[:, 2, ds])[:, :, 0:LA], ALU.mult).then_inc(S("sv_mag"), 1)

            def take_max(s, n):
                nc.vector.reduce_max(mxp[:, n, s:s + 1], PS[:, 2 * (s % 2):2 * (s % 2) + 2, :].rearrange("p a b -> p (a b)"),
                                     AX).then_inc(S("s_free"), 1)

            def keep_max(n, h):
                dve.wait_ge(S("s_free"), 8 * h + 8 + 2)
                nc.vector.tensor_reduce(mx[:, n, :], mxp[:, n, :].rearrange("p (t s) -> p t s", t=TT), AX, ALU.max,
                                        negate=True).then_inc(S("m_ready"), 1)

            def split_row(h):
                dve.wait_ge(S("mrow_full"), h + 1)
                dve.wait_ge(S("m_in"), 16 * h)
                nc.vector.tensor_copy(mrow[96:97, 0, :], bank(7)[96:97, 0:T]).then_inc(S("mrow_high"), 1)
                dve.wait_ge(S("mrow_high"), h + 1)
                tt(mrow[96:97, 1, :], bank(7)[96:97, 0:T], mrow[96:97, 0, :].bitcast(F32), ALU.subtract)\
                    .then_inc(S("mrow_ready"), 1)

            def slots(p, first, after, last_pair=False):
                for i in range(first, after):
                    par, j = divmod(i, SLOTS)
                    if j in S_NEXT and not (last_pair and par == 1):
                        s = S_NEXT[j]
                        dve.wait_ge(S("s_full"), p * 16 + (8 * (par + 1) + s + 1))
                        take_max(s, (par + 1) % 2)
                        if s == 7:
                            keep_max((par + 1) % 2, p * 2 + (par + 1))
                    if j in S_AFTER and not last_pair:
                        s = S_AFTER[j]
                        dve.wait_ge(S("s_full"), p * 16 + (8 * (par + 2) + s + 1))
                        take_max(s, par)
                    if j == M_AT + 1 and not (last_pair and par == 1):
                        split_row(p * 2 + (par + 1))
                    if i % 4 == 3:
                        q = i // 4
                        dve.wait_ge(S("exp_done"), p * 32 + (i + 3))
                        dve.wait_ge(S("pv_done"), p * 32 + (i + 1))
                        nc.vector.tensor_copy(prob_hi[:, 3, :], prob[:, 3, :]).then_inc(S("high_dve"), 1)
                        dve.wait_ge(S("high_dve"), p * 8 + (q + 1))
                        tt(prob_lo[:, 3, :], prob[:, 3, :], prob_hi[:, 3, :].bitcast(F32), ALU.subtract)\
                            .then_inc(S("low_dve"), 1)
                    if i == SLOTS + 2:
                        keep_head(p * 2, 0)

            def keep_head(h, k):
                dve.wait_ge(S("pv_done"), h * SLOTS + (SLOTS + 4))
                dve.wait_ge(S("o_in"), h * 48 + 48)
                nc.vector.tensor_copy(ostage[:, k, :], bank(6 + k)[0:2 * HD + 1, 0:T]).then_inc(S("o_staged"), 1)

            dve.wait_ge(S("K_out"), 17 * 16)
            for h, n in ((0, 8), (1, 5)):
                for s in range(n):
                    dve.wait_ge(S("s_full"), 8 * h + s + 1)
                    take_max(s, h)
                if h == 0:
                    keep_max(0, 0)
                    split_row(0)
            LATE = 3
            slots(0, 0, LATE)
            with dve.Fori(0, PAIRS - 1) as p:
                slots(p, LATE, 2 * SLOTS)
                slots(p + 1, 0, LATE)
                keep_head(p * 2 + 1, 1)
            slots(PAIRS - 1, LATE, 2 * SLOTS, True)
            keep_head(H - 1, 1)
            dve.wait_ge(S("o_in"), 48 * H + 48)
            f = lambda v: v[:, :, :].rearrange("p m t -> p (m t)")
            link(tt(f(oh), f(oh), f(ol), ALU.add))
            link(nc.vector.reciprocal(f(osum), f(osum)))
            tt(f(zT), f(oh), f(osum), ALU.mult).then_inc(S("aT"), 1)
            for t in range(TT):
                dve.wait_ge(S("projected"), t + 1)
                tt(x[:, t, :], x[:, t, :], bank(t)[:, 0:D], ALU.add).then_inc(S("x_new"), 1)
            dve.wait_ge(S("x_new"), 2)

            def add_tokens(b, full, done):
                dve.wait_ge(S(full), 1)
                v = bank(b).rearrange("p (t d) -> p t d", t=TT)
                link(tt(x[:, :, :], x[:, :, :], v, ALU.add))
                nc.vector.sem_inc(S(done), 2)

            ln_stats(dve, link, "ln1", x)
            dve.wait_ge(S("qkv_full"), 1)
            dve.wait_ge(S("self_in"), 16 * 5)
            for t in range(TT):
                for c in range(2):
                    last = tt(qkv[:, t, c * 384:(c + 1) * 384], bank(2 * t + c)[:, 0:384], bqkv[:, c * 384:(c + 1) * 384], ALU.add)
            link(last)
            qkvh = [qkv[:, t, :].rearrange("p (h c) -> p h c", c=3 * HD) for t in range(TT)]
            for n in range(4):
                t, half = divmod(n, 2)
                hs = slice(8 * half, 8 * half + 8)
                q4 = qkvh[t][:, hs, 0:HD].unsqueeze(2).broadcast_to([P, 8, H, HD])
                k4 = qkvh[t][:, :, HD:2 * HD].unsqueeze(1).broadcast_to([P, 8, H, HD])
                pr = prod[:, n % 2, :].rearrange("p (h g d) -> p h g d", h=8, g=H)
                link(tt(pr, q4, k4, ALU.mult))
                link(nc.vector.tensor_reduce(sc[:, t, half * 128:half * 128 + 128],
                                             prod[:, n % 2, :].rearrange("p (a d) -> p a d", d=HD), AX, ALU.add))
            s3 = sc[:, :, :].rearrange("p t (h g) -> p (t h) g", g=H)
            st_ = small[:, 96:128]
            bg = st_.unsqueeze(2).broadcast_to([P, 2 * H, H])
            link(nc.vector.tensor_reduce(st_, s3, AX, ALU.max))
            tt(s3, s3, bg, ALU.subtract).then_inc(S("sc_ready"), 1)
            absmax = lambda o, i: nc.vector.tensor_reduce(o, i, AX, ALU.max, apply_absolute_value=True)
            dve.wait_ge(S("wffn_in"), 16 * 7)
            dve.wait_ge(S("pool_chain2"), 1)
            nc.vector.tensor_copy(identb[:, :], ident[:, :])
            absmax(small[:, 0:6], wraw[:, 0])
            absmax(small[:, 6:12], wraw[:, 1])
            link(absmax(small[:, 12:14], wdraw[:, :, :]))
            link(ts(small[:, 0:14], small[:, 0:14], 1 / QMAX, None, ALU.mult))
            nc.vector.reciprocal(small[:, 16:30], small[:, 0:14]).then_inc(S("wscales"), 1)
            dve.wait_ge(S("sc_exp"), 1)
            link(nc.vector.tensor_reduce(st_, s3, AX, ALU.add))
            link(nc.vector.reciprocal(st_, st_))
            link(tt(s3, s3, bg, ALU.mult))
            for n in range(4):
                t, half = divmod(n, 2)
                a4 = sc[:, t, half * 128:half * 128 + 128].rearrange("p (h g) -> p h g", g=H).unsqueeze(2)\
                    .broadcast_to([P, 8, HD, H])
                v4 = qkvh[t][:, :, 2 * HD:3 * HD].rearrange("p g d -> p d g").unsqueeze(1).broadcast_to([P, 8, HD, H])
                pr = prod[:, n % 2, :].rearrange("p (h d g) -> p h d g", h=8, d=HD)
                link(tt(pr, a4, v4, ALU.mult))
                link(nc.vector.tensor_reduce(z[:, t, half * 128:half * 128 + 128],
                                             prod[:, n % 2, :].rearrange("p (a g) -> p a g", g=H), AX, ALU.add))
            nc.vector.sem_inc(S("z_ready"), 1)
            dve.wait_ge(S("self_in"), 16 * 5)
            link(tt(x[:, :, :], x[:, :, :], bout[:, :].unsqueeze(1).broadcast_to([P, TT, D]), ALU.add))
            for t in range(TT):
                dve.wait_ge(S("projected"), TT + t + 1)
                tt(x[:, t, :], x[:, t, :], bank(t)[:, 0:D], ALU.add).then_inc(S("x_new"), 1)
            dve.wait_ge(S("x_new"), 4)

            dve.wait_ge(S("clip_exp"), 1)
            link(ts(small[:, 32:34], small[:, 32:34], 1.0, None, ALU.add))
            link(nc.vector.reciprocal(small[:, 32:34], small[:, 32:34]))
            link(ts(small[:, 32:34], small[:, 32:34], 1 / QMAX, None, ALU.mult))
            ln_stats(dve, link, "ln2", x)
            absmax(small[:, 34:35], z[:, :, :].rearrange("p t d -> p (t d)")).then_inc(S("absmax_part"), 1)
            dve.wait_ge(S("absmax_all"), 1)
            link(tt(small[:, 38:39], small[:, 36:37], small[:, 32:33], ALU.mult))
            link(nc.vector.reciprocal(small[:, 54:55], small[:, 38:39]))

            def quantise(to, v, inv, done):
                link(ts(v, v, inv, QMAX, ALU.mult, ALU.min))
                link(ts(v, v, -QMAX - 1, ROUND, ALU.max, ALU.add))
                ts(to, v, ROUND, None, ALU.subtract).then_inc(S(done), 1)

            quantise(z[:, :, :], z[:, :, :], small[:, 54:55], "z_ready")
            dve.wait_ge(S("wscales"), 1)
            link(ts(small[:, 40:52], small[:, 0:12], small[:, 38:39], None, ALU.mult))
            nc.vector.sem_inc(S("comb_ready"), 1)
            dve.wait_ge(S("wints"), 3)
            link(nc.vector.memset(hf[64:P, 5, :], 0.0))
            for i, r in enumerate(FR):
                dve.wait_ge(S("sg_ready"), i + 1)
                stt(hf[0:r, i, :], bank(i)[0:r, T:2 * T], small[0:r, 46 + i:47 + i], sg[0:r, i, :], ALU.mult, ALU.mult)\
                    .then_inc(S("hf_ready"), 1)
            dve.wait_ge(S("hf_ready"), 6)
            absmax(small[:, 35:36], hf[:, :, :].rearrange("p i t -> p (i t)")).then_inc(S("absmax_part"), 1)
            dve.wait_ge(S("absmax_all"), 2)
            link(tt(small[:, 39:40], small[:, 37:38], small[:, 33:34], ALU.mult))
            link(nc.vector.reciprocal(small[:, 55:56], small[:, 39:40]))
            link(ts(small[:, 56:58], small[:, 12:14], small[:, 39:40], None, ALU.mult))
            quantise(hq[:, :, :], hf[:, :, :], small[:, 55:56], "hq_ready")
            add_tokens(7, "ffn_y", "x_new")
            nc.vector.sem_inc(S("hq_used"), 1)

            ln_stats(dve, link, "ln3", x)
            link(nc.vector.tensor_copy(xt[:, :, :], z[:, :, :]))
            dve.wait_ge(S("film_in"), 16 * 18)
            link(nc.vector.tensor_copy(tmask[:, :], tmask_u[:, :]))
            for n in range(8):
                t, h = divmod(n, 4)
                a, b, k8 = Asc[:, n % 2, :], EB[:, n % 2, :], m8[:, n % 2, :]
                dve.wait_ge(S("A_masked"), n + 1)
                if n >= 2:
                    dve.wait_ge(S("E_scaled"), n - 1)
                    dve.wait_ge(S("E_added"), (n - 2) // 4 * 3 + (n - 2) % 4)
                for rnd in range(4):
                    src = a if rnd == 0 else b
                    link(nc.vector.max(k8[:, 8 * rnd:8 * rnd + 8], src))
                    link(nc.vector.match_replace(b, k8[:, 8 * rnd:8 * rnd + 8], src, -3e38))
                link(ts(b, b, -2.9e38, LOW, ALU.is_ge, ALU.mult))
                link(tt(a, a, b, ALU.add))
                ts(small[:, 64 + n % 2:65 + n % 2], k8[:, 0:1], -1.0, None, ALU.mult).then_inc(S("top_found"), 1)
                dve.wait_ge(S("E_ready"), n + 1)
                link(stt(b, a, k8[:, 31:32], b, ALU.is_ge, ALU.mult, accum_out=small[:, 68 + n % 2:69 + n % 2]))
                nc.vector.sem_inc(S("top_weighed"), 1)
                link(nc.vector.reciprocal(small[:, 68 + n % 2:69 + n % 2], small[:, 68 + n % 2:69 + n % 2]))
                ts(small[:, 66 + n % 2:67 + n % 2], small[:, 68 + n % 2:69 + n % 2], 0.25, tmask[:, t:t + 1],
                   ALU.mult, ALU.mult).then_inc(S("r_ready"), 1)

            dve.wait_ge(S("film_in"), 16 * 18)
            ln_stats(dve, link, "xin", xt, 0)
            both = lambda v: v.unsqueeze(1).broadcast_to([P, TT, v.shape[-1]])

            def modulate(v, b, bias, full):
                fm = Gh[:, 0:4, :].rearrange("p (t a) d -> p t (a d)", t=TT)
                for t in range(TT):
                    dve.wait_ge(S(full), t + 1)
                    last = tt(fm[:, t, :], bank(b + t), bias, ALU.add)
                link(last)
                link(ts(fm, fm, gate[:, 0:1], None, ALU.mult))
                link(stt(fm[:, :, 0:D], fm[:, :, 0:D], 1.0, v, ALU.add, ALU.mult))
                link(tt(v, fm[:, :, 0:D], fm[:, :, D:2 * D], ALU.add))

            dve.wait_ge(S("zc_ready"), 2)
            modulate(z[:, :, :], 1, bfi[:, :], "film_in_full")
            nc.vector.sem_inc(S("u_ready"), 1)
            link(tt(y[:, :, :], z[:, :, :], both(dskip[:, :]), ALU.mult))
            dve.wait_ge(S("U_full"), 1)
            re, im = bank(6), bank(7)
            kre, kim = (Kf[:, 2 * n:2 * n + 2, :].rearrange("p a d -> p (a d)") for n in range(2))
            yre, yim = (Yf[:, 2 * n:2 * n + 2, :].rearrange("p a d -> p (a d)") for n in range(2))
            tmp = Gh[:, 0:2, :].rearrange("p a d -> p (a d)")
            link(tt(yre, re, kre, ALU.mult))
            link(tt(tmp, im, kim, ALU.mult))
            link(tt(yre, yre, tmp, ALU.subtract))
            link(tt(yim, re, kim, ALU.mult))
            link(tt(tmp, im, kre, ALU.mult))
            tt(yim, yim, tmp, ALU.add).then_inc(S("Y_ready"), 1)
            dve.wait_ge(S("y_full"), 1)
            link(tt(y[:, :, :], y[:, :, :], bank(5).rearrange("p (t d) -> p t d", t=TT), ALU.add))
            modulate(y[:, :, :], 3, bfo[:, :], "film_out_full")
            link(tt(xt[:, :, :], xt[:, :, :], y[:, :, :], ALU.add))
            ln_stats(dve, link, "ln4", xt, 2)
            link(tt(xt[:, :, :], xt[:, :, :], both(b2[:, :]), ALU.add))
            dve.wait_ge(S("h2_full"), 1)
            for t in range(TT):
                last = tt(xt[:, t, :], xt[:, t, :], bank(4 + t)[:, 0:D], ALU.add)
            link(last)
            ln_stats(dve, link, "nout", xt, 4)
            link(tt(x[:, :, :], x[:, :, :], z[:, :, :], ALU.add))
            nc.vector.sem_inc(S("x_new"), 2)

            ln_stats(dve, link, "ln5", x)
            dve.wait_ge(S("gru_act"), 2)
            for m in range(2):
                last = nc.vector.tensor_tensor_scan(cT[:, m, :], gt[:, m, :], cd[:, m, :], 0.0, ALU.mult, ALU.add)
            last.then_inc(S("gru_done"), 1)
            add_tokens(2, "gru_y", "x_new")

            ln_stats(dve, link, "ln6", x)
            dve.wait_ge(S("rest_in"), 16 * 6)
            dve.wait_ge(S("rscores"), 1)
            link(tt(rt[:, 1, :, :], rt[:, 0, :, :], both(rbias[:, :]), ALU.add))
            for t in range(TT):
                k8 = small[:, 72 + 8 * t:80 + 8 * t]
                link(nc.vector.max(k8, rt[:, 1, t, :]))
                link(nc.vector.match_replace(rt[:, 2, t, :], k8, rt[:, 1, t, :], -3e38))
            link(tt(rt[:, 2, :, :], rt[:, 2, :, :], rt[:, 1, :, :], ALU.not_equal))
            link(tt(rt[:, 2, :, :], rt[:, 2, :, :], rt[:, 0, :, :], ALU.mult))
            link(nc.vector.tensor_reduce(small[:, 88:90], rt[:, 2, :, :], AX, ALU.add))
            link(ts(small[:, 88:90], small[:, 88:90], 1e-20, None, ALU.add))
            link(nc.vector.reciprocal(small[:, 88:90], small[:, 88:90]))
            for t in range(TT):
                last = ts(rt[:, 2, t, :], rt[:, 2, t, :], small[:, 88 + t:89 + t], 2.5, ALU.mult, ALU.mult)
            link(last)
            nc.vector.sem_inc(S("wtok"), 1)
            for n in range(E + 4):
                b = n % 2
                dve.wait_ge(S("unit_silu"), n + 1)
                if n >= 2:
                    dve.wait_ge(S("unit_done"), n - 1)
                if n < 4:
                    tt(ehw[:, b, :], bank(b)[:, T:2 * T], esg[:, b, :], ALU.mult).then_inc(S("unit_ready"), 1)
                    nc.vector.sem_inc(S("unit_read"), 1)
                    continue
                link(ts(euc[:, b, :], bank(b)[:, T:2 * T], 7.0, -7.0, ALU.min, ALU.max))
                link(stt(euc[:, b, :], esg[:, b, :], SILU7, euc[:, b, :], ALU.min, ALU.mult))
                tt(ehw[:, b, :], euc[:, b, :], bank(2 + b)[:, 0:T], ALU.mult).then_inc(S("unit_ready"), 1)
                dve.wait_ge(S("unit_ready"), n + 1)
                nc.vector.sem_inc(S("unit_read"), 1)
            dve.wait_ge(S("unit_done"), E + 4)
            for t in range(TT):
                tt(x[:, t, :], x[:, t, :], bank(4 + t)[:, 0:D], ALU.add).then_inc(S("x_new"), 1)


def laid_out(inputs):
    import numpy as np

    i = {name: np.asarray(a) for name, a in inputs.items()}
    turned = lambda a: np.ascontiguousarray(a.T)
    flags = lambda a: np.ascontiguousarray(a).view(np.uint8)
    a = {name: i[name] for name in (
        "L0_xattn_Wq", "L0_xattn_Wk", "L0_xattn_Wv", "L0_xattn_Wo", "L0_attn_W_qkv", "L0_attn_b_qkv", "L0_attn_W_out",
        "L0_attn_b_out", "L0_ffn_clip_x", "L0_ffn_clip_down", "L0_ffn_w_gate", "L0_ffn_w_up", "L0_ffn_w_down",
        "L1_xattn_Wq", "L1_xattn_Wk", "L1_xattn_Wv", "L1_xattn_W_film_in", "L1_xattn_b_film_in", "L1_xattn_W_film_out",
        "L1_xattn_b_film_out", "L1_xattn_g_norm_in", "L1_xattn_b_norm_in", "L1_xattn_g_norm_out", "L1_xattn_b_norm_out",
        "L1_xattn_g_ffn", "L1_xattn_b_ffn", "L1_xattn_W1", "L1_xattn_W2", "L1_xattn_b2", "L1_xattn_log_dt",
        "L1_xattn_D_skip", "L1_ffn_e_score_correction_bias")}
    a["L1_xattn_mod_gate"] = i["L1_xattn_mod_gate"].reshape(1)
    a["x"] = i["x"][0]
    a["ctx"] = i["ctx_768"][0]
    a["ctxT"] = turned(i["ctx_768"][0])
    a["ctx_mask"] = flags(i["mask_BxS2_bf1"][0])
    a["text_mask"] = turned(flags(i["mask_BxS_bf1"][0]).reshape(TT, P))
    for name in ("A_re", "A_im", "C_re", "C_im"):
        a[name + "T"] = turned(i["L1_xattn_" + name])
    a["b1T"] = turned(i["L1_xattn_b1"].reshape(8, P))
    for name in ("g", "c"):
        a[f"W{name}T"] = turned(i["L1_attn_W" + name])
        a[f"b{name}T"] = turned(i["L1_attn_b" + name].reshape(2, P))
    a["routerT"] = turned(i["L1_ffn_router_weight"])
    a["gupT"] = np.ascontiguousarray(i["L1_ffn_gate_up_proj"].reshape(E, 2 * I, 2, P).transpose(3, 0, 2, 1))
    a["downT"] = np.ascontiguousarray(i["L1_ffn_down_proj"].transpose(2, 0, 1))
    both = np.stack([i["L1_ffn_shared_gate"], i["L1_ffn_shared_up"]])
    a["sguT"] = np.ascontiguousarray(both.reshape(2, 512, 2, P).transpose(3, 2, 0, 1).reshape(P, -1))
    a["sdnT"] = np.ascontiguousarray(i["L1_ffn_shared_down"].reshape(D, 4, P).transpose(2, 1, 0).reshape(P, -1))

    a["ident"] = np.eye(P, dtype=np.float32)
    j = np.arange(LA, dtype=np.float32)
    a["lfac"] = np.tile(np.concatenate([LA * j, j]), (P, 1))
    phase = np.zeros((P, 8), np.float32)
    phase[:NS, 0], phase[NS:, 0] = -1, 1
    phase[:NS, 1], phase[NS:, 1] = 1, -1
    phase[:NS, 3] = phase[NS:, 4] = np.pi / 2
    a["phase"] = phase
    angle = np.outer(np.arange(T), (np.arange(T) + 0.5) * (np.pi / T))
    table = np.concatenate([np.cos(angle), -np.sin(angle)], 1)
    a["dft"] = table.astype(np.float32)
    a["dftT"] = turned((table / T).astype(np.float32))
    return a


def kernel(**inputs):
    import numpy as np
    import concourse.bacc as bacc
    from concourse import mybir
    from concourse.bass_utils import run_bass_kernel_spmd

    nc = bacc.Bacc("TRN2", target_bir_lowering=False, num_devices=1)
    arrays, A = {}, {}
    for name, a in laid_out(inputs).items():
        a = np.ascontiguousarray(a)
        arrays[f"in_{name}_dram"] = a
        A[name] = nc.dram_tensor(f"in_{name}_dram", a.shape, mybir.dt.from_np(a.dtype), kind="ExternalInput").ap()
    out = nc.dram_tensor("out_0_dram", (1, T, D), F32, kind="ExternalOutput").ap()
    perceiver_kernel(nc, A, out[0])
    r = run_bass_kernel_spmd(nc, [arrays], core_ids=[0])
    return r.results[0]["out_0_dram"]
```

```python
from contextlib import ExitStack
from math import exp, pi

import numpy as np

import concourse.bass as bass
from concourse import mybir
from concourse.alu_op_type import AluOpType as ALU

F32 = mybir.dt.float32
F32R = mybir.dt.float32r
BF16 = mybir.dt.bfloat16
U8 = mybir.dt.uint8
ACT = mybir.ActivationFunctionType
AX = mybir.AxisListType.X
RMAX = bass.bass_isa.ReduceOp.max

P = 128
T = 256
TT = T // P
D = 256
M = 4096
CD = 192
C1 = CD - P
KT = M // P
H = 16
HD = D // H
PAIRS = H // 2
BUFS = 8
SLOTS = 16
CH = M // 512
NEG = -2.0 ** 127
ROUND = 1.5 * 2.0 ** 23
NS = 64
LA = 16
E = 32
F_ = 704
FR = [min(P, F_ - i * P) for i in range(6)]
TAKEN = -3e38
LOW = -1e38
TOP = 32
PART = 64
ALL_FOUND = int(np.float32(TOP * P).view(np.int32))
SILU7 = 7.0 / (1.0 + exp(-7.0))
QMAX = 127.0
I = 128
SIN_MAX = 3.1415925
TWO_PI = (6.28125, 0.0019350051879882812, 3.0198482e-07)


def perceiver_kernel(nc, A, out):
    ctx = ExitStack()
    with ctx:
        sems = {}

        def S(name):
            if name not in sems:
                sems[name] = ctx.enter_context(nc.semaphore(name))
            return sems[name]

        def sb(name, shape, dt=F32, scope=None):
            return (scope or ctx).enter_context(nc.sbuf_tensor(name, shape, dt))

        def chain(eng, name):
            n = [0]

            def link(ins):
                n[0] += 1
                ins.then_inc(S(name), 1)
                eng.wait_ge(S(name), n[0])
                return ins
            return link

        PS = ctx.enter_context(nc.psum_tensor("PS", [P, 8, 512], F32))

        x = sb("x", [P, TT, D])
        z = sb("z", [P, TT, D])
        zT = sb("zT", [P, 2, T])
        ident = sb("ident", [P, P])
        stats = sb("stats", [P, TT, 6])
        mv = sb("mv", [P, TT, 2])
        sd = sb("sd", [P, TT])
        rs = sb("rs", [P, TT])
        eps = sb("eps", [P, 1])
        rows_scratch = nc.dram_tensor("rows_scratch", [16, M], F32).ap()
        q_scratch = nc.dram_tensor("q_scratch", [2, P, 2, T], F32).ap()
        K_scratch = nc.dram_tensor("K_scratch", [LA, LA, D], F32).ap()

        ph1 = ExitStack()
        qst = sb("qst", [P, 4, T], F32R, ph1)
        k_hi = sb("k_hi", [P, 2, M], F32R, ph1)
        k_lo = sb("k_lo", [P, 2, M], F32R, ph1)
        vst = sb("vst", [P, KT, H, 2 * HD + 1], F32R, ph1)
        sub = ExitStack()
        ctxT = sb("ctxT", [P, 2, M], F32, sub)
        sub.close()
        kst = sb("kst", [P, 2, M], F32R, ph1)
        prep = ExitStack()
        q_hi = sb("q_hi", [P, 2, T], F32R, prep)
        q_lo = sb("q_lo", [P, 2, T], F32R, prep)
        wv = sb("wv", [P, 2, D], F32, prep)
        s4 = sb("s4", [P, 4, D], F32, prep)
        dtb = sb("dtb", [P, D], F32, prep)
        sw = sb("sw", [P, 5, D], F32, prep)
        fac = sb("fac", [P, 2 * LA], F32, prep)
        phs = sb("phs", [P, 8], F32, prep)
        mku = sb("mku", [P, 32], U8, prep)
        ang = sb("ang", [P, 2, LA, 2 * LA], F32, prep)
        kk = sb("kk", [P, 2, LA, 2 * LA], F32, prep)
        yA = kk
        mag = sb("mag", [P, LA, 2 * LA], F32, prep)
        maskb = mag
        SV = sb("SV", [P, LA, 2 * LA], F32, prep)
        T2 = sb("T2", [P, LA, LA], F32, prep)
        first = ExitStack()
        wq = sb("wq", [P, 2, D], F32, first)
        wk = sb("wk", [P, 2, D], F32, first)
        first.close()
        UV = sb("UV", [P, 2, LA, 2 * LA], F32, prep)
        Kstage = sw[0:LA, 3:5, :]
        prep.close()
        loop = ExitStack()
        whole = ExitStack()
        prob = sb("prob", [P, BUFS, 512], F32, whole)
        whole.close()
        prob_lo = sb("prob_lo", [P, BUFS, 512], F32R, loop)
        prob_hi = sb("prob_hi", [P, BUFS, 512], F32R, loop)
        mxp = sb("mxp", [P, 2, 8], F32, loop)
        mx = sb("mx", [P, 2, TT], F32, loop)
        rows = sb("rows", [P, 2, T], F32, loop)
        mrow = rows[:, :, :].bitcast(F32R)
        ostage = rows[0:2 * HD + 1, :, :]
        oh, ol, osum = x, zT, z
        loop.close()
        ph1.close()
        small = sb("small", [P, 128])
        zc = sb("zc", [P, 2, T])
        identb = sb("identb", [P, P], BF16)
        q1 = sb("q1", [P, T])
        xt = sb("xt", [P, TT, D])
        wo = sb("wo", [P, 2, D])
        wqkv = sb("wqkv", [P, 2, 3 * D])
        bqkv = sb("bqkv", [P, 3 * D])
        wout = sb("wout", [P, 2, D])
        bout = sb("bout", [P, D])
        clips = sb("clips", [P, 2])
        wq1 = sb("wq1", [P, 2, P])
        wk1 = sb("wk1", [P, 2, P])
        wv1 = sb("wv1", [P, 2, D])
        wfi = sb("wfi", [P, 2, 2 * D])
        wfo = sb("wfo", [P, 2, 2 * D])
        bfi = sb("bfi", [P, 2 * D])
        bfo = sb("bfo", [P, 2 * D])
        gb = sb("gb", [P, 6, D])
        b1 = sb("b1", [P, 8])
        b2 = sb("b2", [P, D])
        dskip = sb("dskip", [P, D])
        gate = sb("gate", [P, 1])
        tmask_u = sb("tmask_u", [P, TT], U8)
        tmask = sb("tmask", [P, TT])
        dft = sb("dft", [P, 2, 2 * T])
        dftT = sb("dftT", [P, 4, T])
        Kf = sb("Kf", [P, 4, D])
        wgg = sb("wgg", [P, 2, D])
        wgc = sb("wgc", [P, 2, D])
        bgc = sb("bgc", [P, 2, 2])
        router = sb("router", [P, 2, E])
        rbias = sb("rbias", [P, E])
        cT = sb("cT", [P, 2, T])
        y = sb("y", [P, TT, D])
        Kt = y
        big = ExitStack()
        over_ctx = ExitStack()
        ctxT2 = sb("ctxT2", [P, 2, M], F32, over_ctx)
        over_ctx.close()
        EB = sb("EB", [P, 2, M], F32, big)
        k1T = sb("k1T", [P, M], F32, big)
        attn = ExitStack()
        prod = sb("prod", [P, 2, 8 * H * HD], F32, attn)
        qkv = sb("qkv", [P, TT, 3 * D], F32, attn)
        sc = sb("sc", [P, TT, H * H], F32, attn)
        attn.close()
        AM = sb("AM", [P, M], F32, big)
        ctxn = sb("ctxn", [P, KT, CD], F32, big)
        ffn = ExitStack()
        wraw = sb("wraw", [P, 2, 6, D], F32, ffn)
        wdraw = sb("wdraw", [P, 2, F_], F32, ffn)
        wint = sb("wint", [P, 2, 6, D], BF16, ffn)
        wdint = sb("wdint", [P, 2, F_], BF16, ffn)
        guT = sb("guT", [P, 2, 2, F_], BF16, ffn)
        wdT = sb("wdT", [P, 6, D], BF16, ffn)
        xqT = sb("xqT", [P, 2, T], BF16, ffn)
        sg, hf = wraw[:, 0], wraw[:, 1]
        hq = sb("hq", [P, 6, T], BF16, ffn)
        ffn.close()
        Asc = sb("Asc", [P, 3, M], F32, big)
        cand, cand_left = (v[:, :, :].rearrange("p t d -> p (t d)") for v in (y, zT))
        mask8, mask8b = ([v[32 * h:32 * h + 8] for h in range(4)] for v in (bqkv[:, 0:512], cT[:, 0, :].bitcast(BF16)))
        AMT = wqkv[:, :, 0:4 * P].rearrange("p n (u t) -> p n u t", u=4)
        m8 = sb("m8", [P, 2, 32], F32, big)
        big.close()
        moe = ExitStack()
        Gh = sb("Gh", [P, 8, T], F32, moe)
        Yf = sb("Yf", [P, 4, D], F32, moe)
        gup = sb("gup", [P, E, 2, 2 * I], F32, moe)
        down = sb("down", [P, E, D], F32, moe)
        sgu = sb("sgu", [P, 2, 2, 512], F32, moe)
        sdn = sb("sdn", [P, 4, D], F32, moe)
        dense = ExitStack()
        w1 = sb("w1", [P, 2, 4 * D], F32, dense)
        w2 = sb("w2", [P, 8, D], F32, dense)
        dense.close()
        esg = sb("esg", [P, 2, T], F32, moe)
        euc = sb("euc", [P, 2, T], F32, moe)
        ehw = sb("ehw", [P, 2, T], F32, moe)
        gt = sb("gt", [P, 2, T], F32, moe)
        cd = sb("cd", [P, 2, T], F32, moe)
        wT = sb("wT", [E, T], F32, moe)
        rt = sb("rt", [P, 4, TT, E], F32, moe)
        moe.close()

        bank = lambda b: PS[:, b, :]
        at = lambda *tags: {tag: n + 1 for n, tag in enumerate(tags)}
        LN = at("ln0", "ln1", "ln2", "ln3", "xin", "ln4", "nout", "ln5", "ln6")
        Z = at("ln0", "ln1", "attn_out", "ln2", "ffn_q", "ln3", "xin", "ln4", "nout", "ln5", "ln6")
        ZT = at("ln0", "ln1", "attn_out", "ffn_q", "ln3", "ln4", "ln5", "ln6")

        def ln_stats(dve, link, tag, src, affine=None):
            for t in range(TT):
                last = nc.vector.bn_stats(stats[:, t, :], src[:, t, :])
            link(last)
            for t in range(TT):
                last = nc.vector.bn_aggr(mv[:, t, :], stats[:, t, :])
            last.then_inc(S("ln_var"), 1)
            dve.wait_ge(S("ln_sd"), LN[tag])
            link(nc.vector.reciprocal(rs[:, :], sd[:, :]))
            for t in range(TT):
                last = nc.vector.tensor_scalar(z[:, t, :], src[:, t, :], mv[:, t, 0:1], rs[:, t:t + 1],
                                               ALU.subtract, ALU.mult)
            if affine is not None:
                link(last)
                g, s = (gb[:, affine + n, :].unsqueeze(1).broadcast_to([P, TT, D]) for n in range(2))
                link(nc.vector.tensor_tensor(z[:, :, :], z[:, :, :], g, ALU.mult))
                last = nc.vector.tensor_tensor(z[:, :, :], z[:, :, :], s, ALU.add)
            last.then_inc(S("z_ready"), 1)
            dve.wait_ge(S("z_ready"), Z[tag])

        def ln_sqrt(act, tag):
            act.wait_ge(S("ln_var"), LN[tag])
            nc.scalar.activation(sd[:, :], mv[:, :, 1], ACT.Sqrt, bias=eps[:, 0:1]).then_inc(S("ln_sd"), 1)

        def to_features(pe, src, b, tag):
            pe.wait_ge(S("z_ready"), Z[tag])
            for m in range(2):
                for t in range(TT):
                    last = nc.tensor.transpose(bank(b)[:, m * T + t * P:m * T + (t + 1) * P],
                                               src[:, t, m * P:(m + 1) * P], ident[:, :])
            last.then_inc(S("zT_full"), 1)

        def keep_features(act, dst, b, tag):
            act.wait_ge(S("zT_full"), ZT[tag])
            nc.scalar.copy(dst[:, :, :], bank(b)).then_inc(S("zT_kept"), 1)

        S_NEXT = {0: 5, 2: 6, 4: 7}
        S_AFTER = {6: 0, 8: 1, 10: 2, 12: 3, 14: 4}
        M_AT = 8
        DVE_EARLY = 1
        AHEAD = 4

        block = ctx.enter_context(nc.Block())

        @block.sync
        def _(sp):
            def move(to, rows_, done):
                sp.dma_start(to.bitcast(F32), rows_.bitcast(F32)).then_inc(S(done), 16)

            sp.dma_start(x[:, :, :], A["x"].rearrange("(t p) d -> p t d", p=P)).then_inc(S("x_in"), 16)
            sp.dma_start(wk[:, 0, :], A["L0_xattn_Wk"][0:P, :]).then_inc(S("wk_in"), 16)
            sp.dma_start(wk[0:C1, 1, :], A["L0_xattn_Wk"][P:CD, :]).then_inc(S("wk_in"), 16)
            for c in range(4):
                cs = slice(c * 1024, (c + 1) * 1024)
                sp.dma_start(ctxT[:, 0, cs], A["ctxT"][0:P, cs]).then_inc(S(f"ctxT_in{c}"), 16)
                sp.dma_start(ctxT[0:C1, 1, cs], A["ctxT"][P:CD, cs]).then_inc(S(f"ctxT_in{c}"), 16)
                if c == 0:
                    sp.dma_start(ident[:, :], A["ident"]).then_inc(S("ident_in"), 16)
                    sp.dma_start(wq[:, :, :], A["L0_xattn_Wq"].rearrange("(k p) d -> p k d", p=P)).then_inc(S("wq_in"), 16)
                    sp.dma_start(fac[:, :], A["lfac"]).then_inc(S("s4_in"), 16)
                    sp.dma_start(phs[:, :], A["phase"]).then_inc(S("s4_in"), 16)
                    sp.dma_start(dtb[:, :], A["L1_xattn_log_dt"].partition_broadcast(P)).then_inc(S("s4_in"), 16)
                    for n, name in enumerate(("A_reT", "A_imT", "C_reT", "C_imT")):
                        for half in range(2):
                            sp.dma_start(s4[NS * half:NS * (half + 1), n, :], A[name]).then_inc(S("s4_in"), 16)
                    sp.dma_start(mku[:, :], A["ctx_mask"].rearrange("(p j) -> p j", p=P)).then_inc(S("mku_in"), 16)
                if c == 1:
                    sp.dma_start(wv[:, 0, :], A["L0_xattn_Wv"][0:P, :]).then_inc(S("wv_in"), 16)
                    sp.dma_start(wv[0:C1, 1, :], A["L0_xattn_Wv"][P:CD, :]).then_inc(S("wv_in"), 16)
            sp.wait_ge(S("maskb_ready"), 1)
            sp.dma_start(rows_scratch.rearrange("r (p j) -> p r j", p=P), maskb[:, :, :]).then_inc(S("mask_out"), 16)
            def store_kernel(n):
                sp.wait_ge(S("K_staged"), n + 2)
                sp.dma_start(K_scratch[:, :, LA * n:LA * (n + 1)],
                             Kstage[:, n % 2, :].rearrange("a (b d) -> a b d", d=LA)).then_inc(S("K_out"), 16)

            sp.wait_ge(S("q_lo_ready"), 2)
            for n, q in enumerate((q_hi, q_lo)):
                move(q_scratch[n], q[:, :, :], "q_out")
            for n in range(5):
                store_kernel(n)
            sp.wait_ge(S("kv_low"), 4 + 32)
            sp.wait_ge(S("mask_out"), 16)
            for s in range(2):
                for par in range(2):
                    sp.dma_start(kst[64 * par + 48:64 * par + 64, s, :].bitcast(F32), rows_scratch).then_inc(S("kmask_in"), 16)

            def load_stack(p):
                for par in range(2):
                    src = 32 * (p % 4) + HD * par
                    for r, k in enumerate((k_hi, k_hi, k_lo)):
                        b = 64 * par + HD * r
                        move(kst[b:b + HD, p % 2, :], k[src:src + HD, p // 4, :], "kst_in")

            def load_queries(h):
                if h >= 4:
                    sp.wait_ge(S("st_full"), SLOTS * (h - 3))
                b, f = 64 * (h % 2), slice(HD * (h % 8), HD * (h % 8 + 1))
                for r, part in enumerate((0, 1, 0)):
                    move(qst[b + HD * r:b + HD * (r + 1), h % 4, :], q_scratch[part, f, h // 8, :], f"q_in{h % 4}")
                sp.dma_start(qst[b + 48:b + 62, h % 4, :].bitcast(F32), rows_scratch[2:16, 0:T])\
                    .then_inc(S(f"q_in{h % 4}"), 16)

            def load_max(h):
                sp.wait_ge(S("mrow_ready"), h + 1)
                b = 64 * (h % 2) + 49
                move(qst[b:b + 2, h % 4, :], mrow[96:97, :, :], "m_in")

            def gather_head(h):
                sp.wait_ge(S("o_staged"), h + 3)
                f = slice(HD * (h % 8), HD * (h % 8 + 1))
                st = ostage[:, h % 2, :]
                sp.dma_start(oh[f, h // 8, :], st[0:HD, :]).then_inc(S("o_in"), 16)
                sp.dma_start(ol[f, h // 8, :], st[HD + 1:2 * HD + 1, :]).then_inc(S("o_in"), 16)
                sp.dma_start(osum[f, h // 8, :], st[HD:HD + 1, :].unsqueeze(1).broadcast_to([1, HD, T])).then_inc(S("o_in"), 16)

            store_kernel(5)
            load_stack(0)
            store_kernel(6)
            load_stack(1)
            store_kernel(7)
            sp.wait_ge(S("q_out"), 32)
            sp.wait_ge(S("stacks_set"), 2)
            for h in range(4):
                load_queries(h)
                store_kernel(8 + h)
            for n in range(12, 16):
                store_kernel(n)
            def load(to, rows_, done):
                sp.dma_start(to, rows_).then_inc(S(done), 16)

            rows2 = lambda a: a.rearrange("(k p) n -> p k n", p=P)
            across = lambda a: a.partition_broadcast(P)

            def load_weights(part):
                if part == 0:
                    load(wo[:, :, :], rows2(A["L0_xattn_Wo"]), "self_in")
                    load(wqkv[:, :, :], rows2(A["L0_attn_W_qkv"]), "self_in")
                    load(bqkv[:, :], across(A["L0_attn_b_qkv"]), "self_in")
                elif part == 1:
                    load(wout[:, :, :], rows2(A["L0_attn_W_out"]), "self_in")
                    load(bout[:, :], across(A["L0_attn_b_out"]), "self_in")
                    load(clips[:, 0:1], across(A["L0_ffn_clip_x"]), "wffn_in")
                    load(clips[:, 1:2], across(A["L0_ffn_clip_down"]), "wffn_in")
                    load(wk1[:, 0, :], A["L1_xattn_Wk"][0:P, :], "keys2_in")
                    load(wk1[0:C1, 1, :], A["L1_xattn_Wk"][P:CD, :], "keys2_in")
                elif part == 2:
                    load(dft[:, :, :], rows2(A["dft"]), "keys2_in")
                    load(dftT[:, :, :], rows2(A["dftT"]), "keys2_in")
                    load(wq1[:, :, :], rows2(A["L1_xattn_Wq"]), "film_in")
                    load(tmask_u[:, :], A["text_mask"], "film_in")
                elif part == 3:
                    load(wv1[:, 0, :], A["L1_xattn_Wv"][0:P, :], "film_in")
                    load(wv1[0:C1, 1, :], A["L1_xattn_Wv"][P:CD, :], "film_in")
                    load(wfi[:, :, :], rows2(A["L1_xattn_W_film_in"]), "film_in")
                    load(wfo[:, :, :], rows2(A["L1_xattn_W_film_out"]), "film_in")
                elif part == 4:
                    load(bfi[:, :], across(A["L1_xattn_b_film_in"]), "film_in")
                    load(bfo[:, :], across(A["L1_xattn_b_film_out"]), "film_in")
                    load(bgc[:, 0, :], A["bgT"], "rest_in")
                    load(bgc[:, 1, :], A["bcT"], "rest_in")
                    load(router[:, :, :], rows2(A["routerT"]), "rest_in")
                    load(rbias[:, :], across(A["L1_ffn_e_score_correction_bias"]), "rest_in")
                    for n, name in enumerate(("g_norm_in", "b_norm_in", "g_ffn", "b_ffn", "g_norm_out", "b_norm_out")):
                        load(gb[:, n, :], across(A["L1_xattn_" + name]), "film_in")
                elif part == 5:
                    load(b2[:, :], across(A["L1_xattn_b2"]), "film_in")
                    load(dskip[:, :], across(A["L1_xattn_D_skip"]), "film_in")
                    load(gate[:, :], across(A["L1_xattn_mod_gate"]), "film_in")
                    load(b1[:, :], A["b1T"], "film_in")
                    load(wgg[:, :, :], rows2(A["WgT"]), "rest_in")
                    load(wgc[:, :, :], rows2(A["WcT"]), "rest_in")

            load_max(0)
            for p in range(PAIRS):
                if p == PAIRS - 2:
                    sp.wait_ge(S("kst_in"), 96 * PAIRS)
                load_max(2 * p + 1)
                if p + 2 < PAIRS:
                    load_queries(2 * p + 4)
                else:
                    load_weights(3 * (p - PAIRS + 2))
                gather_head(2 * p)
                if p + 2 >= PAIRS:
                    load_weights(3 * (p - PAIRS + 2) + 1)
                if p + 1 < PAIRS:
                    load_max(2 * p + 2)
                    if p + 2 < PAIRS:
                        sp.wait_ge(S("st_full"), 2 * SLOTS * (p + 1))
                        load_stack(p + 2)
                        load_queries(2 * p + 5)
                    else:
                        load_weights(2)
                gather_head(2 * p + 1)
            load_weights(5)
            sp.wait_ge(S("aT"), 1)
            load(x[:, :, :], A["x"].rearrange("(t p) d -> p t d", p=P), "x_in")
            for n, name in enumerate(("L0_ffn_w_gate", "L0_ffn_w_up")):
                load(wraw[:, n, 0:5, :], A[name][0:5 * P, :].rearrange("(i p) n -> p i n", p=P), "wffn_in")
                load(wraw[0:FR[5], n, 5, :], A[name][5 * P:F_, :], "wffn_in")
            load(wdraw[:, :, :], rows2(A["L0_ffn_w_down"]), "wffn_in")
            load(ctxT2[:, 0, :], A["ctxT"][0:P, :], "keys2_in")
            load(ctxT2[0:C1, 1, :], A["ctxT"][P:CD, :], "keys2_in")
            load(Kt[:, 0, :], K_scratch[0:8].rearrange("a b d -> (a b) d"), "keys2_in")
            load(Kt[:, 1, :], K_scratch[8:16].rearrange("a b d -> (a b) d"), "keys2_in")
            sp.wait_ge(S("x_new"), 4)
            load(ctxn[:, :, :], A["ctx"].rearrange("(k p) c -> p k c", p=P), "ctxn_in")
            for h in range(4):
                load(mask8[h], rows_scratch[0].rearrange("(c k) -> c k", c=8), "mask8_in")
            sp.wait_ge(S("zc_ready"), 2)
            load(w1[:, :, :], rows2(A["L1_xattn_W1"]), "w12_in")
            load(w2[:, :, :], rows2(A["L1_xattn_W2"]), "w12_in")
            load(sgu[:, :, :, :], A["sguT"].rearrange("p (k g i) -> p k g i", k=2, g=2), "shared_in")
            load(sdn[:, :, :], A["sdnT"].rearrange("p (k n) -> p k n", k=4), "shared_in")
            for g in range(4):
                es = slice(8 * g, 8 * g + 8)
                load(gup[:, es, :, :], A["gupT"][:, es, :, :], f"experts_in{g}")
                load(down[:, es, :], A["downT"][:, es, :], f"experts_in{g}")
            sp.wait_ge(S("x_new"), 12)
            sp.dma_start(out.rearrange("(t p) d -> p t d", p=P), x[:, :, :]).then_inc(S("out_done"), 16)
            sp.wait_ge(S("out_done"), 16)

        @block.tensor
        def _(pe):
            pe.wait_ge(S("wk_in"), 32)

            def fill_k(c, n):
                for j, m in enumerate((0, 1)):
                    b = n + j
                    for k in range(2):
                        r = P if k == 0 else C1
                        last = nc.tensor.matmul(bank(b), wk[0:r, k, m * P:(m + 1) * P],
                                                ctxT[0:r, k, bass.ds(c * 512, 512)], start=(k == 0), stop=(k == 1))
                    last.then_inc(S("fill"), 1)

            for i in range(4):
                pe.wait_ge(S(f"ctxT_in{i}"), 32)
                for u in range(2):
                    pe.wait_ge(S("kv_low"), 4 * i + 2 * u + 2)
                    fill_k(2 * i + u, 2 * u)
            pe.wait_ge(S("ident_in"), 16)
            to_features(pe, z, 4, "ln0")
            pe.wait_ge(S("zT_kept"), ZT["ln0"])
            pe.wait_ge(S("wq_in"), 16)
            for m in range(2):
                for k in range(2):
                    last = nc.tensor.matmul(bank(5)[:, m * T:(m + 1) * T], wq[:, k, m * P:(m + 1) * P], zT[:, k, :],
                                            start=(k == 0), stop=(k == 1))
                last.then_inc(S("q_full"), 1)
            pe.wait_ge(S("wv_in"), 32)
            def fill_v(n):
                pe.wait_ge(S("kv_low"), 16 + n + 1)
                for u in range(2):
                    for k in range(2):
                        r = P if k == 0 else C1
                        last = nc.tensor.matmul(bank(n % 4)[:, u * D:(u + 1) * D],
                                                ctxT[0:r, k, (2 * n + u) * P:(2 * n + u + 1) * P], wv[0:r, k, :],
                                                start=(k == 0), stop=(k == 1))
                last.then_inc(S("fill"), 1)

            for n in range(4):
                fill_v(n)
            for n in range(16):
                s = n % 2
                pe.wait_ge(S("uv_ready"), n + 2)
                pe.wait_ge(S("K_staged"), n + 1)
                o = bank(6 + s)[0:LA, 0:LA * LA].rearrange("a (b d) -> a d b", d=LA)
                for d in range(LA):
                    last = nc.tensor.matmul(o[:, d, :], UV[:, s, d, 0:LA], UV[:, s, d, LA:2 * LA],
                                            start=True, stop=True)
                last.then_inc(S("K_full"), 1)
                for m in (2 * n + 4, 2 * n + 5):
                    if m < 16:
                        fill_v(m)

            def scores(h, s):
                t, c = s // 4, s % 4
                for u in range(2):
                    last = nc.tensor.matmul(bank(2 * (s % 2) + u), qst[:, h % 4, t * P:(t + 1) * P],
                                            kst[:, h // 2 % 2, c * 1024 + u * 512:c * 1024 + (u + 1) * 512],
                                            start=True, stop=True)
                last.then_inc(S("s_full"), 1)

            def scores_t(h, j):
                for u in range(2):
                    last = nc.tensor.matmul(bank(4 + j % 2)[:, u * T:(u + 1) * T],
                                            kst[:, h // 2 % 2, (2 * j + u) * P:(2 * j + u + 1) * P],
                                            qst[:, h % 4, :], start=True, stop=True)
                last.then_inc(S("st_full"), 1)

            def max_row(h):
                for t in range(TT):
                    last = nc.tensor.matmul(bank(7)[96:97, t * P:(t + 1) * P], mx[:, h % 2, t:t + 1], ident[:, :],
                                            start=True, stop=True)
                last.then_inc(S("mrow_full"), 1)

            def weigh(p, par, j):
                for u in range(2):
                    for part in (prob_hi, prob_lo):
                        last = nc.tensor.matmul(bank(6 + par)[0:2 * HD + 1, 0:T],
                                                vst[:, 2 * j + u, p * 2 + par, :],
                                                part[:, j % BUFS, u * T:(u + 1) * T],
                                                start=(j == 0 and u == 0 and part is prob_hi),
                                                stop=(j == SLOTS - 1 and u == 1 and part is prob_lo))
                last.then_inc(S("pv_done"), 1)

            def pair(p):
                for i in range(2 * SLOTS):
                    par, j = divmod(i, SLOTS)
                    h = 2 * p + par
                    g, s = (h + 1, S_NEXT[j]) if j in S_NEXT else (h + 2, S_AFTER[j]) if j in S_AFTER else (H, 0)
                    if g < H:
                        if g % 2 == 0 and s == 0:
                            pe.wait_ge(S("kst_in"), 96 * (g // 2 + 1))
                        if s == 0:
                            pe.wait_ge(S(f"q_in{g % 4}"), 64 * (g // 4 + 1))
                        pe.wait_ge(S("s_free"), 8 * g + s + 1)
                        scores(g, s)
                    if j == M_AT and h + 1 < H:
                        pe.wait_ge(S("m_ready"), h + 2)
                        pe.wait_ge(S("mrow_ready"), h + 1)
                        max_row(h + 1)
                    n = 2 * SLOTS * p + i + AHEAD
                    if n < SLOTS * H:
                        slot_t(n)
                    if j == 0:
                        pe.wait_ge(S("o_staged"), h + 1)
                    q, r = divmod(i, 4)
                    if r < 3:
                        pe.wait_ge(S("low_pool"), p * 24 + (3 * q + r + 1))
                    else:
                        pe.wait_ge(S("low_dve"), p * 8 + (q + 1))
                    weigh(p, par, j)

            def slot_t(n):
                h, j = divmod(n, SLOTS)
                if j == 0:
                    pe.wait_ge(S("m_in"), 16 * (h + 1))
                pe.wait_ge(S("exp_done"), n + 1)
                scores_t(h, j)

            for h in range(2):
                pe.wait_ge(S(f"q_in{h}"), 64)
            pe.wait_ge(S("kmask_in"), 16 * 4)
            pe.wait_ge(S("kst_in"), 192)
            pe.wait_ge(S("stacks_set"), 2)
            pe.wait_ge(S("q_lo_ready"), 2)
            pe.wait_ge(S("kv_low"), 4 + 32)
            for h, n in ((0, 8), (1, 5)):
                for s in range(n):
                    pe.wait_ge(S("s_free"), 8 * h + s + 1)
                    scores(h, s)
                if h == 0:
                    pe.wait_ge(S("m_ready"), 1)
                    pe.wait_ge(S("K_staged"), 17)
                    max_row(0)
            for n in range(AHEAD):
                slot_t(n)
            for p in range(PAIRS):
                pair(p)
            pe.wait_ge(S("self_in"), 16 * 5)
            pe.wait_ge(S("aT"), 1)
            for t in range(TT):
                for k in range(2):
                    last = nc.tensor.matmul(bank(t)[:, 0:D], zT[:, k, t * P:(t + 1) * P], wo[:, k, :],
                                            start=(k == 0), stop=(k == 1))
                last.then_inc(S("projected"), 1)

            def features(tag, b=6, src=z):
                to_features(pe, src, b, tag)
                pe.wait_ge(S("zT_kept"), ZT[tag])

            def project(lhs, w, n, cols, b, done, width=None):
                for t in range(TT):
                    for k in range(2):
                        last = nc.tensor.matmul(bank(b + t)[:, 0:n], lhs[:, k, t * P:(t + 1) * P], w[:, k, cols:cols + n],
                                                start=(k == 0), stop=(k == 1))
                    last.then_inc(S(done), 1)

            def to_tokens(src, b, tag, ready):
                pe.wait_ge(S(ready), 1)
                for t in range(TT):
                    for m in range(2):
                        last = nc.tensor.transpose(bank(b)[:, t * D + m * P:t * D + (m + 1) * P],
                                                   src[:, m, t * P:(t + 1) * P], ident[:, :])
                last.then_inc(S(tag), 1)

            features("ln1")
            pe.wait_ge(S("self_in"), 16 * 5)
            for t in range(TT):
                for c in range(2):
                    for k in range(2):
                        last = nc.tensor.matmul(bank(2 * t + c)[:, 0:384], zT[:, k, t * P:(t + 1) * P],
                                                wqkv[:, k, c * 384:(c + 1) * 384], start=(k == 0), stop=(k == 1))
            last.then_inc(S("qkv_full"), 1)
            pe.wait_ge(S("keys2_in"), 16 * 8)
            for c in range(CH):
                if c >= 2:
                    pe.wait_ge(S("k1_kept"), c - 1)
                for k in range(2):
                    r = P if k == 0 else C1
                    last = nc.tensor.matmul(bank(4 + c % 2), wk1[0:r, k, :], ctxT2[0:r, k, c * 512:(c + 1) * 512],
                                            start=(k == 0), stop=(k == 1))
                last.then_inc(S("k1_full"), 1)

            def spectrum(src, done):
                for f in range(4):
                    for k in range(2):
                        last = nc.tensor.matmul(bank(6 + f // 2)[:, f % 2 * D:(f % 2 + 1) * D],
                                                dft[:, k, f * P:(f + 1) * P], src[:, k, :],
                                                start=(k == 0), stop=(k == 1))
                last.then_inc(S(done), 1)

            pe.wait_ge(S("keys2_in"), 16 * 8)
            spectrum(Kt, "Kf_full")
            pe.wait_ge(S("wints"), 1)
            pe.wait_ge(S("k1_kept"), CH)
            pe.wait_ge(S("Kf_kept"), 2)
            for n in range(2):
                for k in range(2):
                    b = (4 + k if n == 0 else 6 + k)
                    for i, r in enumerate(FR):
                        last = nc.tensor.transpose(bank(b).bitcast(BF16)[:, i * P:i * P + r],
                                                   wint[0:r, n, i, k * P:(k + 1) * P], identb[0:r, 0:r])
                    last.then_inc(S("wT_full"), 1)
            for m in range(2):
                pe.wait_ge(S("wT_kept"), m + 1)
                for i, r in enumerate(FR):
                    last = nc.tensor.transpose(bank(4 + m).bitcast(BF16)[0:r, i * P:(i + 1) * P],
                                               wdint[:, m, i * P:i * P + r], identb[:, :])
                last.then_inc(S("wT_full"), 1)
            pe.wait_ge(S("wT_kept"), 6)
            features("attn_out")
            pe.wait_ge(S("self_in"), 16 * 5)
            project(zT, wout, D, 0, 0, "projected")

            features("ffn_q")
            for i, r in enumerate(FR):
                for n in range(2):
                    for k in range(2):
                        last = nc.tensor.matmul(bank(i)[0:r, n * T:(n + 1) * T], guT[:, n, k, i * P:i * P + r],
                                                xqT[:, k, :], start=(k == 0), stop=(k == 1))
                last.then_inc(S("gu_full"), 1)
            pe.wait_ge(S("hq_ready"), 1)
            for m in range(2):
                for i, r in enumerate(FR):
                    last = nc.tensor.matmul(bank(6)[:, m * T:(m + 1) * T], wdT[0:r, i, m * P:(m + 1) * P],
                                            hq[0:r, i, :], start=(i == 0), stop=(i == 5))
            last.then_inc(S("down_full"), 1)
            to_tokens(zT, 7, "ffn_y", "down_kept")

            features("ln3")
            pe.wait_ge(S("film_in"), 16 * 18)
            for k in range(2):
                last = nc.tensor.matmul(bank(5)[:, 0:T], wq1[:, k, :], zT[:, k, :], start=(k == 0), stop=(k == 1))
            last.then_inc(S("q1_full"), 1)
            pe.wait_ge(S("q1_kept"), 1)

            def weigh_context(t):
                for g in range(8):
                    n = 8 * t + g
                    pe.wait_ge(S("AM_ready"), t + 1)
                    if n >= 2:
                        pe.wait_ge(S("AMT_kept"), n - 1)
                    for u in range(4):
                        last = nc.tensor.transpose(bank(4 + g % 2)[:, u * P:(u + 1) * P],
                                                   AM[:, (4 * g + u) * P:(4 * g + u + 1) * P], ident[:, :])
                    last.then_inc(S("AMT_full"), 1)
                    if g > 0:
                        context_sum(t, g - 1)
                context_sum(t, 7)

            def context_sum(t, g):
                pe.wait_ge(S("AMT_kept"), 8 * t + g + 1)
                pe.wait_ge(S("ctxn_in"), 16)
                for u in range(4):
                    kt = 4 * g + u
                    for c, w in ((0, P), (1, C1)):
                        last = nc.tensor.matmul(bank(6 + c)[0:w, t * P:(t + 1) * P], ctxn[:, kt, c * P:c * P + w],
                                                AMT[:, g % 2, u, :], start=(kt == 0), stop=(kt == KT - 1))
                last.then_inc(S("zc_full"), 1)

            def masked_scores(n):
                t, h = divmod(n, 4)
                for c in range(CH):
                    m = CH * n + c
                    if m >= 4:
                        pe.wait_ge(S("A_copied"), m - 3)
                    nc.tensor.matmul(bank(c % 4), q1[32 * h:32 * h + 32, t * P:(t + 1) * P],
                                     k1T[32 * h:32 * h + 32, c * 512:(c + 1) * 512], start=True, stop=False)
                    last = nc.tensor.matmul(bank(c % 4), identb[32 * h:32 * h + 8, 32 * h + c:32 * h + c + 1].broadcast_to([8, P]), mask8b[h],
                                            start=False, stop=True)
                    last.then_inc(S("A_full"), 1)

            pe.wait_ge(S("mask8_ready"), 1)
            for n in range(2):
                masked_scores(n)
            for n in range(8):
                pe.wait_ge(S("counted"), n + 1)
                nc.tensor.matmul(bank(7)[96:97, 0:1], small[:, 112 + n % 2:113 + n % 2], small[:, 114:115],
                                 start=True, stop=True).then_inc(S("count_full"), 1)
                if n == 5:
                    weigh_context(0)
                if n + 2 < 8:
                    masked_scores(n + 2)
            weigh_context(1)
            pe.wait_ge(S("zc_ready"), 2)
            pe.wait_ge(S("film_in"), 16 * 18)
            for m in range(2):
                for k in range(2):
                    r = P if k == 0 else C1
                    last = nc.tensor.matmul(bank(0)[:, m * T:(m + 1) * T], wv1[0:r, k, m * P:(m + 1) * P], zc[0:r, k, :],
                                            start=(k == 0), stop=(k == 1))
            last.then_inc(S("cT_full"), 1)
            pe.wait_ge(S("cT_ready"), 1)
            project(cT, wfi, 2 * D, 0, 1, "film_in_full")
            project(cT, wfo, 2 * D, 0, 3, "film_out_full")
            pe.wait_ge(S("u_ready"), 1)
            spectrum(z, "U_full")
            pe.wait_ge(S("Y_ready"), 1)
            for t in range(TT):
                for f in range(4):
                    last = nc.tensor.matmul(bank(5)[:, t * D:(t + 1) * D], dftT[:, f, t * P:(t + 1) * P], Yf[:, f, :],
                                            start=(f == 0), stop=(f == 3))
            last.then_inc(S("y_full"), 1)
            features("ln4")
            pe.wait_ge(S("w12_in"), 32)
            for m in range(8):
                for k in range(2):
                    last = nc.tensor.matmul(bank(m // 2)[:, m % 2 * T:(m % 2 + 1) * T], w1[:, k, m * P:(m + 1) * P],
                                            zT[:, k, :], start=(k == 0), stop=(k == 1))
                if m % 2 == 1:
                    last.then_inc(S("h1_full"), 1)
            for m in range(8):
                if m % 2 == 0:
                    pe.wait_ge(S("Gh_ready"), m // 2 + 1)
                for t in range(TT):
                    last = nc.tensor.matmul(bank(4 + t)[:, 0:D], Gh[:, m, t * P:(t + 1) * P], w2[:, m, :],
                                            start=(m == 0), stop=(m == 7))
            last.then_inc(S("h2_full"), 1)

            features("ln5")
            pe.wait_ge(S("rest_in"), 16 * 6)
            for n, w in enumerate((wgg, wgc)):
                for m in range(2):
                    for k in range(2):
                        last = nc.tensor.matmul(bank(n)[:, m * T:(m + 1) * T], w[:, k, m * P:(m + 1) * P], zT[:, k, :],
                                                start=(k == 0), stop=(k == 1))
                last.then_inc(S("gru_full"), 1)
            to_tokens(cT, 2, "gru_y", "gru_done")

            features("ln6")
            pe.wait_ge(S("rest_in"), 16 * 6)
            for t in range(TT):
                for k in range(2):
                    last = nc.tensor.matmul(bank(7)[:, t * E:(t + 1) * E], zT[:, k, t * P:(t + 1) * P], router[:, k, :],
                                            start=(k == 0), stop=(k == 1))
            last.then_inc(S("logits"), 1)

            def expert_in(n):
                if n >= 2:
                    pe.wait_ge(S("unit_read"), n - 1)
                for g in range(2):
                    for k in range(2):
                        w = sgu[:, k, g, n * P:(n + 1) * P] if n < 4 else gup[:, n - 4, k, g * I:(g + 1) * I]
                        last = nc.tensor.matmul(bank(n % 2)[:, g * T:(g + 1) * T], w, zT[:, k, :],
                                                start=(k == 0), stop=(k == 1))
                if n >= 4:
                    e = n - 4
                    last = nc.tensor.matmul(bank(2 + n % 2)[:, 0:T], ident[0:E, e:e + 1].broadcast_to([E, P]), wT[:, :],
                                            start=True, stop=True)
                last.then_inc(S("unit_full"), 1)

            def expert_out(n):
                pe.wait_ge(S("unit_ready"), n + 1)
                w = sdn[:, n, :] if n < 4 else down[:, n - 4, :]
                for t in range(TT):
                    last = nc.tensor.matmul(bank(4 + t)[:, 0:D], ehw[:, n % 2, t * P:(t + 1) * P], w,
                                            start=(n == 0), stop=(n == E + 3))
                last.then_inc(S("unit_done"), 1)

            pe.wait_ge(S("shared_in"), 32)
            for n in range(E + 4):
                if n == 4:
                    pe.wait_ge(S("wtok"), 1)
                    for t in range(TT):
                        last = nc.tensor.transpose(bank(7)[0:E, t * P:(t + 1) * P], rt[:, 2, t, :], ident[:, :])
                    last.then_inc(S("wT_t"), 1)
                    pe.wait_ge(S("wT_ready"), 1)
                if n >= 4 and n % 8 == 4:
                    pe.wait_ge(S(f"experts_in{(n - 4) // 8}"), 32)
                expert_in(n)
                if n >= 1:
                    expert_out(n - 1)
            expert_out(E + 3)

        @block.scalar
        def _(act):
            act.wait_ge(S("eps_set"), 1)
            ln_sqrt(act, "ln0")
            act.wait_ge(S("s4_in"), 16 * 11)
            nc.scalar.activation(dtb[:, :], dtb[:, :], ACT.Exp).then_inc(S("dt_ready"), 1)
            for i in range(4):
                for u in range(4):
                    c, m = 2 * i + u // 2, u % 2
                    act.wait_ge(S("fill"), 4 * i + u + 1)
                    nc.scalar.copy(k_hi[:, m, c * 512:(c + 1) * 512], bank(u)).then_inc(S("kv_high"), 1)
                if i == 1:
                    act.wait_ge(S("step_ready"), 1)
                    nc.scalar.activation(sw[:, 2, :], sw[:, 0, :], ACT.Tanh, scale=0.5)
                    nc.scalar.activation(sw[:, 3, :], sw[:, 4, :], ACT.Sin, scale=0.5)
                    nc.scalar.activation(sw[:, 4, :], sw[:, 4, :], ACT.Sin).then_inc(S("step_funcs"), 1)
            keep_features(act, zT, 4, "ln0")
            for m in range(2):
                act.wait_ge(S("q_full"), 2)
                nc.scalar.copy(q_hi[:, m, :], bank(5)[:, m * T:(m + 1) * T]).then_inc(S("q_hi_ready"), 1)

            def waves(i, j, values=True):
                n = 4 * i + j
                for m in (2 * j, 2 * j + 1) if values else ():
                    act.wait_ge(S("fill"), i * 8 + m + 17)
                    nc.scalar.copy(vst[:, bass.ds(i * 16 + 2 * m, 2), :, 0:HD],
                                   bank(m % 4).rearrange("p (u h d) -> p u h d", u=2, d=HD)).then_inc(S("kv_high"), 1)
                act.wait_ge(S("mag_arg"), n + 1)
                nc.scalar.activation(mag[:, :, :], mag[:, :, :], ACT.Exp).then_inc(S("mag_ready"), 1)
                act.wait_ge(S("ang_ready"), n + 1)
                act.wait_ge(S("uv_ready"), n + 1)
                nc.scalar.activation(SV[:, :, 0:LA], yA[:, j % 2, :, 0:LA], ACT.Sin, bias=phs[:, 3:4], scale=-1.0)
                nc.scalar.activation(SV[:, :, LA:2 * LA], yA[:, j % 2, :, LA:2 * LA], ACT.Sin, bias=phs[:, 3:4], scale=phs[:, 0:1])
                nc.scalar.activation(T2[:, :, :], ang[:, j % 2, :, 0:LA], ACT.Sin, bias=phs[:, 4:5], scale=phs[:, 1:2])\
                    .then_inc(S("sin_ready"), 1)

            def stage(n, s=None):
                s = n % 2 if s is None else s
                act.wait_ge(S("K_full"), n + 3)
                act.wait_ge(S("K_out"), n * 16 + 16)
                nc.scalar.copy(Kstage[:, s, :], bank(6 + s)[0:LA, 0:LA * LA]).then_inc(S("K_staged"), 1)

            waves(0, 0)
            for j in range(1, 4):
                waves(0, j)
                stage(j - 1)
            for j in range(4):
                waves(1, j)
                stage(3 + j)
            with act.Fori(2, 4) as i:
                for j in range(4):
                    waves(i, j, False)
                    stage(i * 4 + (j - 1), (j - 1) % 2)
            stage(15)
            act.wait_ge(S("K_out"), 17 * 16)

            def keep_turned(act, t, g):
                act.wait_ge(S("AMT_full"), 8 * t + g + 1)
                if 8 * t + g >= 2:
                    act.wait_ge(S("zc_full"), 8 * t + g - 1)
                nc.scalar.copy(AMT[:, g % 2, :, :], bank(4 + g % 2)).then_inc(S("AMT_kept"), 1)

            with act.Fori(0, PAIRS) as p:
                for i in range(2 * SLOTS):
                    q, r = divmod(i, 4)
                    act.wait_ge(S("st_full"), p * 32 + i + 1)
                    act.wait_ge(S("pv_done"), p * 32 + (i + 1))
                    nc.scalar.activation(prob[:, i % BUFS, :], bank(4 + i % 2), ACT.Exp, scale=HD ** -0.5)\
                        .then_inc(S("exp_done"), 1)
                    if r < 3:
                        act.wait_ge(S("exp_done"), p * 32 + (i + 3))
                        nc.scalar.copy(prob_hi[:, i % BUFS, :], prob[:, i % BUFS, :]).then_inc(S("high_act"), 1)

            def copy(to, frm, waits, done):
                for name, v in waits:
                    act.wait_ge(S(name), v)
                nc.scalar.copy(to, frm).then_inc(S(done), 1)

            ln_sqrt(act, "ln1")
            keep_features(act, zT, 6, "ln1")
            for c in range(CH):
                copy(k1T[:, c * 512:(c + 1) * 512], bank(4 + c % 2), [("k1_full", c + 1)], "k1_kept")
            for n in range(2):
                copy(Kf[:, 2 * n:2 * n + 2, :], bank(6 + n), [("Kf_full", 1)], "Kf_kept")
            act.wait_ge(S("sc_ready"), 1)
            nc.scalar.activation(sc[:, :, :], sc[:, :, :], ACT.Exp, scale=HD ** -0.5).then_inc(S("sc_exp"), 1)
            for n in range(2):
                for k in range(2):
                    b = (4 + k if n == 0 else 6 + k)
                    copy(guT[:, n, k, :], bank(b).bitcast(BF16)[:, 0:F_], [("wT_full", 2 * n + k + 1)], "wT_kept")
            for m in range(2):
                act.wait_ge(S("wT_full"), 5 + m)
                nc.scalar.copy(wdT[:, 0:5, m * P:(m + 1) * P],
                               bank(4 + m).bitcast(BF16)[:, 0:5 * P].rearrange("p (i h) -> p i h", i=5))
                nc.scalar.copy(wdT[0:FR[5], 5, m * P:(m + 1) * P], bank(4 + m).bitcast(BF16)[0:FR[5], 5 * P:6 * P])\
                    .then_inc(S("wT_kept"), 1)
            keep_features(act, zT, 6, "attn_out")

            act.wait_ge(S("wffn_in"), 16 * 7)
            nc.scalar.activation(small[:, 32:34], clips[:, :], ACT.Exp, scale=-1.0).then_inc(S("clip_exp"), 1)
            ln_sqrt(act, "ln2")
            act.wait_ge(S("zT_full"), ZT["ffn_q"])
            nc.scalar.copy(xqT[:, :, :], bank(6)).then_inc(S("zT_kept"), 1)
            act.wait_ge(S("comb_ready"), 1)
            for i, r in enumerate(FR):
                act.wait_ge(S("gu_full"), i + 1)
                nc.scalar.activation(sg[0:r, i, :], bank(i)[0:r, 0:T], ACT.Silu, scale=small[0:r, 40 + i:41 + i])\
                    .then_inc(S("sg_ready"), 1)
            act.wait_ge(S("down_full"), 1)
            for m in range(2):
                last = nc.scalar.activation(zT[:, m, :], bank(6)[:, m * T:(m + 1) * T], ACT.Copy,
                                            scale=small[:, 56 + m:57 + m])
            last.then_inc(S("down_kept"), 1)

            ln_sqrt(act, "ln3")
            keep_features(act, zT, 6, "ln3")
            copy(q1[:, :], bank(5)[:, 0:T], [("q1_full", 1)], "q1_kept")

            def keep_scores(n):
                for c in range(CH):
                    act.wait_ge(S("A_full"), CH * n + c + 1)
                    if c == 0 and n >= 3:
                        act.wait_ge(S("top_weighed"), n - 2)
                    nc.scalar.activation(Asc[:, n % 3, c * 512:(c + 1) * 512], bank(c % 4), ACT.Copy, scale=32 ** -0.5)\
                        .then_inc(S("A_copied"), 1)

            act.wait_ge(S("x_new"), 6)
            keep_scores(0)
            keep_scores(1)
            for n in range(8):
                t, h = divmod(n, 4)
                act.wait_ge(S("top_found"), n + 1)
                nc.scalar.activation(EB[:, n % 2, :], Asc[:, n % 3, :], ACT.Exp, bias=small[:, 64 + n % 2:65 + n % 2])\
                    .then_inc(S("E_ready"), 1)
                if n + 2 < 8:
                    keep_scores(n + 2)
                act.wait_ge(S("r_ready"), n + 1)
                act.wait_ge(S("r_ready"), n + 1)
                if h == 0:
                    if t == 1:
                        for g in range(8):
                            keep_turned(act, 0, g)
                    nc.scalar.activation(AM[:, :], EB[:, n % 2, :], ACT.Copy, scale=small[:, 66 + n % 2:67 + n % 2])\
                        .then_inc(S("E_scaled"), 1)
                else:
                    nc.scalar.activation(EB[:, n % 2, :], EB[:, n % 2, :], ACT.Copy, scale=small[:, 66 + n % 2:67 + n % 2])\
                        .then_inc(S("E_scaled"), 1)
            for g in range(8):
                keep_turned(act, 1, g)
            act.wait_ge(S("zc_full"), 16)
            nc.scalar.copy(zc[:, 0, :], bank(6)[:, 0:T]).then_inc(S("zc_ready"), 1)
            nc.scalar.copy(zc[0:C1, 1, :], bank(7)[0:C1, 0:T]).then_inc(S("zc_ready"), 1)
            copy(cT[:, :, :], bank(0), [("cT_full", 1)], "cT_ready")
            ln_sqrt(act, "xin")
            ln_sqrt(act, "ln4")
            keep_features(act, zT, 6, "ln4")
            for m in range(8):
                act.wait_ge(S("h1_full"), m // 2 + 1)
                last = nc.scalar.activation(Gh[:, m, :], bank(m // 2)[:, m % 2 * T:(m % 2 + 1) * T], ACT.Gelu,
                                            bias=b1[:, m:m + 1])
                if m % 2 == 1:
                    last.then_inc(S("Gh_ready"), 1)
            ln_sqrt(act, "nout")

            ln_sqrt(act, "ln5")
            keep_features(act, zT, 6, "ln5")
            for n, (to, f) in enumerate(((gt, ACT.Sigmoid), (cd, ACT.Tanh))):
                act.wait_ge(S("gru_full"), n + 1)
                for m in range(2):
                    last = nc.scalar.activation(to[:, m, :], bank(n)[:, m * T:(m + 1) * T], f, bias=bgc[:, n, m:m + 1])
                last.then_inc(S("gru_act"), 1)

            ln_sqrt(act, "ln6")
            keep_features(act, zT, 6, "ln6")
            act.wait_ge(S("logits"), 1)
            nc.scalar.activation(rt[:, 0, :, :], bank(7)[:, 0:TT * E].rearrange("p (t e) -> p t e", t=TT), ACT.Sigmoid)\
                .then_inc(S("rscores"), 1)
            for n in range(E + 4):
                if n == 4:
                    copy(wT[:, :], bank(7)[0:E, 0:T], [("wT_t", 1)], "wT_ready")
                act.wait_ge(S("unit_full"), n + 1)
                if n >= 2:
                    act.wait_ge(S("unit_ready"), n - 1)
                nc.scalar.activation(esg[:, n % 2, :], bank(n % 2)[:, 0:T], ACT.Silu).then_inc(S("unit_silu"), 1)

        @block.gpsimd
        def _(pool):
            link = chain(pool, "pool_chain")
            nc.gpsimd.memset(eps[:, :], 1e-5).then_inc(S("eps_set"), 1)
            nc.gpsimd.memset(vst[:, :, :, HD:HD + 1].bitcast(F32), 1.0).then_inc(S("stacks_set"), 1)
            pool.wait_ge(S("stacks_set"), 1)
            nc.gpsimd.memset(qst[:, :, :].bitcast(F32), 0.0).then_inc(S("stacks_set"), 1)
            pool.wait_ge(S("stacks_set"), 2)
            pool.wait_ge(S("mku_in"), 16)
            link(nc.gpsimd.memset(maskb[:, 1:3, :], 1.0))
            link(nc.gpsimd.memset(maskb[:, 3:16, :], 0.0))
            link(nc.gpsimd.tensor_copy(maskb[:, 0, :], mku[:, :]))
            nc.gpsimd.tensor_scalar(maskb[:, 0, :], maskb[:, 0, :], -NEG, NEG, ALU.mult, ALU.add).then_inc(S("maskb_ready"), 1)
            bd = lambda v: v.unsqueeze(2).broadcast_to([P, LA, 2 * LA])
            facb = fac[:, :].unsqueeze(1).broadcast_to([P, LA, 2 * LA])
            bh = lambda v: v.unsqueeze(2).broadcast_to([P, LA, LA])
            pool.wait_ge(S("dC_ready"), 1)
            pool.wait_ge(S("mask_out"), 16)
            with pool.Fori(0, 8) as i:
                for s in range(2):
                    ds = bass.ds(i * 32 + s * LA, LA)
                    pool.wait_ge(S("uv_ready"), i * 2 + s + 1)
                    nc.gpsimd.tensor_tensor(mag[:, :, :], bd(sw[:, 0, ds]), facb, ALU.mult).then_inc(S("mag_arg"), 1)
                    pool.wait_ge(S("mag_ready"), i * 2 + s + 1)
                    pool.wait_ge(S("sin_ready"), i * 2 + s + 3)
                    nc.gpsimd.tensor_tensor(T2[:, :, :], T2[:, :, :], mag[:, :, 0:LA], ALU.mult).then_inc(S("t2_a"), 1)
                    pool.wait_ge(S("t2_a"), i * 2 + s + 1)
                    nc.gpsimd.tensor_tensor(T2[:, :, :], T2[:, :, :], bh(s4[:, 3, ds]), ALU.mult).then_inc(S("t2_b"), 1)
                    pool.wait_ge(S("t2_b"), i * 2 + s + 1)
                    pool.wait_ge(S("sv_mag"), i * 2 + s + 1)
                    pool.wait_ge(S("K_full"), i * 2 + s + 1)
                    nc.gpsimd.tensor_tensor(UV[:, s, :, 0:LA], SV[:, :, 0:LA], T2[:, :, :], ALU.subtract)\
                        .then_inc(S("uv_ready"), 1)
            pool.wait_ge(S("K_out"), 17 * 16)
            with pool.Fori(0, PAIRS) as p:
                for i in range(2 * SLOTS):
                    q, r = divmod(i, 4)
                    if r < 3:
                        pool.wait_ge(S("high_act"), p * 24 + (3 * q + r + 1))
                        b = i % BUFS
                        nc.gpsimd.tensor_tensor(prob_lo[:, b, :], prob[:, b, :], prob_hi[:, b, :].bitcast(F32),
                                                ALU.subtract).then_inc(S("low_pool"), 1)

            pool.wait_ge(S("aT"), 1)
            nc.gpsimd.memset(wraw[64:P, :, 5, :], 1.0).then_inc(S("wraw_set"), 1)
            for n in range(2):
                pool.wait_ge(S("absmax_part"), n + 1)
                nc.gpsimd.partition_all_reduce(small[:, 36 + n:37 + n], small[:, 34 + n:35 + n], P, RMAX)\
                    .then_inc(S("absmax_all"), 1)
                pool.wait_ge(S("absmax_all"), n + 1)
            for n in range(8):
                t, h = divmod(n, 4)
                pool.wait_ge(S("E_scaled"), n + 1)
                if h > 0:
                    nc.gpsimd.tensor_tensor(AM[:, :], AM[:, :], EB[:, n % 2, :], ALU.add).then_inc(S("E_added"), 1)
                    pool.wait_ge(S("E_added"), 3 * t + h)
                if h == 3:
                    nc.gpsimd.sem_inc(S("AM_ready"), 1)

        @block.vector
        def _(dve):
            link = chain(dve, "dve_chain")
            nc.vector.sem_inc(S("kv_low"), 4)
            nc.vector.sem_inc(S("s_free"), 2)
            nc.vector.sem_inc(S("exp_done"), 2)
            nc.vector.sem_inc(S("o_staged"), 2)
            nc.vector.sem_inc(S("pv_done"), BUFS)
            nc.vector.sem_inc(S("K_full"), 2)
            for name, n in (("uv_ready", 1), ("sin_ready", 2), ("K_staged", 1), ("K_out", 16), ("o_in", 48)):
                nc.vector.sem_inc(S(name), n)
            dve.wait_ge(S("x_in"), 16)
            ln_stats(dve, link, "ln0", x)
            tt = nc.vector.tensor_tensor
            stt = nc.vector.scalar_tensor_tensor
            ts = nc.vector.tensor_scalar
            Ar, Ai, Cr, Ci = (s4[:, n, :] for n in range(4))
            a, w1, th, s2, sn = (sw[:, n, :] for n in range(5))

            def reduce_angle(y, k):
                link(ts(k, y, 1 / (2 * pi), ROUND, ALU.mult, ALU.add))
                link(ts(k, k, ROUND, None, ALU.subtract))
                for part in TWO_PI:
                    link(stt(y, k, -part, y, ALU.mult, ALU.add))
                link(ts(y, y, SIN_MAX, -SIN_MAX, ALU.min, ALU.max))

            def low_keys(i):
                for u in range(4):
                    c, m = 2 * i + u // 2, u % 2
                    dve.wait_ge(S("kv_high"), 4 * i + u + 1)
                    nc.vector.tensor_tensor(k_lo[:, m, c * 512:(c + 1) * 512], bank(u),
                                            k_hi[:, m, c * 512:(c + 1) * 512].bitcast(F32),
                                            ALU.subtract).then_inc(S("kv_low"), 1)

            low_keys(0)
            dve.wait_ge(S("dt_ready"), 1)
            link(tt(sw[:, 0, :], dtb[:, :], Ar, ALU.mult))
            link(tt(dtb[:, :], dtb[:, :], Ai, ALU.mult))
            link(nc.vector.tensor_copy(sn, dtb[:, :]))
            reduce_angle(sn, w1)
            nc.vector.sem_inc(S("step_ready"), 1)
            low_keys(1)
            dve.wait_ge(S("step_funcs"), 1)
            link(ts(w1, th, -1.0, 1.0, ALU.mult, ALU.add))
            link(nc.vector.reciprocal(w1, w1))
            link(stt(th, th, 2.0, w1, ALU.mult, ALU.mult))
            link(tt(s2, s2, s2, ALU.mult))
            link(ts(s2, s2, 2.0, None, ALU.mult))
            link(stt(sn, th, 1.0, sn, ALU.add, ALU.mult))
            link(stt(w1, th, -1.0, s2, ALU.mult, ALU.mult))
            link(tt(w1, w1, th, ALU.add))
            link(tt(th, w1, s2, ALU.subtract))
            link(tt(w1, th, Ar, ALU.mult))
            link(tt(s2, sn, Ai, ALU.mult))
            link(tt(w1, w1, s2, ALU.add))
            low_keys(2)
            link(tt(s2, sn, Ar, ALU.mult))
            link(tt(th, th, Ai, ALU.mult))
            link(tt(s2, s2, th, ALU.subtract))
            link(tt(Ar, Ar, Ar, ALU.mult))
            link(tt(Ai, Ai, Ai, ALU.mult))
            link(tt(Ar, Ar, Ai, ALU.add))
            link(nc.vector.reciprocal(Ar, Ar))
            link(stt(w1, w1, 2.0, Ar, ALU.mult, ALU.mult))
            link(stt(s2, s2, 2.0, Ar, ALU.mult, ALU.mult))
            link(tt(Ar, Cr, w1, ALU.mult))
            link(tt(Ai, Ci, s2, ALU.mult))
            link(tt(th, Ar, Ai, ALU.subtract))
            link(tt(Ar, Cr, s2, ALU.mult))
            link(tt(Ai, Ci, w1, ALU.mult))
            link(tt(Ci, Ar, Ai, ALU.add))
            link(nc.vector.tensor_copy(Cr, th))
            nc.vector.sem_inc(S("dC_ready"), 1)
            low_keys(3)
            for m in range(2):
                dve.wait_ge(S("q_hi_ready"), 2)
                nc.vector.tensor_tensor(q_lo[:, m, :], bank(5)[:, m * T:(m + 1) * T], q_hi[:, m, :].bitcast(F32),
                                        ALU.subtract).then_inc(S("q_lo_ready"), 1)

            def low_values(i, m):
                dve.wait_ge(S("kv_high"), i * 8 + (16 + m + 1))
                v = bank(m % 4).rearrange("p (u h d) -> p u h d", u=2, d=HD)
                for u in range(2):
                    kt = i * 16 + (2 * m + u)
                    last = tt(vst[:, kt, :, HD + 1:2 * HD + 1], v[:, u], vst[:, kt, :, 0:HD].bitcast(F32), ALU.subtract)
                last.then_inc(S("kv_low"), 1)

            bd = lambda v: v.unsqueeze(2).broadcast_to([P, LA, 2 * LA])
            facb = fac[:, :].unsqueeze(1).broadcast_to([P, LA, 2 * LA])
            f = lambda v: v.rearrange("p d j -> p (d j)")

            def angles(i, j):
                ds = bass.ds(i * 64 + j * LA, LA)
                n, an, kn = i * 4 + j, ang[:, j % 2], kk[:, j % 2]
                step = [0]

                def then(ins):
                    step[0] += 1
                    ins.then_inc(S("angle_step"), 1)
                    dve.wait_ge(S("angle_step"), n * 8 + step[0])
                dve.wait_ge(S("sin_ready"), n + 1)
                then(tt(an, bd(dtb[:, ds]), facb, ALU.mult))
                then(ts(kn, an, 1 / (2 * pi), ROUND, ALU.mult, ALU.add))
                then(ts(kn, kn, ROUND, None, ALU.subtract))
                for part in TWO_PI:
                    then(stt(f(an), f(kn), -part, f(an), ALU.mult, ALU.add))
                then(ts(f(an), f(an), SIN_MAX, -SIN_MAX, ALU.min, ALU.max))
                then(stt(f(kn), f(an), phs[:, 0:1], f(an), ALU.mult, ALU.max))
                stt(an[:, :, 0:LA], an[:, :, 0:LA], phs[:, 1:2], an[:, :, 0:LA], ALU.mult, ALU.max)\
                    .then_inc(S("ang_ready"), 1)

            def products(i, j):
                ds = bass.ds(i * 64 + j * LA, LA)
                n, s = i * 4 + j, j % 2
                dve.wait_ge(S("mag_ready"), n + 1)
                dve.wait_ge(S("sin_ready"), n + 3)
                dve.wait_ge(S("K_full"), n + 1)
                tt(UV[:, s, :, LA:2 * LA], SV[:, :, LA:2 * LA], mag[:, :, LA:2 * LA], ALU.mult).then_inc(S("sv_1"), 1)
                tt(SV[:, :, 0:LA], SV[:, :, 0:LA], mag[:, :, 0:LA], ALU.mult).then_inc(S("sv_1"), 1)
                dve.wait_ge(S("sv_1"), n * 2 + 2)
                tt(SV[:, :, 0:LA], SV[:, :, 0:LA], bd(s4[:, 2, ds])[:, :, 0:LA], ALU.mult).then_inc(S("sv_mag"), 1)

            angles(0, 0)
            with dve.Fori(0, 2) as i:
                for j in range(4):
                    for m in (2 * j, 2 * j + 1):
                        low_values(i, m)
                    angles(i, j + 1)
                    products(i, j)
            for i in range(2, 4):
                for j in range(4):
                    if (i, j) != (3, 3):
                        angles(i, j + 1)
                    products(i, j)

            def take_max(s, n):
                nc.vector.reduce_max(mxp[:, n, s:s + 1], PS[:, 2 * (s % 2):2 * (s % 2) + 2, :].rearrange("p a b -> p (a b)"),
                                     AX).then_inc(S("s_free"), 1)

            def keep_max(n, h):
                dve.wait_ge(S("s_free"), 8 * h + 8 + 2)
                nc.vector.tensor_reduce(mx[:, n, :], mxp[:, n, :].rearrange("p (t s) -> p t s", t=TT), AX, ALU.max,
                                        negate=True).then_inc(S("m_ready"), 1)

            def split_row(h):
                dve.wait_ge(S("mrow_full"), h + 1)
                dve.wait_ge(S("m_in"), 16 * h)
                nc.vector.tensor_copy(mrow[96:97, 0, :], bank(7)[96:97, 0:T]).then_inc(S("mrow_high"), 1)
                dve.wait_ge(S("mrow_high"), h + 1)
                tt(mrow[96:97, 1, :], bank(7)[96:97, 0:T], mrow[96:97, 0, :].bitcast(F32), ALU.subtract)\
                    .then_inc(S("mrow_ready"), 1)

            def slots(p, first, after, last_pair=False):
                for i in range(first, after):
                    par, j = divmod(i, SLOTS)
                    if (i + DVE_EARLY) % 4 == 3:
                        k = i + DVE_EARLY
                        q = k // 4
                        dve.wait_ge(S("exp_done"), p * 32 + (k + 3))
                        b = k % BUFS
                        nc.vector.tensor_copy(prob_hi[:, b, :], prob[:, b, :]).then_inc(S("high_dve"), 1)
                        dve.wait_ge(S("high_dve"), p * 8 + (q + 1))
                        tt(prob_lo[:, b, :], prob[:, b, :], prob_hi[:, b, :].bitcast(F32), ALU.subtract)\
                            .then_inc(S("low_dve"), 1)
                    if j in S_NEXT and not (last_pair and par == 1):
                        s = S_NEXT[j]
                        dve.wait_ge(S("s_full"), p * 16 + (8 * (par + 1) + s + 1))
                        take_max(s, (par + 1) % 2)
                        if s == 7:
                            keep_max((par + 1) % 2, p * 2 + (par + 1))
                    if j in S_AFTER and not last_pair:
                        s = S_AFTER[j]
                        dve.wait_ge(S("s_full"), p * 16 + (8 * (par + 2) + s + 1))
                        take_max(s, par)
                    if j == M_AT + 1 and not (last_pair and par == 1):
                        split_row(p * 2 + (par + 1))
                    if i == SLOTS + LATE - 1:
                        keep_head(p * 2, 0)

            def keep_head(h, k):
                dve.wait_ge(S("pv_done"), h * SLOTS + (SLOTS + BUFS))
                dve.wait_ge(S("o_in"), h * 48 + 48)
                nc.vector.tensor_copy(ostage[:, k, :], bank(6 + k)[0:2 * HD + 1, 0:T]).then_inc(S("o_staged"), 1)

            dve.wait_ge(S("K_out"), 17 * 16)
            for h, n in ((0, 8), (1, 5)):
                for s in range(n):
                    dve.wait_ge(S("s_full"), 8 * h + s + 1)
                    take_max(s, h)
                if h == 0:
                    keep_max(0, 0)
                    split_row(0)
            LATE = 3
            slots(0, 0, LATE)
            with dve.Fori(0, PAIRS - 1) as p:
                slots(p, LATE, 2 * SLOTS)
                slots(p + 1, 0, LATE)
                keep_head(p * 2 + 1, 1)
            slots(PAIRS - 1, LATE, 2 * SLOTS, True)
            keep_head(H - 1, 1)
            dve.wait_ge(S("o_in"), 48 * H + 48)
            f = lambda v: v[:, :, :].rearrange("p m t -> p (m t)")
            link(tt(f(oh), f(oh), f(ol), ALU.add))
            link(nc.vector.reciprocal(f(osum), f(osum)))
            tt(f(zT), f(oh), f(osum), ALU.mult).then_inc(S("aT"), 1)
            dve.wait_ge(S("x_in"), 32)
            for t in range(TT):
                dve.wait_ge(S("projected"), t + 1)
                tt(x[:, t, :], x[:, t, :], bank(t)[:, 0:D], ALU.add).then_inc(S("x_new"), 1)
            dve.wait_ge(S("x_new"), 2)

            def add_tokens(b, full, done):
                dve.wait_ge(S(full), 1)
                v = bank(b).rearrange("p (t d) -> p t d", t=TT)
                link(tt(x[:, :, :], x[:, :, :], v, ALU.add))
                nc.vector.sem_inc(S(done), 2)

            ln_stats(dve, link, "ln1", x)
            dve.wait_ge(S("qkv_full"), 1)
            dve.wait_ge(S("self_in"), 16 * 5)
            for t in range(TT):
                for c in range(2):
                    last = tt(qkv[:, t, c * 384:(c + 1) * 384], bank(2 * t + c)[:, 0:384], bqkv[:, c * 384:(c + 1) * 384], ALU.add)
            link(last)
            qkvh = [qkv[:, t, :].rearrange("p (h c) -> p h c", c=3 * HD) for t in range(TT)]
            for n in range(4):
                t, half = divmod(n, 2)
                hs = slice(8 * half, 8 * half + 8)
                q4 = qkvh[t][:, hs, 0:HD].unsqueeze(2).broadcast_to([P, 8, H, HD])
                k4 = qkvh[t][:, :, HD:2 * HD].unsqueeze(1).broadcast_to([P, 8, H, HD])
                pr = prod[:, n % 2, :].rearrange("p (h g d) -> p h g d", h=8, g=H)
                link(tt(pr, q4, k4, ALU.mult))
                link(nc.vector.tensor_reduce(sc[:, t, half * 128:half * 128 + 128],
                                             prod[:, n % 2, :].rearrange("p (a d) -> p a d", d=HD), AX, ALU.add))
            s3 = sc[:, :, :].rearrange("p t (h g) -> p (t h) g", g=H)
            st_ = small[:, 96:128]
            bg = st_.unsqueeze(2).broadcast_to([P, 2 * H, H])
            link(nc.vector.tensor_reduce(st_, s3, AX, ALU.max))
            tt(s3, s3, bg, ALU.subtract).then_inc(S("sc_ready"), 1)
            absmax = lambda o, i: nc.vector.tensor_reduce(o, i, AX, ALU.max, apply_absolute_value=True)
            dve.wait_ge(S("wffn_in"), 16 * 7)
            dve.wait_ge(S("wraw_set"), 1)
            nc.vector.tensor_copy(identb[:, :], ident[:, :])
            absmax(small[:, 0:6], wraw[:, 0])
            absmax(small[:, 6:12], wraw[:, 1])
            link(absmax(small[:, 12:14], wdraw[:, :, :]))
            link(ts(small[:, 0:14], small[:, 0:14], 1 / QMAX, None, ALU.mult))
            link(nc.vector.reciprocal(small[:, 16:30], small[:, 0:14]))
            rows_of = [(w[:, i, :], 6 * n + i) for n, w in ((0, wraw[:, 0]), (1, wraw[:, 1])) for i in range(6)]
            rows_of += [(wdraw[:, m, :], 12 + m) for m in range(2)]
            for w, a in rows_of:
                last = ts(w, w, small[:, 16 + a:17 + a], QMAX, ALU.mult, ALU.min)
            link(last)
            flat_w = wraw[:, :, :, :].rearrange("p n i k -> p (n i k)")
            ts(flat_w, flat_w, -QMAX - 1, ROUND, ALU.max, ALU.add)
            link(ts(wdraw[:, :, :], wdraw[:, :, :], -QMAX - 1, ROUND, ALU.max, ALU.add))
            ts(wint[:, :, :, :].rearrange("p n i k -> p (n i k)"), flat_w, ROUND, None, ALU.subtract)
            ts(wdint[:, :, :], wdraw[:, :, :], ROUND, None, ALU.subtract).then_inc(S("wints"), 1)
            dve.wait_ge(S("sc_exp"), 1)
            link(nc.vector.tensor_reduce(st_, s3, AX, ALU.add))
            link(nc.vector.reciprocal(st_, st_))
            link(tt(s3, s3, bg, ALU.mult))
            for n in range(4):
                t, half = divmod(n, 2)
                a4 = sc[:, t, half * 128:half * 128 + 128].rearrange("p (h g) -> p h g", g=H).unsqueeze(2)\
                    .broadcast_to([P, 8, HD, H])
                v4 = qkvh[t][:, :, 2 * HD:3 * HD].rearrange("p g d -> p d g").unsqueeze(1).broadcast_to([P, 8, HD, H])
                pr = prod[:, n % 2, :].rearrange("p (h d g) -> p h d g", h=8, d=HD)
                link(tt(pr, a4, v4, ALU.mult))
                link(nc.vector.tensor_reduce(z[:, t, half * 128:half * 128 + 128],
                                             prod[:, n % 2, :].rearrange("p (a g) -> p a g", g=H), AX, ALU.add))
            nc.vector.sem_inc(S("z_ready"), 1)
            dve.wait_ge(S("self_in"), 16 * 5)
            link(tt(x[:, :, :], x[:, :, :], bout[:, :].unsqueeze(1).broadcast_to([P, TT, D]), ALU.add))
            for t in range(TT):
                dve.wait_ge(S("projected"), TT + t + 1)
                tt(x[:, t, :], x[:, t, :], bank(t)[:, 0:D], ALU.add).then_inc(S("x_new"), 1)
            dve.wait_ge(S("x_new"), 4)

            dve.wait_ge(S("clip_exp"), 1)
            link(ts(small[:, 32:34], small[:, 32:34], 1.0, None, ALU.add))
            link(nc.vector.reciprocal(small[:, 32:34], small[:, 32:34]))
            link(ts(small[:, 32:34], small[:, 32:34], 1 / QMAX, None, ALU.mult))
            ln_stats(dve, link, "ln2", x)
            absmax(small[:, 34:35], z[:, :, :].rearrange("p t d -> p (t d)")).then_inc(S("absmax_part"), 1)
            dve.wait_ge(S("absmax_all"), 1)
            link(tt(small[:, 38:39], small[:, 36:37], small[:, 32:33], ALU.mult))
            link(nc.vector.reciprocal(small[:, 54:55], small[:, 38:39]))

            def quantise(to, v, inv, done):
                link(ts(v, v, inv, QMAX, ALU.mult, ALU.min))
                link(ts(v, v, -QMAX - 1, ROUND, ALU.max, ALU.add))
                ts(to, v, ROUND, None, ALU.subtract).then_inc(S(done), 1)

            quantise(z[:, :, :], z[:, :, :], small[:, 54:55], "z_ready")
            link(ts(small[:, 40:52], small[:, 0:12], small[:, 38:39], None, ALU.mult))
            nc.vector.sem_inc(S("comb_ready"), 1)
            link(nc.vector.memset(hf[64:P, 5, :], 0.0))
            for i, r in enumerate(FR):
                dve.wait_ge(S("sg_ready"), i + 1)
                stt(hf[0:r, i, :], bank(i)[0:r, T:2 * T], small[0:r, 46 + i:47 + i], sg[0:r, i, :], ALU.mult, ALU.mult)\
                    .then_inc(S("hf_ready"), 1)
            dve.wait_ge(S("hf_ready"), 6)
            absmax(small[:, 35:36], hf[:, :, :].rearrange("p i t -> p (i t)")).then_inc(S("absmax_part"), 1)
            dve.wait_ge(S("absmax_all"), 2)
            link(tt(small[:, 39:40], small[:, 37:38], small[:, 33:34], ALU.mult))
            link(nc.vector.reciprocal(small[:, 55:56], small[:, 39:40]))
            link(ts(small[:, 56:58], small[:, 12:14], small[:, 39:40], None, ALU.mult))
            quantise(hq[:, :, :], hf[:, :, :], small[:, 55:56], "hq_ready")
            add_tokens(7, "ffn_y", "x_new")
            nc.vector.sem_inc(S("hq_used"), 1)

            ln_stats(dve, link, "ln3", x)
            link(nc.vector.tensor_copy(xt[:, :, :], z[:, :, :]))
            dve.wait_ge(S("film_in"), 16 * 18)
            link(nc.vector.tensor_copy(tmask[:, :], tmask_u[:, :]))
            link(nc.vector.memset(small[:, 104:112], 1.0))
            link(nc.vector.memset(small[:, 111:112], 2.0 * TOP))
            link(nc.vector.memset(small[:, 114:115], 1.0))
            dve.wait_ge(S("mask8_in"), 4 * 16)
            for h in range(4):
                last = nc.vector.tensor_copy(mask8b[h], mask8[h])
            last.then_inc(S("mask8_ready"), 1)
            in_full = chain(dve, "in_full_chain")
            IN_FULL = 10

            def find(n):
                a, k8 = Asc[:, n % 3, :], m8[:, n % 2, :]
                dve.wait_ge(S("A_copied"), CH * (n + 1))
                for c in range(M // PART):
                    last = nc.vector.max(cand[:, 8 * c:8 * c + 8], a[:, PART * c:PART * (c + 1)])
                link(last)
                for rnd in range(TOP // 8):
                    src, top = cand if rnd == 0 else cand_left, k8[:, 8 * rnd:8 * rnd + 8]
                    link(nc.vector.max(top, src))
                    if rnd < TOP // 8 - 1:
                        link(nc.vector.match_replace(cand_left, top, src, TAKEN))
                parts = lambda v: v.rearrange("p (c k) -> p c k", k=8)
                stt(parts(cand_left), parts(cand), k8[:, TOP - 1:TOP],
                    small[:, 104:112].unsqueeze(1).broadcast_to([P, M // PART, 8]), ALU.is_ge, ALU.mult,
                    accum_out=small[:, 112 + n % 2:113 + n % 2]).then_inc(S("counted"), 1)
                dve.wait_ge(S("counted"), n + 1)

            def search_in_full(n):
                a, b, k8 = Asc[:, n % 3, :], EB[:, n % 2, :], m8[:, n % 2, :]
                for rnd in range(TOP // 8):
                    src, top = a if rnd == 0 else b, k8[:, 8 * rnd:8 * rnd + 8]
                    in_full(nc.vector.max(top, src))
                    in_full(nc.vector.match_replace(b, top, src, TAKEN))
                in_full(ts(b, b, 0.99 * TAKEN, LOW, ALU.is_ge, ALU.mult))
                in_full(tt(a, a, b, ALU.add))

            def settle(n):
                if n >= 2:
                    dve.wait_ge(S("E_scaled"), n - 1)
                    dve.wait_ge(S("E_added"), (n - 2) // 4 * 3 + (n - 2) % 4)
                dve.wait_ge(S("count_full"), n + 1)
                link(nc.vector.tensor_copy(small[96:97, 116:117], bank(7)[96:97, 0:1]))
                total = nc.values_load(small[96:97, 116:117].bitcast(mybir.dt.int32), engines=(mybir.EngineType.DVE,))
                with dve.If(total != ALL_FOUND):
                    search_in_full(n)
                with dve.Else():
                    nc.vector.sem_inc(S("in_full_chain"), IN_FULL)
                ts(small[:, 64 + n % 2:65 + n % 2], m8[:, n % 2, 0:1], -1.0, None, ALU.mult).then_inc(S("top_found"), 1)

            def weigh_top(n):
                t, s = n // 4, n % 2
                dve.wait_ge(S("E_ready"), n + 1)
                link(stt(EB[:, s, :], Asc[:, n % 3, :], m8[:, s, TOP - 1:TOP], EB[:, s, :], ALU.is_ge, ALU.mult,
                         accum_out=small[:, 68 + s:69 + s]))
                nc.vector.sem_inc(S("top_weighed"), 1)
                link(nc.vector.reciprocal(small[:, 68 + s:69 + s], small[:, 68 + s:69 + s]))
                ts(small[:, 66 + s:67 + s], small[:, 68 + s:69 + s], 0.25, tmask[:, t:t + 1], ALU.mult, ALU.mult)\
                    .then_inc(S("r_ready"), 1)

            for n in range(8):
                find(n)
                if n >= 1:
                    weigh_top(n - 1)
                settle(n)
            weigh_top(7)

            dve.wait_ge(S("film_in"), 16 * 18)
            ln_stats(dve, link, "xin", xt, 0)
            both = lambda v: v.unsqueeze(1).broadcast_to([P, TT, v.shape[-1]])

            def modulate(v, b, bias, full):
                fm = Gh[:, 0:4, :].rearrange("p (t a) d -> p t (a d)", t=TT)
                for t in range(TT):
                    dve.wait_ge(S(full), t + 1)
                    last = tt(fm[:, t, :], bank(b + t), bias, ALU.add)
                link(last)
                link(ts(fm, fm, gate[:, 0:1], None, ALU.mult))
                link(stt(fm[:, :, 0:D], fm[:, :, 0:D], 1.0, v, ALU.add, ALU.mult))
                link(tt(v, fm[:, :, 0:D], fm[:, :, D:2 * D], ALU.add))

            dve.wait_ge(S("zc_ready"), 2)
            modulate(z[:, :, :], 1, bfi[:, :], "film_in_full")
            nc.vector.sem_inc(S("u_ready"), 1)
            link(tt(y[:, :, :], z[:, :, :], both(dskip[:, :]), ALU.mult))
            dve.wait_ge(S("U_full"), 1)
            re, im = bank(6), bank(7)
            kre, kim = (Kf[:, 2 * n:2 * n + 2, :].rearrange("p a d -> p (a d)") for n in range(2))
            yre, yim = (Yf[:, 2 * n:2 * n + 2, :].rearrange("p a d -> p (a d)") for n in range(2))
            tmp = Gh[:, 0:2, :].rearrange("p a d -> p (a d)")
            link(tt(yre, re, kre, ALU.mult))
            link(tt(tmp, im, kim, ALU.mult))
            link(tt(yre, yre, tmp, ALU.subtract))
            link(tt(yim, re, kim, ALU.mult))
            link(tt(tmp, im, kre, ALU.mult))
            tt(yim, yim, tmp, ALU.add).then_inc(S("Y_ready"), 1)
            dve.wait_ge(S("y_full"), 1)
            link(tt(y[:, :, :], y[:, :, :], bank(5).rearrange("p (t d) -> p t d", t=TT), ALU.add))
            modulate(y[:, :, :], 3, bfo[:, :], "film_out_full")
            link(tt(xt[:, :, :], xt[:, :, :], y[:, :, :], ALU.add))
            ln_stats(dve, link, "ln4", xt, 2)
            link(tt(xt[:, :, :], xt[:, :, :], both(b2[:, :]), ALU.add))
            dve.wait_ge(S("h2_full"), 1)
            for t in range(TT):
                last = tt(xt[:, t, :], xt[:, t, :], bank(4 + t)[:, 0:D], ALU.add)
            link(last)
            ln_stats(dve, link, "nout", xt, 4)
            link(tt(x[:, :, :], x[:, :, :], z[:, :, :], ALU.add))
            nc.vector.sem_inc(S("x_new"), 2)

            ln_stats(dve, link, "ln5", x)
            dve.wait_ge(S("gru_act"), 2)
            for m in range(2):
                last = nc.vector.tensor_tensor_scan(cT[:, m, :], gt[:, m, :], cd[:, m, :], 0.0, ALU.mult, ALU.add)
            last.then_inc(S("gru_done"), 1)
            add_tokens(2, "gru_y", "x_new")

            ln_stats(dve, link, "ln6", x)
            dve.wait_ge(S("rest_in"), 16 * 6)
            dve.wait_ge(S("rscores"), 1)
            link(tt(rt[:, 1, :, :], rt[:, 0, :, :], both(rbias[:, :]), ALU.add))
            for t in range(TT):
                k8 = small[:, 72 + 8 * t:80 + 8 * t]
                link(nc.vector.max(k8, rt[:, 1, t, :]))
                link(nc.vector.match_replace(rt[:, 2, t, :], k8, rt[:, 1, t, :], -3e38))
            link(tt(rt[:, 2, :, :], rt[:, 2, :, :], rt[:, 1, :, :], ALU.not_equal))
            link(tt(rt[:, 2, :, :], rt[:, 2, :, :], rt[:, 0, :, :], ALU.mult))
            link(nc.vector.tensor_reduce(small[:, 88:90], rt[:, 2, :, :], AX, ALU.add))
            link(ts(small[:, 88:90], small[:, 88:90], 1e-20, None, ALU.add))
            link(nc.vector.reciprocal(small[:, 88:90], small[:, 88:90]))
            for t in range(TT):
                last = ts(rt[:, 2, t, :], rt[:, 2, t, :], small[:, 88 + t:89 + t], 2.5, ALU.mult, ALU.mult)
            link(last)
            nc.vector.sem_inc(S("wtok"), 1)
            for n in range(E + 4):
                b = n % 2
                dve.wait_ge(S("unit_silu"), n + 1)
                if n >= 2:
                    dve.wait_ge(S("unit_done"), n - 1)
                if n < 4:
                    tt(ehw[:, b, :], bank(b)[:, T:2 * T], esg[:, b, :], ALU.mult).then_inc(S("unit_ready"), 1)
                    nc.vector.sem_inc(S("unit_read"), 1)
                    continue
                link(ts(euc[:, b, :], bank(b)[:, T:2 * T], 7.0, -7.0, ALU.min, ALU.max))
                link(stt(euc[:, b, :], esg[:, b, :], SILU7, euc[:, b, :], ALU.min, ALU.mult))
                tt(ehw[:, b, :], euc[:, b, :], bank(2 + b)[:, 0:T], ALU.mult).then_inc(S("unit_ready"), 1)
                dve.wait_ge(S("unit_ready"), n + 1)
                nc.vector.sem_inc(S("unit_read"), 1)
            dve.wait_ge(S("unit_done"), E + 4)
            for t in range(TT):
                tt(x[:, t, :], x[:, t, :], bank(4 + t)[:, 0:D], ALU.add).then_inc(S("x_new"), 1)


def laid_out(inputs):
    import numpy as np

    i = {name: np.asarray(a) for name, a in inputs.items()}
    turned = lambda a: np.ascontiguousarray(a.T)
    flags = lambda a: np.ascontiguousarray(a).view(np.uint8)
    a = {name: i[name] for name in (
        "L0_xattn_Wq", "L0_xattn_Wk", "L0_xattn_Wv", "L0_xattn_Wo", "L0_attn_W_qkv", "L0_attn_b_qkv", "L0_attn_W_out",
        "L0_attn_b_out", "L0_ffn_clip_x", "L0_ffn_clip_down", "L0_ffn_w_gate", "L0_ffn_w_up", "L0_ffn_w_down",
        "L1_xattn_Wq", "L1_xattn_Wk", "L1_xattn_Wv", "L1_xattn_W_film_in", "L1_xattn_b_film_in", "L1_xattn_W_film_out",
        "L1_xattn_b_film_out", "L1_xattn_g_norm_in", "L1_xattn_b_norm_in", "L1_xattn_g_norm_out", "L1_xattn_b_norm_out",
        "L1_xattn_g_ffn", "L1_xattn_b_ffn", "L1_xattn_W1", "L1_xattn_W2", "L1_xattn_b2", "L1_xattn_log_dt",
        "L1_xattn_D_skip", "L1_ffn_e_score_correction_bias")}
    a["L1_xattn_mod_gate"] = i["L1_xattn_mod_gate"].reshape(1)
    a["x"] = i["x"][0]
    a["ctx"] = i["ctx_768"][0]
    a["ctxT"] = turned(i["ctx_768"][0])
    a["ctx_mask"] = flags(i["mask_BxS2_bf1"][0])
    a["text_mask"] = turned(flags(i["mask_BxS_bf1"][0]).reshape(TT, P))
    for name in ("A_re", "A_im", "C_re", "C_im"):
        a[name + "T"] = turned(i["L1_xattn_" + name])
    a["b1T"] = turned(i["L1_xattn_b1"].reshape(8, P))
    for name in ("g", "c"):
        a[f"W{name}T"] = turned(i["L1_attn_W" + name])
        a[f"b{name}T"] = turned(i["L1_attn_b" + name].reshape(2, P))
    a["routerT"] = turned(i["L1_ffn_router_weight"])
    a["gupT"] = np.ascontiguousarray(i["L1_ffn_gate_up_proj"].reshape(E, 2 * I, 2, P).transpose(3, 0, 2, 1))
    a["downT"] = np.ascontiguousarray(i["L1_ffn_down_proj"].transpose(2, 0, 1))
    both = np.stack([i["L1_ffn_shared_gate"], i["L1_ffn_shared_up"]])
    a["sguT"] = np.ascontiguousarray(both.reshape(2, 512, 2, P).transpose(3, 2, 0, 1).reshape(P, -1))
    a["sdnT"] = np.ascontiguousarray(i["L1_ffn_shared_down"].reshape(D, 4, P).transpose(2, 1, 0).reshape(P, -1))

    a["ident"] = np.eye(P, dtype=np.float32)
    j = np.arange(LA, dtype=np.float32)
    a["lfac"] = np.tile(np.concatenate([LA * j, j]), (P, 1))
    phase = np.zeros((P, 8), np.float32)
    phase[:NS, 0], phase[NS:, 0] = -1, 1
    phase[:NS, 1], phase[NS:, 1] = 1, -1
    phase[:NS, 3] = phase[NS:, 4] = np.pi / 2
    a["phase"] = phase
    angle = np.outer(np.arange(T), (np.arange(T) + 0.5) * (np.pi / T))
    table = np.concatenate([np.cos(angle), -np.sin(angle)], 1)
    a["dft"] = table.astype(np.float32)
    a["dftT"] = turned((table / T).astype(np.float32))
    return a


def kernel(**inputs):
    import numpy as np
    import concourse.bacc as bacc
    from concourse import mybir
    from concourse.bass_utils import run_bass_kernel_spmd

    nc = bacc.Bacc("TRN2", target_bir_lowering=False, num_devices=1)
    arrays, A = {}, {}
    for name, a in laid_out(inputs).items():
        a = np.ascontiguousarray(a)
        arrays[f"in_{name}_dram"] = a
        A[name] = nc.dram_tensor(f"in_{name}_dram", a.shape, mybir.dt.from_np(a.dtype), kind="ExternalInput").ap()
    out = nc.dram_tensor("out_0_dram", (1, T, D), F32, kind="ExternalOutput").ap()
    perceiver_kernel(nc, A, out[0])
    r = run_bass_kernel_spmd(nc, [arrays], core_ids=[0])
    return r.results[0]["out_0_dram"]
```

```python
from contextlib import ExitStack
from math import exp, pi

import numpy as np

import concourse.bass as bass
from concourse import mybir
from concourse.alu_op_type import AluOpType as ALU

F32 = mybir.dt.float32
F32R = mybir.dt.float32r
BF16 = mybir.dt.bfloat16
U8 = mybir.dt.uint8
ACT = mybir.ActivationFunctionType
AX = mybir.AxisListType.X
RMAX = bass.bass_isa.ReduceOp.max

P = 128
T = 256
TT = T // P
D = 256
M = 4096
CD = 192
C1 = CD - P
KT = M // P
H = 16
HD = D // H
PAIRS = H // 2
BUFS = 8
SLOTS = 16
CH = M // 512
NEG = -2.0 ** 127
ROUND = 1.5 * 2.0 ** 23
NS = 64
LA = 16
E = 32
F_ = 704
FR = [min(P, F_ - i * P) for i in range(6)]
TAKEN = -3e38
LOW = -1e38
TOP = 32
PART = 64
ALL_FOUND = int(np.float32(TOP * P).view(np.int32))
SILU7 = 7.0 / (1.0 + exp(-7.0))
QMAX = 127.0
I = 128
SIN_MAX = 3.1415925
TWO_PI = (6.28125, 2 * pi - 6.28125)


def perceiver_kernel(nc, A, out):
    ctx = ExitStack()
    with ctx:
        sems = {}

        def S(name):
            if name not in sems:
                sems[name] = ctx.enter_context(nc.semaphore(name))
            return sems[name]

        def sb(name, shape, dt=F32, scope=None):
            return (scope or ctx).enter_context(nc.sbuf_tensor(name, shape, dt))

        def chain(eng, name):
            n = [0]

            def link(ins):
                n[0] += 1
                ins.then_inc(S(name), 1)
                eng.wait_ge(S(name), n[0])
                return ins
            return link

        PS = ctx.enter_context(nc.psum_tensor("PS", [P, 8, 512], F32))

        x = sb("x", [P, TT, D])
        z = sb("z", [P, TT, D])
        zT = sb("zT", [P, 2, T])
        ident = sb("ident", [P, P])
        stats = sb("stats", [P, TT, 6])
        mv = sb("mv", [P, TT, 2])
        sd = sb("sd", [P, TT])
        rs = sb("rs", [P, TT])
        eps = sb("eps", [P, 1])
        primer = sb("primer", [P, 1])
        mxp = sb("mxp", [P, 2, 8])
        mx = sb("mx", [P, 2, TT])
        rows_scratch = nc.dram_tensor("rows_scratch", [16, M], F32).ap()
        q_scratch = nc.dram_tensor("q_scratch", [2, P, 2, T], F32).ap()
        K_scratch = nc.dram_tensor("K_scratch", [LA, LA, D], F32).ap()

        ph1 = ExitStack()
        qst = sb("qst", [P, 4, T], F32R, ph1)
        k_hi = sb("k_hi", [P, 2, M], F32R, ph1)
        k_lo = sb("k_lo", [P, 2, M], F32R, ph1)
        vst = sb("vst", [P, KT, H, 2 * HD + 1], F32R, ph1)
        sub = ExitStack()
        ctxT = sb("ctxT", [P, 2, M], F32, sub)
        sub.close()
        kst = sb("kst", [P, 2, M], F32R, ph1)
        prep = ExitStack()
        q_hi = sb("q_hi", [P, 2, T], F32R, prep)
        q_lo = sb("q_lo", [P, 2, T], F32R, prep)
        wv = sb("wv", [P, 2, D], F32, prep)
        s4 = sb("s4", [P, 4, D], F32, prep)
        dtb = sb("dtb", [P, D], F32, prep)
        sw = sb("sw", [P, 5, D], F32, prep)
        fac = sb("fac", [P, 2 * LA], F32, prep)
        phs = sb("phs", [P, 8], F32, prep)
        mku = sb("mku", [P, 32], U8, prep)
        kk = sb("kk", [P, 2, LA, 2 * LA], F32, prep)
        phases_of = [v[:, :, :].rearrange("p t (d j) -> p (t d) j", j=2 * LA) for v in (z, zT)]
        yA = kk
        mag = sb("mag", [P, 2, LA, 2 * LA], F32, prep)
        maskb = mag[:, 0]
        SV = sb("SV", [P, LA, 2 * LA], F32, prep)
        T2 = sb("T2", [P, LA, LA], F32, prep)
        first = ExitStack()
        wq = sb("wq", [P, 2, D], F32, first)
        wk = sb("wk", [P, 2, D], F32, first)
        first.close()
        UV = sb("UV", [P, 2, LA, 2 * LA], F32, prep)
        Kstage = sw[0:LA, 3:5, :]
        prep.close()
        loop = ExitStack()
        whole = ExitStack()
        prob = sb("prob", [P, BUFS, 512], F32, whole)
        whole.close()
        prob_lo = sb("prob_lo", [P, BUFS, 512], F32R, loop)
        prob_hi = sb("prob_hi", [P, BUFS, 512], F32R, loop)
        rows = sb("rows", [P, 2, T], F32, loop)
        mrow = rows[:, :, :].bitcast(F32R)
        ostage = rows[0:2 * HD + 1, :, :]
        oh, ol, osum = x, zT, z
        loop.close()
        ph1.close()
        small = sb("small", [P, 128])
        zc = sb("zc", [P, 2, T])
        identb = sb("identb", [P, P], BF16)
        q1 = sb("q1", [P, T])
        xt = sb("xt", [P, TT, D])
        unit = ExitStack()
        gu_part = sb("gu_part", [P, 3, 2, 2, 2 * I], F32R, unit)
        down_part = sb("down_part", [P, 3, 2, D], F32R, unit)
        z_part = sb("z_part", [P, 2, 2, T], F32R, unit)
        h_part = sb("h_part", [P, 3, 2, T], F32R, unit)
        hw = sb("hw", [P, 2, T], F32, unit)
        esg = sb("esg", [P, 2, T], F32, unit)
        euc = sb("euc", [P, 2, T], F32, unit)
        unit.close()
        wo = sb("wo", [P, 2, D])
        wqkv = sb("wqkv", [P, 2, 3 * D])
        bqkv = sb("bqkv", [P, 3 * D])
        wout = sb("wout", [P, 2, D])
        bout = sb("bout", [P, D])
        clips = sb("clips", [P, 2])
        wq1 = sb("wq1", [P, 2, P])
        wk1 = sb("wk1", [P, 2, P])
        wv1 = sb("wv1", [P, 2, D])
        wfi = sb("wfi", [P, 2, 2 * D])
        wfo = sb("wfo", [P, 2, 2 * D])
        bfi = sb("bfi", [P, 2 * D])
        bfo = sb("bfo", [P, 2 * D])
        gb = sb("gb", [P, 6, D])
        b1 = sb("b1", [P, 8])
        b2 = sb("b2", [P, D])
        dskip = sb("dskip", [P, D])
        gate = sb("gate", [P, 1])
        tmask_u = sb("tmask_u", [P, TT], U8)
        tmask = sb("tmask", [P, TT])
        dft = sb("dft", [P, 2, 2 * T])
        dftT = sb("dftT", [P, 4, T])
        Kf = sb("Kf", [P, 4, D])
        wgg = sb("wgg", [P, 2, D])
        wgc = sb("wgc", [P, 2, D])
        bgc = sb("bgc", [P, 2, 2])
        router = sb("router", [P, 2, E])
        rbias = sb("rbias", [P, E])
        cT = sb("cT", [P, 2, T])
        y = sb("y", [P, TT, D])
        Kt = y
        big = ExitStack()
        over_ctx = ExitStack()
        ctxT2 = sb("ctxT2", [P, 2, M], F32, over_ctx)
        over_ctx.close()
        EB = sb("EB", [P, 2, M], F32, big)
        k1T = sb("k1T", [P, M], F32, big)
        attn = ExitStack()
        prod = sb("prod", [P, 2, 8 * H * HD], F32, attn)
        qkv = sb("qkv", [P, TT, 3 * D], F32, attn)
        sc = sb("sc", [P, TT, H * H], F32, attn)
        attn.close()
        AM = sb("AM", [P, M], F32, big)
        ctxn = sb("ctxn", [P, KT, CD], F32, big)
        ffn = ExitStack()
        wraw = sb("wraw", [P, 2, 6, D], F32, ffn)
        wdraw = sb("wdraw", [P, 2, F_], F32, ffn)
        wint = sb("wint", [P, 2, 6, D], BF16, ffn)
        wdint = sb("wdint", [P, 2, F_], BF16, ffn)
        guT = sb("guT", [P, 2, 2, F_], BF16, ffn)
        wdT = sb("wdT", [P, 6, D], BF16, ffn)
        xqT = sb("xqT", [P, 2, T], BF16, ffn)
        sg, hf = wraw[:, 0], wraw[:, 1]
        hq = sb("hq", [P, 6, T], BF16, ffn)
        ffn.close()
        Asc = sb("Asc", [P, 3, M], F32, big)
        cand, cand_left = (v[:, :, :].rearrange("p t d -> p (t d)") for v in (y, zT))
        mask8, mask8b = ([v[32 * h:32 * h + 8] for h in range(4)] for v in (bqkv[:, 0:512], cT[:, 0, :].bitcast(BF16)))
        AMT = wqkv[:, :, 0:4 * P].rearrange("p n (u t) -> p n u t", u=4)
        m8 = sb("m8", [P, 2, 32], F32, big)
        big.close()
        moe = ExitStack()
        Gh = sb("Gh", [P, 8, T], F32, moe)
        Yf = sb("Yf", [P, 4, D], F32, moe)
        gup = sb("gup", [P, E, 2, 2 * I], F32, moe)
        down = sb("down", [P, E, D], F32, moe)
        sgu = sb("sgu", [P, 2, 2, 512], F32, moe)
        sdn = sb("sdn", [P, 4, D], F32, moe)
        dense = ExitStack()
        w1 = sb("w1", [P, 2, 4 * D], F32, dense)
        w2 = sb("w2", [P, 8, D], F32, dense)
        dense.close()
        gt = sb("gt", [P, 2, T], F32, moe)
        cd = sb("cd", [P, 2, T], F32, moe)
        wT = sb("wT", [2 * E, T], F32R, moe)
        wtok = sb("wtok", [P, TT, 2 * E], F32, moe)
        pick = sb("pick", [2 * E, E], F32R, moe)
        rt = sb("rt", [P, 4, TT, E], F32, moe)
        moe.close()

        bank = lambda b: PS[:, b, :]
        at = lambda *tags: {tag: n + 1 for n, tag in enumerate(tags)}
        LN = at("ln0", "ln1", "ln2", "ln3", "xin", "ln4", "nout", "ln5", "ln6")
        Z = at("ln0", "ln1", "attn_out", "ln2", "ffn_q", "ln3", "xin", "ln4", "nout", "ln5", "ln6")
        ZT = at("ln0", "ln1", "attn_out", "ffn_q", "ln3", "ln4", "ln5", "ln6")

        def ln_stats(dve, link, tag, src, affine=None):
            for t in range(TT):
                last = nc.vector.bn_stats(stats[:, t, :], src[:, t, :])
            link(last)
            for t in range(TT):
                last = nc.vector.bn_aggr(mv[:, t, :], stats[:, t, :])
            last.then_inc(S("ln_var"), 1)
            dve.wait_ge(S("ln_sd"), LN[tag])
            link(nc.vector.reciprocal(rs[:, :], sd[:, :]))
            for t in range(TT):
                last = nc.vector.tensor_scalar(z[:, t, :], src[:, t, :], mv[:, t, 0:1], rs[:, t:t + 1],
                                               ALU.subtract, ALU.mult)
            if affine is not None:
                link(last)
                g, s = (gb[:, affine + n, :].unsqueeze(1).broadcast_to([P, TT, D]) for n in range(2))
                link(nc.vector.tensor_tensor(z[:, :, :], z[:, :, :], g, ALU.mult))
                last = nc.vector.tensor_tensor(z[:, :, :], z[:, :, :], s, ALU.add)
            last.then_inc(S("z_ready"), 1)
            dve.wait_ge(S("z_ready"), Z[tag])

        def ln_sqrt(act, tag):
            act.wait_ge(S("ln_var"), LN[tag])
            nc.scalar.activation(sd[:, :], mv[:, :, 1], ACT.Sqrt, bias=eps[:, 0:1]).then_inc(S("ln_sd"), 1)

        def to_features(pe, src, b, tag):
            pe.wait_ge(S("z_ready"), Z[tag])
            for m in range(2):
                for t in range(TT):
                    last = nc.tensor.transpose(bank(b)[:, m * T + t * P:m * T + (t + 1) * P],
                                               src[:, t, m * P:(m + 1) * P], ident[:, :])
            last.then_inc(S("zT_full"), 1)

        def keep_features(act, dst, b, tag):
            act.wait_ge(S("zT_full"), ZT[tag])
            nc.scalar.copy(dst[:, :, :], bank(b)).then_inc(S("zT_kept"), 1)

        S_NEXT = {0: 5, 2: 6, 4: 7}
        S_AFTER = {6: 0, 8: 1, 10: 2, 12: 3, 14: 4}
        M_AT = 8
        DVE_EARLY = 1
        WEIGHT_BANK = (3, 6, 7)
        AHEAD = 4

        def gu_of(n):
            return sgu[:, :, :, n * P:(n + 1) * P] if n < 4 else gup[:, n - 4].rearrange("p k (g i) -> p k g i", g=2)

        def down_of(n):
            return sdn[:, n, :] if n < 4 else down[:, n - 4, :]

        def arrived(eng, n):
            if n == 0:
                eng.wait_ge(S("x_new"), 10)
            eng.wait_ge(S("shared_in"), 32) if n < 4 else eng.wait_ge(S(f"experts_in{(n - 4) // 8}"), 32)

        qkvh = [qkv[:, t, :].rearrange("p (h c) -> p h c", c=3 * HD) for t in range(TT)]

        def score_products(n):
            t, half = divmod(n, 2)
            q4 = qkvh[t][:, 8 * half:8 * half + 8, 0:HD].unsqueeze(2).broadcast_to([P, 8, H, HD])
            k4 = qkvh[t][:, :, HD:2 * HD].unsqueeze(1).broadcast_to([P, 8, H, HD])
            return prod[:, n % 2, :].rearrange("p (h g d) -> p h g d", h=8, g=H), q4, k4

        def value_products(n):
            t, half = divmod(n, 2)
            a4 = sc[:, t, half * 128:half * 128 + 128].rearrange("p (h g) -> p h g", g=H).unsqueeze(2)\
                .broadcast_to([P, 8, HD, H])
            v4 = qkvh[t][:, :, 2 * HD:3 * HD].rearrange("p g d -> p d g").unsqueeze(1).broadcast_to([P, 8, HD, H])
            return prod[:, n % 2, :].rearrange("p (h d g) -> p h d g", h=8, d=HD), a4, v4

        block = ctx.enter_context(nc.Block())

        @block.sync
        def _(sp):
            def move(to, rows_, done):
                sp.dma_start(to.bitcast(F32), rows_.bitcast(F32)).then_inc(S(done), 16)

            sp.dma_start(x[:, :, :], A["x"].rearrange("(t p) d -> p t d", p=P)).then_inc(S("x_in"), 16)
            sp.dma_start(wk[:, 0, :], A["L0_xattn_Wk"][0:P, :]).then_inc(S("wk_in"), 16)
            sp.dma_start(wk[0:C1, 1, :], A["L0_xattn_Wk"][P:CD, :]).then_inc(S("wk_in"), 16)
            for c in range(4):
                cs = slice(c * 1024, (c + 1) * 1024)
                sp.dma_start(ctxT[:, 0, cs], A["ctxT"][0:P, cs]).then_inc(S(f"ctxT_in{c}"), 16)
                sp.dma_start(ctxT[0:C1, 1, cs], A["ctxT"][P:CD, cs]).then_inc(S(f"ctxT_in{c}"), 16)
                if c == 0:
                    sp.dma_start(ident[:, :], A["ident"]).then_inc(S("wq_in"), 16)
                    sp.dma_start(wq[:, :, :], A["L0_xattn_Wq"].rearrange("(k p) d -> p k d", p=P)).then_inc(S("wq_in"), 16)
                    sp.dma_start(fac[:, :], A["lfac"]).then_inc(S("s4_in"), 16)
                    sp.dma_start(phs[:, :], A["phase"]).then_inc(S("s4_in"), 16)
                    sp.dma_start(dtb[:, :], A["L1_xattn_log_dt"].partition_broadcast(P)).then_inc(S("s4_in"), 16)
                    for n, name in enumerate(("A_reT", "A_imT", "C_reT", "C_imT")):
                        for half in range(2):
                            sp.dma_start(s4[NS * half:NS * (half + 1), n, :], A[name]).then_inc(S("s4_in"), 16)
                    sp.dma_start(mku[:, :], A["ctx_mask"].rearrange("(p j) -> p j", p=P)).then_inc(S("mku_in"), 16)
                if c == 1:
                    sp.dma_start(wv[:, 0, :], A["L0_xattn_Wv"][0:P, :]).then_inc(S("wv_in"), 16)
                    sp.dma_start(wv[0:C1, 1, :], A["L0_xattn_Wv"][P:CD, :]).then_inc(S("wv_in"), 16)
            sp.wait_ge(S("maskb_ready"), 1)
            sp.dma_start(rows_scratch.rearrange("r (p j) -> p r j", p=P), maskb[:, :, :]).then_inc(S("mask_out"), 16)
            def store_kernel(n):
                sp.wait_ge(S("K_staged"), n + 2)
                sp.dma_start(K_scratch[:, :, LA * n:LA * (n + 1)],
                             Kstage[:, n % 2, :].rearrange("a (b d) -> a b d", d=LA)).then_inc(S("K_out"), 16)

            sp.wait_ge(S("q_lo_ready"), 2)
            for n, q in enumerate((q_hi, q_lo)):
                move(q_scratch[n], q[:, :, :], "q_out")
            for n in range(5):
                store_kernel(n)
            sp.wait_ge(S("kv_low"), 4 + 32)
            sp.wait_ge(S("mask_out"), 16)
            for s in range(2):
                for par in range(2):
                    sp.dma_start(kst[64 * par + 48:64 * par + 64, s, :].bitcast(F32), rows_scratch).then_inc(S("kmask_in"), 16)

            def load_stack(p):
                for par in range(2):
                    src = 32 * (p % 4) + HD * par
                    for r, k in enumerate((k_hi, k_hi, k_lo)):
                        b = 64 * par + HD * r
                        move(kst[b:b + HD, p % 2, :], k[src:src + HD, p // 4, :], "kst_in")

            def load_queries(h):
                if h >= 4:
                    sp.wait_ge(S("st_full"), SLOTS * (h - 3))
                b, f = 64 * (h % 2), slice(HD * (h % 8), HD * (h % 8 + 1))
                for r, part in enumerate((0, 1, 0)):
                    move(qst[b + HD * r:b + HD * (r + 1), h % 4, :], q_scratch[part, f, h // 8, :], f"q_in{h % 4}")
                sp.dma_start(qst[b + 48:b + 62, h % 4, :].bitcast(F32), rows_scratch[2:16, 0:T])\
                    .then_inc(S(f"q_in{h % 4}"), 16)

            def load_max(h):
                sp.wait_ge(S("mrow_ready"), h + 1)
                b = 64 * (h % 2) + 49
                move(qst[b:b + 2, h % 4, :], mrow[96:97, :, :], "m_in")

            def gather_head(h):
                sp.wait_ge(S("o_staged"), h + 3)
                f = slice(HD * (h % 8), HD * (h % 8 + 1))
                st = ostage[:, h % 2, :]
                sp.dma_start(oh[f, h // 8, :], st[0:HD, :]).then_inc(S("o_in"), 16)
                sp.dma_start(ol[f, h // 8, :], st[HD + 1:2 * HD + 1, :]).then_inc(S("o_in"), 16)
                sp.dma_start(osum[f, h // 8, :], st[HD:HD + 1, :].unsqueeze(1).broadcast_to([1, HD, T])).then_inc(S("o_in"), 16)

            store_kernel(5)
            load_stack(0)
            store_kernel(6)
            load_stack(1)
            store_kernel(7)
            sp.wait_ge(S("q_out"), 32)
            sp.wait_ge(S("stacks_set"), 2)
            for h in range(4):
                load_queries(h)
                store_kernel(8 + h)
            for n in range(12, 16):
                store_kernel(n)
            def load(to, rows_, done):
                sp.dma_start(to, rows_).then_inc(S(done), 16)

            rows2 = lambda a: a.rearrange("(k p) n -> p k n", p=P)
            across = lambda a: a.partition_broadcast(P)

            def load_weights(part):
                if part == 0:
                    load(wo[:, :, :], rows2(A["L0_xattn_Wo"]), "self_in")
                    load(wqkv[:, :, :], rows2(A["L0_attn_W_qkv"]), "self_in")
                    load(bqkv[:, :], across(A["L0_attn_b_qkv"]), "self_in")
                elif part == 1:
                    load(wout[:, :, :], rows2(A["L0_attn_W_out"]), "self_in")
                    load(bout[:, :], across(A["L0_attn_b_out"]), "self_in")
                    load(clips[:, 0:1], across(A["L0_ffn_clip_x"]), "wffn_in")
                    load(clips[:, 1:2], across(A["L0_ffn_clip_down"]), "wffn_in")
                    load(wk1[:, 0, :], A["L1_xattn_Wk"][0:P, :], "keys2_in")
                    load(wk1[0:C1, 1, :], A["L1_xattn_Wk"][P:CD, :], "keys2_in")
                elif part == 2:
                    load(dft[:, :, :], rows2(A["dft"]), "keys2_in")
                    load(dftT[:, :, :], rows2(A["dftT"]), "keys2_in")
                    load(wq1[:, :, :], rows2(A["L1_xattn_Wq"]), "film_in")
                    load(tmask_u[:, :], A["text_mask"], "film_in")
                elif part == 3:
                    load(wv1[:, 0, :], A["L1_xattn_Wv"][0:P, :], "film_in")
                    load(wv1[0:C1, 1, :], A["L1_xattn_Wv"][P:CD, :], "film_in")
                    load(wfi[:, :, :], rows2(A["L1_xattn_W_film_in"]), "film_in")
                    load(wfo[:, :, :], rows2(A["L1_xattn_W_film_out"]), "film_in")
                elif part == 4:
                    load(bfi[:, :], across(A["L1_xattn_b_film_in"]), "film_in")
                    load(bfo[:, :], across(A["L1_xattn_b_film_out"]), "film_in")
                    load(bgc[:, 0, :], A["bgT"], "rest_in")
                    load(bgc[:, 1, :], A["bcT"], "rest_in")
                    load(router[:, :, :], rows2(A["routerT"]), "rest_in")
                    load(rbias[:, :], across(A["L1_ffn_e_score_correction_bias"]), "rest_in")
                    for n, name in enumerate(("g_norm_in", "b_norm_in", "g_ffn", "b_ffn", "g_norm_out", "b_norm_out")):
                        load(gb[:, n, :], across(A["L1_xattn_" + name]), "film_in")
                elif part == 5:
                    load(b2[:, :], across(A["L1_xattn_b2"]), "film_in")
                    load(dskip[:, :], across(A["L1_xattn_D_skip"]), "film_in")
                    load(gate[:, :], across(A["L1_xattn_mod_gate"]), "film_in")
                    load(b1[:, :], A["b1T"], "film_in")
                    load(wgg[:, :, :], rows2(A["WgT"]), "rest_in")
                    load(wgc[:, :, :], rows2(A["WcT"]), "rest_in")

            load_max(0)
            for p in range(PAIRS):
                if p == PAIRS - 2:
                    sp.wait_ge(S("kst_in"), 96 * PAIRS)
                load_max(2 * p + 1)
                if p + 2 < PAIRS:
                    load_queries(2 * p + 4)
                else:
                    load_weights(3 * (p - PAIRS + 2))
                gather_head(2 * p)
                if p + 2 >= PAIRS:
                    load_weights(3 * (p - PAIRS + 2) + 1)
                if p + 1 < PAIRS:
                    load_max(2 * p + 2)
                    if p + 2 < PAIRS:
                        sp.wait_ge(S("st_full"), 2 * SLOTS * (p + 1))
                        load_stack(p + 2)
                        load_queries(2 * p + 5)
                    else:
                        load_weights(2)
                gather_head(2 * p + 1)
            load_weights(5)
            sp.wait_ge(S("aT"), 2)
            load(x[:, :, :], A["x"].rearrange("(t p) d -> p t d", p=P), "x_in")
            for n, name in enumerate(("L0_ffn_w_gate", "L0_ffn_w_up")):
                load(wraw[:, n, 0:5, :], A[name][0:5 * P, :].rearrange("(i p) n -> p i n", p=P), "wffn_in")
                load(wraw[0:FR[5], n, 5, :], A[name][5 * P:F_, :], "wffn_in")
            load(wdraw[:, :, :], rows2(A["L0_ffn_w_down"]), "wffn_in")
            load(ctxT2[:, 0, :], A["ctxT"][0:P, :], "keys2_in")
            load(ctxT2[0:C1, 1, :], A["ctxT"][P:CD, :], "keys2_in")
            load(Kt[:, 0, :], K_scratch[0:8].rearrange("a b d -> (a b) d"), "keys2_in")
            load(Kt[:, 1, :], K_scratch[8:16].rearrange("a b d -> (a b) d"), "keys2_in")
            sp.wait_ge(S("x_new"), 4)
            load(ctxn[:, :, :], A["ctx"].rearrange("(k p) c -> p k c", p=P), "ctxn_in")
            for h in range(4):
                load(mask8[h], rows_scratch[0].rearrange("(c k) -> c k", c=8), "mask8_in")
            sp.wait_ge(S("zc_ready"), 2)
            load(w1[:, :, :], rows2(A["L1_xattn_W1"]), "w12_in")
            load(w2[:, :, :], rows2(A["L1_xattn_W2"]), "w12_in")
            load(sgu[:, :, :, :], A["sguT"].rearrange("p (k g i) -> p k g i", k=2, g=2), "shared_in")
            load(sdn[:, :, :], A["sdnT"].rearrange("p (k n) -> p k n", k=4), "shared_in")
            for g in range(4):
                es = slice(8 * g, 8 * g + 8)
                load(gup[:, es, :, :], A["gupT"][:, es, :, :], f"experts_in{g}")
                load(down[:, es, :], A["downT"][:, es, :], f"experts_in{g}")
            sp.wait_ge(S("x_new"), 12)
            sp.dma_start(out.rearrange("(t p) d -> p t d", p=P), x[:, :, :]).then_inc(S("out_done"), 16)
            sp.wait_ge(S("out_done"), 16)

        @block.tensor
        def _(pe):
            pe.wait_ge(S("wk_in"), 32)

            def fill_k(c, n):
                for j, m in enumerate((0, 1)):
                    b = n + j
                    for k in range(2):
                        r = P if k == 0 else C1
                        last = nc.tensor.matmul(bank(b), wk[0:r, k, m * P:(m + 1) * P],
                                                ctxT[0:r, k, bass.ds(c * 512, 512)], start=(k == 0), stop=(k == 1))
                    last.then_inc(S("fill"), 1)

            for i in range(4):
                pe.wait_ge(S(f"ctxT_in{i}"), 32)
                for u in range(2):
                    pe.wait_ge(S("kv_low"), 4 * i + 2 * u + 2)
                    fill_k(2 * i + u, 2 * u)
            pe.wait_ge(S("wq_in"), 32)
            to_features(pe, z, 4, "ln0")
            pe.wait_ge(S("zT_kept"), ZT["ln0"])
            for m in range(2):
                for k in range(2):
                    last = nc.tensor.matmul(bank(5)[:, m * T:(m + 1) * T], wq[:, k, m * P:(m + 1) * P], zT[:, k, :],
                                            start=(k == 0), stop=(k == 1))
                last.then_inc(S("q_full"), 1)
            pe.wait_ge(S("wv_in"), 32)
            def fill_v(n):
                pe.wait_ge(S("kv_low"), 16 + n + 1)
                for u in range(2):
                    for k in range(2):
                        r = P if k == 0 else C1
                        last = nc.tensor.matmul(bank(n % 4)[:, u * D:(u + 1) * D],
                                                ctxT[0:r, k, (2 * n + u) * P:(2 * n + u + 1) * P], wv[0:r, k, :],
                                                start=(k == 0), stop=(k == 1))
                last.then_inc(S("fill"), 1)

            for n in range(4):
                fill_v(n)
            for n in range(16):
                s = n % 2
                pe.wait_ge(S("uv_ready"), n + 2)
                pe.wait_ge(S("K_staged"), n + 1)
                o = bank(6 + s)[0:LA, 0:LA * LA].rearrange("a (b d) -> a d b", d=LA)
                for d in range(LA):
                    last = nc.tensor.matmul(o[:, d, :], UV[:, s, d, 0:LA], UV[:, s, d, LA:2 * LA],
                                            start=True, stop=True)
                last.then_inc(S("K_full"), 1)
                for m in (2 * n + 4, 2 * n + 5):
                    if m < 16:
                        fill_v(m)

            def scores(h, s):
                t, c = s // 4, s % 4
                for u in range(2):
                    last = nc.tensor.matmul(bank(2 * (s % 2) + u), qst[:, h % 4, t * P:(t + 1) * P],
                                            kst[:, h // 2 % 2, c * 1024 + u * 512:c * 1024 + (u + 1) * 512],
                                            start=True, stop=True)
                last.then_inc(S("s_full"), 1)

            def scores_t(h, j):
                for u in range(2):
                    last = nc.tensor.matmul(bank(4 + j % 2)[:, u * T:(u + 1) * T],
                                            kst[:, h // 2 % 2, (2 * j + u) * P:(2 * j + u + 1) * P],
                                            qst[:, h % 4, :], start=True, stop=True)
                last.then_inc(S("st_full"), 1)

            def max_row(h):
                for t in range(TT):
                    last = nc.tensor.matmul(bank(7)[96:97, t * P:(t + 1) * P], mx[:, h % 2, t:t + 1], ident[:, :],
                                            start=True, stop=True)
                last.then_inc(S("mrow_full"), 1)

            def weigh(p, par, j):
                for u in range(2):
                    for part in (prob_hi, prob_lo):
                        last = nc.tensor.matmul(bank(6 + par)[0:2 * HD + 1, 0:T],
                                                vst[:, 2 * j + u, p * 2 + par, :],
                                                part[:, j % BUFS, u * T:(u + 1) * T],
                                                start=(j == 0 and u == 0 and part is prob_hi),
                                                stop=(j == SLOTS - 1 and u == 1 and part is prob_lo))
                last.then_inc(S("pv_done"), 1)

            def pair(p):
                for i in range(2 * SLOTS):
                    par, j = divmod(i, SLOTS)
                    h = 2 * p + par
                    g, s = (h + 1, S_NEXT[j]) if j in S_NEXT else (h + 2, S_AFTER[j]) if j in S_AFTER else (H, 0)
                    if g < H:
                        if g % 2 == 0 and s == 0:
                            pe.wait_ge(S("kst_in"), 96 * (g // 2 + 1))
                        if s == 0:
                            pe.wait_ge(S(f"q_in{g % 4}"), 64 * (g // 4 + 1))
                        pe.wait_ge(S("s_free"), 8 * g + s + 1)
                        scores(g, s)
                    if j == M_AT and h + 1 < H:
                        pe.wait_ge(S("m_ready"), h + 2)
                        pe.wait_ge(S("mrow_ready"), h + 1)
                        max_row(h + 1)
                    n = 2 * SLOTS * p + i + AHEAD
                    if n < SLOTS * H:
                        slot_t(n)
                    if j == 0:
                        pe.wait_ge(S("o_staged"), h + 1)
                    q, r = divmod(i, 4)
                    if r < 3:
                        pe.wait_ge(S("low_pool"), p * 24 + (3 * q + r + 1))
                    else:
                        pe.wait_ge(S("low_dve"), p * 8 + (q + 1))
                    weigh(p, par, j)

            def slot_t(n):
                h, j = divmod(n, SLOTS)
                if j == 0:
                    pe.wait_ge(S("m_in"), 16 * (h + 1))
                pe.wait_ge(S("exp_done"), n + 1)
                scores_t(h, j)

            for h in range(2):
                pe.wait_ge(S(f"q_in{h}"), 64)
            pe.wait_ge(S("kmask_in"), 16 * 4)
            pe.wait_ge(S("kst_in"), 192)
            pe.wait_ge(S("stacks_set"), 2)
            pe.wait_ge(S("q_lo_ready"), 2)
            pe.wait_ge(S("kv_low"), 4 + 32)
            for h, n in ((0, 8), (1, 5)):
                for s in range(n):
                    pe.wait_ge(S("s_free"), 8 * h + s + 1)
                    scores(h, s)
                if h == 0:
                    pe.wait_ge(S("m_ready"), 1)
                    pe.wait_ge(S("K_staged"), 17)
                    max_row(0)
            for n in range(AHEAD):
                slot_t(n)
            for p in range(PAIRS):
                pair(p)
            pe.wait_ge(S("self_in"), 16 * 5)
            pe.wait_ge(S("aT"), 2)
            for t in range(TT):
                for k in range(2):
                    last = nc.tensor.matmul(bank(t)[:, 0:D], zT[:, k, t * P:(t + 1) * P], wo[:, k, :],
                                            start=(k == 0), stop=(k == 1))
                last.then_inc(S("projected"), 1)

            def features(tag, b=6, src=z):
                to_features(pe, src, b, tag)
                pe.wait_ge(S("zT_kept"), ZT[tag])

            def project(lhs, w, n, cols, b, done, width=None):
                for t in range(TT):
                    for k in range(2):
                        last = nc.tensor.matmul(bank(b + t)[:, 0:n], lhs[:, k, t * P:(t + 1) * P], w[:, k, cols:cols + n],
                                                start=(k == 0), stop=(k == 1))
                    last.then_inc(S(done), 1)

            def to_tokens(src, b, ready):
                pe.wait_ge(S(ready), 1)
                for t in range(TT):
                    for m in range(2):
                        last = nc.tensor.transpose(bank(b)[:, t * D + m * P:t * D + (m + 1) * P],
                                                   src[:, m, t * P:(t + 1) * P], ident[:, :])
                last.then_inc(S("tokens_full"), 1)

            features("ln1")
            pe.wait_ge(S("self_in"), 16 * 5)
            for t in range(TT):
                for c in range(2):
                    for k in range(2):
                        last = nc.tensor.matmul(bank(2 * t + c)[:, 0:384], zT[:, k, t * P:(t + 1) * P],
                                                wqkv[:, k, c * 384:(c + 1) * 384], start=(k == 0), stop=(k == 1))
            last.then_inc(S("qkv_full"), 1)
            pe.wait_ge(S("keys2_in"), 16 * 8)
            for c in range(CH):
                if c >= 2:
                    pe.wait_ge(S("k1_kept"), c - 1)
                for k in range(2):
                    r = P if k == 0 else C1
                    last = nc.tensor.matmul(bank(4 + c % 2), wk1[0:r, k, :], ctxT2[0:r, k, c * 512:(c + 1) * 512],
                                            start=(k == 0), stop=(k == 1))
                last.then_inc(S("k1_full"), 1)

            def spectrum(src, done):
                for f in range(4):
                    for k in range(2):
                        last = nc.tensor.matmul(bank(6 + f // 2)[:, f % 2 * D:(f % 2 + 1) * D],
                                                dft[:, k, f * P:(f + 1) * P], src[:, k, :],
                                                start=(k == 0), stop=(k == 1))
                last.then_inc(S(done), 1)

            pe.wait_ge(S("keys2_in"), 16 * 8)
            spectrum(Kt, "Kf_full")
            pe.wait_ge(S("wints"), 1)
            pe.wait_ge(S("k1_kept"), CH)
            pe.wait_ge(S("Kf_kept"), 2)
            for n in range(2):
                for k in range(2):
                    b = (4 + k if n == 0 else 6 + k)
                    for i, r in enumerate(FR):
                        last = nc.tensor.transpose(bank(b).bitcast(BF16)[:, i * P:i * P + r],
                                                   wint[0:r, n, i, k * P:(k + 1) * P], identb[0:r, 0:r])
                    last.then_inc(S("wT_full"), 1)
            for m in range(2):
                pe.wait_ge(S("wT_kept"), m + 1)
                for i, r in enumerate(FR):
                    last = nc.tensor.transpose(bank(4 + m).bitcast(BF16)[0:r, i * P:(i + 1) * P],
                                               wdint[:, m, i * P:i * P + r], identb[:, :])
                last.then_inc(S("wT_full"), 1)
            pe.wait_ge(S("wT_kept"), 6)
            features("attn_out")
            pe.wait_ge(S("self_in"), 16 * 5)
            project(zT, wout, D, 0, 0, "projected")

            features("ffn_q")
            for i, r in enumerate(FR):
                for n in range(2):
                    for k in range(2):
                        last = nc.tensor.matmul(bank(i)[0:r, n * T:(n + 1) * T], guT[:, n, k, i * P:i * P + r],
                                                xqT[:, k, :], start=(k == 0), stop=(k == 1))
                last.then_inc(S("gu_full"), 1)
            pe.wait_ge(S("hq_ready"), 1)
            for m in range(2):
                for i, r in enumerate(FR):
                    last = nc.tensor.matmul(bank(6)[:, m * T:(m + 1) * T], wdT[0:r, i, m * P:(m + 1) * P],
                                            hq[0:r, i, :], start=(i == 0), stop=(i == 5))
            last.then_inc(S("down_full"), 1)
            to_tokens(zT, 7, "down_kept")

            features("ln3")
            pe.wait_ge(S("film_in"), 16 * 18)
            for k in range(2):
                last = nc.tensor.matmul(bank(5)[:, 0:T], wq1[:, k, :], zT[:, k, :], start=(k == 0), stop=(k == 1))
            last.then_inc(S("feature_proj"), 1)
            pe.wait_ge(S("feature_kept"), 1)

            def weigh_context(t):
                for g in range(8):
                    n = 8 * t + g
                    pe.wait_ge(S("AM_ready"), 1 if t == 0 else g + 2)
                    if n >= 2:
                        pe.wait_ge(S("AMT_kept"), n - 1)
                    for u in range(4):
                        last = nc.tensor.transpose(bank(4 + g % 2)[:, u * P:(u + 1) * P],
                                                   AM[:, (4 * g + u) * P:(4 * g + u + 1) * P], ident[:, :])
                    last.then_inc(S("AMT_full"), 1)
                    if g > 0:
                        context_sum(t, g - 1)
                context_sum(t, 7)

            def context_sum(t, g):
                pe.wait_ge(S("AMT_kept"), 8 * t + g + 1)
                pe.wait_ge(S("ctxn_in"), 16)
                for u in range(4):
                    kt = 4 * g + u
                    for c, w in ((0, P), (1, C1)):
                        last = nc.tensor.matmul(bank(6 + c)[0:w, t * P:(t + 1) * P], ctxn[:, kt, c * P:c * P + w],
                                                AMT[:, g % 2, u, :], start=(kt == 0), stop=(kt == KT - 1))
                last.then_inc(S("zc_full"), 1)

            def masked_scores(n):
                t, h = divmod(n, 4)
                for c in range(CH):
                    m = CH * n + c
                    if m >= 4:
                        pe.wait_ge(S("A_copied"), m - 3)
                    nc.tensor.matmul(bank(c % 4), q1[32 * h:32 * h + 32, t * P:(t + 1) * P],
                                     k1T[32 * h:32 * h + 32, c * 512:(c + 1) * 512], start=True, stop=False)
                    last = nc.tensor.matmul(bank(c % 4), identb[32 * h:32 * h + 8, 32 * h + c:32 * h + c + 1].broadcast_to([8, P]), mask8b[h],
                                            start=False, stop=True)
                    last.then_inc(S("A_full"), 1)

            pe.wait_ge(S("mask8_ready"), 1)
            for n in range(2):
                masked_scores(n)
            for n in range(8):
                pe.wait_ge(S("counted"), n + 1)
                nc.tensor.matmul(bank(7)[96:97, 0:1], small[:, 112 + n % 2:113 + n % 2], small[:, 114:115],
                                 start=True, stop=True).then_inc(S("count_full"), 1)
                if n == 5:
                    weigh_context(0)
                if n + 2 < 8:
                    masked_scores(n + 2)
            weigh_context(1)
            pe.wait_ge(S("zc_ready"), 2)
            pe.wait_ge(S("film_in"), 16 * 18)
            for m in range(2):
                for k in range(2):
                    r = P if k == 0 else C1
                    last = nc.tensor.matmul(bank(0)[:, m * T:(m + 1) * T], wv1[0:r, k, m * P:(m + 1) * P], zc[0:r, k, :],
                                            start=(k == 0), stop=(k == 1))
            last.then_inc(S("feature_proj"), 1)
            pe.wait_ge(S("feature_kept"), 2)
            project(cT, wfi, 2 * D, 0, 1, "film_in_full")
            project(cT, wfo, 2 * D, 0, 3, "film_out_full")
            pe.wait_ge(S("conv_ready"), 1)
            spectrum(z, "conv_full")
            pe.wait_ge(S("conv_ready"), 2)
            for t in range(TT):
                for f in range(4):
                    last = nc.tensor.matmul(bank(5)[:, t * D:(t + 1) * D], dftT[:, f, t * P:(t + 1) * P], Yf[:, f, :],
                                            start=(f == 0), stop=(f == 3))
            last.then_inc(S("conv_full"), 1)
            features("ln4")
            pe.wait_ge(S("w12_in"), 32)
            for m in range(8):
                for k in range(2):
                    last = nc.tensor.matmul(bank(m // 2)[:, m % 2 * T:(m % 2 + 1) * T], w1[:, k, m * P:(m + 1) * P],
                                            zT[:, k, :], start=(k == 0), stop=(k == 1))
                if m % 2 == 1:
                    last.then_inc(S("h1_full"), 1)
            for m in range(8):
                if m % 2 == 0:
                    pe.wait_ge(S("Gh_ready"), m // 2 + 1)
                for t in range(TT):
                    last = nc.tensor.matmul(bank(4 + t)[:, 0:D], Gh[:, m, t * P:(t + 1) * P], w2[:, m, :],
                                            start=(m == 0), stop=(m == 7))
            last.then_inc(S("conv_full"), 1)

            features("ln5")
            pe.wait_ge(S("rest_in"), 16 * 6)
            for n, w in enumerate((wgg, wgc)):
                for m in range(2):
                    for k in range(2):
                        last = nc.tensor.matmul(bank(n)[:, m * T:(m + 1) * T], w[:, k, m * P:(m + 1) * P], zT[:, k, :],
                                                start=(k == 0), stop=(k == 1))
                last.then_inc(S("gru_full"), 1)
            to_tokens(cT, 2, "gru_done")

            features("ln6")
            pe.wait_ge(S("rest_in"), 16 * 6)
            for t in range(TT):
                for k in range(2):
                    last = nc.tensor.matmul(bank(7)[:, t * E:(t + 1) * E], zT[:, k, t * P:(t + 1) * P], router[:, k, :],
                                            start=(k == 0), stop=(k == 1))
            last.then_inc(S("logits"), 1)

            def expert_in(n):
                if n >= 3:
                    pe.wait_ge(S("unit_read"), n - 2)
                pe.wait_ge(S("gu_low"), n + 1)
                for g in range(2):
                    for k in range(2):
                        for wp, zp in ((0, 0), (0, 1), (1, 0)):
                            last = nc.tensor.matmul(bank(n % 3)[:, g * T:(g + 1) * T],
                                                    gu_part[:, n % 3, wp, k, g * I:(g + 1) * I], z_part[:, zp, k, :],
                                                    start=(k + wp + zp == 0), stop=(k == 1 and wp == 1))
                if n >= 4:
                    e = n - 4
                    last = nc.tensor.matmul(bank(WEIGHT_BANK[n % 3])[:, 0:T], pick[:, e:e + 1].broadcast_to([2 * E, P]),
                                            wT[:, :], start=True, stop=True)
                last.then_inc(S("unit_full"), 1)

            def expert_out(n):
                pe.wait_ge(S("down_low"), n + 1)
                pe.wait_ge(S("h_low"), n + 1)
                for t in range(TT):
                    for hp, wp in ((0, 0), (1, 0), (0, 1)):
                        last = nc.tensor.matmul(bank(4 + t)[:, 0:D], h_part[:, n % 3, hp, t * P:(t + 1) * P],
                                                down_part[:, n % 3, wp, :],
                                                start=(n + hp + wp == 0), stop=(n == E + 3 and wp == 1))
                last.then_inc(S("unit_done"), 1)

            pe.wait_ge(S("z_low"), 1)
            expert_in(0)
            expert_in(1)
            for n in range(E + 4):
                if n == 2:
                    pe.wait_ge(S("wtok"), 1)
                    for t in range(TT):
                        last = nc.tensor.transpose(bank(7)[0:2 * E, t * P:(t + 1) * P],
                                                   wtok[:, t, :], ident[:, :])
                    last.then_inc(S("wT_t"), 1)
                    pe.wait_ge(S("wT_ready"), 2)
                if n + 2 < E + 4:
                    expert_in(n + 2)
                expert_out(n)

        @block.scalar
        def _(act):
            act.wait_ge(S("eps_set"), 1)
            ln_sqrt(act, "ln0")
            act.wait_ge(S("s4_in"), 16 * 11)
            nc.scalar.activation(dtb[:, :], dtb[:, :], ACT.Exp).then_inc(S("dt_ready"), 1)
            for i in range(4):
                for u in range(4):
                    c, m = 2 * i + u // 2, u % 2
                    act.wait_ge(S("fill"), 4 * i + u + 1)
                    nc.scalar.copy(k_hi[:, m, c * 512:(c + 1) * 512], bank(u)).then_inc(S("kv_high"), 1)
                if i == 1:
                    act.wait_ge(S("step_ready"), 1)
                    nc.scalar.activation(sw[:, 2, :], sw[:, 0, :], ACT.Tanh, scale=0.5)
                    nc.scalar.activation(sw[:, 3, :], sw[:, 4, :], ACT.Sin, scale=0.5)
                    nc.scalar.activation(sw[:, 4, :], sw[:, 4, :], ACT.Sin).then_inc(S("step_funcs"), 1)
            keep_features(act, zT, 4, "ln0")
            for m in range(2):
                act.wait_ge(S("q_full"), 2)
                nc.scalar.copy(q_hi[:, m, :], bank(5)[:, m * T:(m + 1) * T]).then_inc(S("q_hi_ready"), 1)

            def waves(i, j, values=True):
                n = 4 * i + j
                for m in (2 * j, 2 * j + 1) if values else ():
                    act.wait_ge(S("fill"), i * 8 + m + 17)
                    nc.scalar.copy(vst[:, bass.ds(i * 16 + 2 * m, 2), :, 0:HD],
                                   bank(m % 4).rearrange("p (u h d) -> p u h d", u=2, d=HD)).then_inc(S("kv_high"), 1)
                act.wait_ge(S("mag_arg"), n + 1)
                nc.scalar.activation(mag[:, j % 2], mag[:, j % 2], ACT.Exp).then_inc(S("mag_ready"), 1)
                act.wait_ge(S("primed"), n + 1)
                nc.scalar.activation(primer[:, 0:1], eps[:, 0:1], ACT.Sin).then_inc(S("primed"), 1)
                act.wait_ge(S("ang_ready"), n + 1)
                act.wait_ge(S("uv_ready"), n + 1)
                nc.scalar.activation(SV[:, :, 0:LA], yA[:, j % 2, :, 0:LA], ACT.Sin, bias=phs[:, 3:4], scale=-1.0)
                nc.scalar.activation(SV[:, :, LA:2 * LA], yA[:, j % 2, :, LA:2 * LA], ACT.Sin, bias=phs[:, 3:4], scale=phs[:, 0:1])
                nc.scalar.activation(T2[:, :, :], phases_of[j % 2][:, :, 0:LA], ACT.Sin, bias=phs[:, 4:5], scale=phs[:, 1:2])\
                    .then_inc(S("sin_ready"), 1)

            def stage(n, s=None):
                s = n % 2 if s is None else s
                act.wait_ge(S("K_full"), n + 3)
                act.wait_ge(S("K_out"), n * 16 + 16)
                nc.scalar.copy(Kstage[:, s, :], bank(6 + s)[0:LA, 0:LA * LA]).then_inc(S("K_staged"), 1)

            waves(0, 0)
            for j in range(1, 4):
                waves(0, j)
                stage(j - 1)
            for j in range(4):
                waves(1, j)
                stage(3 + j)
            with act.Fori(2, 4) as i:
                for j in range(4):
                    waves(i, j, False)
                    stage(i * 4 + (j - 1), (j - 1) % 2)
            stage(15)
            act.wait_ge(S("K_out"), 17 * 16)

            def keep_turned(act, t, g):
                act.wait_ge(S("AMT_full"), 8 * t + g + 1)
                if 8 * t + g >= 2:
                    act.wait_ge(S("zc_full"), 8 * t + g - 1)
                nc.scalar.copy(AMT[:, g % 2, :, :], bank(4 + g % 2)).then_inc(S("AMT_kept"), 1)

            with act.Fori(0, PAIRS) as p:
                for i in range(2 * SLOTS):
                    q, r = divmod(i, 4)
                    act.wait_ge(S("st_full"), p * 32 + i + 1)
                    act.wait_ge(S("pv_done"), p * 32 + (i + 1))
                    if r < 3:
                        nc.scalar.activation(prob_hi[:, i % BUFS, :], bank(4 + i % 2), ACT.Exp, scale=HD ** -0.5)
                    nc.scalar.activation(prob[:, i % BUFS, :], bank(4 + i % 2), ACT.Exp, scale=HD ** -0.5)\
                        .then_inc(S("exp_done"), 1)

            def copy(to, frm, waits, done):
                for name, v in waits:
                    act.wait_ge(S(name), v)
                nc.scalar.copy(to, frm).then_inc(S(done), 1)

            ln_sqrt(act, "ln1")
            keep_features(act, zT, 6, "ln1")
            for c in range(CH):
                copy(k1T[:, c * 512:(c + 1) * 512], bank(4 + c % 2), [("k1_full", c + 1)], "k1_kept")
            for n in range(2):
                copy(Kf[:, 2 * n:2 * n + 2, :], bank(6 + n), [("Kf_full", 1)], "Kf_kept")
            act.wait_ge(S("sc_ready"), 1)
            nc.scalar.activation(sc[:, :, :], sc[:, :, :], ACT.Exp, scale=HD ** -0.5).then_inc(S("sc_exp"), 1)
            for n in range(2):
                for k in range(2):
                    b = (4 + k if n == 0 else 6 + k)
                    copy(guT[:, n, k, :], bank(b).bitcast(BF16)[:, 0:F_], [("wT_full", 2 * n + k + 1)], "wT_kept")
            for m in range(2):
                act.wait_ge(S("wT_full"), 5 + m)
                nc.scalar.copy(wdT[:, 0:5, m * P:(m + 1) * P],
                               bank(4 + m).bitcast(BF16)[:, 0:5 * P].rearrange("p (i h) -> p i h", i=5))
                nc.scalar.copy(wdT[0:FR[5], 5, m * P:(m + 1) * P], bank(4 + m).bitcast(BF16)[0:FR[5], 5 * P:6 * P])\
                    .then_inc(S("wT_kept"), 1)
            keep_features(act, zT, 6, "attn_out")

            act.wait_ge(S("wffn_in"), 16 * 7)
            nc.scalar.activation(small[:, 32:34], clips[:, :], ACT.Exp, scale=-1.0).then_inc(S("clip_exp"), 1)
            ln_sqrt(act, "ln2")
            act.wait_ge(S("zT_full"), ZT["ffn_q"])
            nc.scalar.copy(xqT[:, :, :], bank(6)).then_inc(S("zT_kept"), 1)
            act.wait_ge(S("comb_ready"), 1)
            for i, r in enumerate(FR):
                act.wait_ge(S("gu_full"), i + 1)
                nc.scalar.activation(sg[0:r, i, :], bank(i)[0:r, 0:T], ACT.Silu, scale=small[0:r, 40 + i:41 + i])\
                    .then_inc(S("sg_ready"), 1)
            act.wait_ge(S("down_full"), 1)
            for m in range(2):
                last = nc.scalar.activation(zT[:, m, :], bank(6)[:, m * T:(m + 1) * T], ACT.Copy,
                                            scale=small[:, 56 + m:57 + m])
            last.then_inc(S("down_kept"), 1)

            ln_sqrt(act, "ln3")
            keep_features(act, zT, 6, "ln3")
            copy(q1[:, :], bank(5)[:, 0:T], [("feature_proj", 1)], "feature_kept")

            def keep_scores(n):
                for c in range(CH):
                    act.wait_ge(S("A_full"), CH * n + c + 1)
                    if c == 0 and n >= 3:
                        act.wait_ge(S("top_weighed"), n - 2)
                    nc.scalar.activation(Asc[:, n % 3, c * 512:(c + 1) * 512], bank(c % 4), ACT.Copy, scale=32 ** -0.5)\
                        .then_inc(S("A_copied"), 1)

            act.wait_ge(S("x_new"), 6)
            keep_scores(0)
            keep_scores(1)
            for n in range(8):
                t, h = divmod(n, 4)
                act.wait_ge(S("top_found"), n + 1)
                nc.scalar.activation(EB[:, n % 2, :], Asc[:, n % 3, :], ACT.Exp, bias=small[:, 64 + n % 2:65 + n % 2])\
                    .then_inc(S("E_ready"), 1)
                if n + 2 < 8:
                    keep_scores(n + 2)
                if n >= 6:
                    continue
                act.wait_ge(S("r_ready"), n + 1)
                act.wait_ge(S("r_ready"), n + 1)
                if h == 0:
                    if t == 1:
                        for g in range(8):
                            keep_turned(act, 0, g)
                    nc.scalar.activation(AM[:, :], EB[:, n % 2, :], ACT.Copy, scale=small[:, 66 + n % 2:67 + n % 2])\
                        .then_inc(S("E_scaled"), 1)
                else:
                    nc.scalar.activation(EB[:, n % 2, :], EB[:, n % 2, :], ACT.Copy, scale=small[:, 66 + n % 2:67 + n % 2])\
                        .then_inc(S("E_scaled"), 1)
            for g in range(8):
                keep_turned(act, 1, g)
                if g == 4:
                    ln_sqrt(act, "xin")
            act.wait_ge(S("zc_full"), 16)
            nc.scalar.copy(zc[:, 0, :], bank(6)[:, 0:T]).then_inc(S("zc_ready"), 1)
            nc.scalar.copy(zc[0:C1, 1, :], bank(7)[0:C1, 0:T]).then_inc(S("zc_ready"), 1)
            copy(cT[:, :, :], bank(0), [("feature_proj", 2)], "feature_kept")
            ln_sqrt(act, "ln4")
            keep_features(act, zT, 6, "ln4")
            for m in range(8):
                act.wait_ge(S("h1_full"), m // 2 + 1)
                last = nc.scalar.activation(Gh[:, m, :], bank(m // 2)[:, m % 2 * T:(m % 2 + 1) * T], ACT.Gelu,
                                            bias=b1[:, m:m + 1])
                if m % 2 == 1:
                    last.then_inc(S("Gh_ready"), 1)
            ln_sqrt(act, "nout")

            ln_sqrt(act, "ln5")
            keep_features(act, zT, 6, "ln5")
            for n, (to, f) in enumerate(((gt, ACT.Sigmoid), (cd, ACT.Tanh))):
                act.wait_ge(S("gru_full"), n + 1)
                for m in range(2):
                    last = nc.scalar.activation(to[:, m, :], bank(n)[:, m * T:(m + 1) * T], f, bias=bgc[:, n, m:m + 1])
                last.then_inc(S("gru_act"), 1)

            ln_sqrt(act, "ln6")
            keep_features(act, zT, 6, "ln6")
            act.wait_ge(S("logits"), 1)
            nc.scalar.activation(rt[:, 0, :, :], bank(7)[:, 0:TT * E].rearrange("p (t e) -> p t e", t=TT), ACT.Sigmoid)\
                .then_inc(S("rscores"), 1)
            copy(z_part[:, 0, :, :], zT[:, :, :], [], "z_high")

            def high_gu(n):
                arrived(act, n)
                if n >= 3:
                    act.wait_ge(S("unit_full"), n - 2)
                copy(gu_part[:, n % 3, 0].rearrange("p k (g i) -> p k g i", g=2), gu_of(n), [], "gu_high")

            def high_down(n):
                arrived(act, n)
                if n >= 3:
                    act.wait_ge(S("unit_done"), n - 2)
                copy(down_part[:, n % 3, 0], down_of(n), [], "down_high")

            def high_h(n):
                if n >= 3:
                    act.wait_ge(S("unit_done"), n - 2)
                copy(h_part[:, n % 3, 0], hw[:, n % 2, :], [("unit_ready", n + 1)], "h_high")

            high_gu(0)
            high_gu(1)
            high_down(0)
            for n in range(E + 4):
                if n >= 1:
                    high_h(n - 1)
                if n == 2:
                    copy(wT[:, :], bank(7)[0:2 * E, 0:T], [("wT_t", 1)], "wT_ready")
                act.wait_ge(S("unit_full"), n + 1)
                if n >= 2:
                    act.wait_ge(S("unit_ready"), n - 1)
                nc.scalar.activation(esg[:, n % 2, :], bank(n % 3)[:, 0:T], ACT.Silu).then_inc(S("unit_silu"), 1)
                if n + 2 < E + 4:
                    high_gu(n + 2)
                if n + 1 < E + 4:
                    high_down(n + 1)
            high_h(E + 3)

        @block.gpsimd
        def _(pool):
            link = chain(pool, "pool_chain")
            nc.gpsimd.memset(eps[:, :], 1e-5).then_inc(S("eps_set"), 1)
            nc.gpsimd.memset(vst[:, :, :, HD:HD + 1].bitcast(F32), 1.0).then_inc(S("stacks_set"), 1)
            pool.wait_ge(S("stacks_set"), 1)
            nc.gpsimd.memset(qst[:, :, :].bitcast(F32), 0.0).then_inc(S("stacks_set"), 1)
            pool.wait_ge(S("stacks_set"), 2)
            pool.wait_ge(S("mku_in"), 16)
            link(nc.gpsimd.memset(maskb[:, 1:3, :], 1.0))
            link(nc.gpsimd.memset(maskb[:, 3:16, :], 0.0))
            link(nc.gpsimd.tensor_copy(maskb[:, 0, :], mku[:, :]))
            nc.gpsimd.tensor_scalar(maskb[:, 0, :], maskb[:, 0, :], -NEG, NEG, ALU.mult, ALU.add).then_inc(S("maskb_ready"), 1)
            bd = lambda v: v.unsqueeze(2).broadcast_to([P, LA, 2 * LA])
            facb = fac[:, :].unsqueeze(1).broadcast_to([P, LA, 2 * LA])
            bh = lambda v: v.unsqueeze(2).broadcast_to([P, LA, LA])
            pool.wait_ge(S("dC_ready"), 1)
            pool.wait_ge(S("mask_out"), 16)
            def phases(i, s):
                nc.gpsimd.tensor_tensor(phases_of[s % 2], bd(dtb[:, bass.ds(i * 32 + s * LA, LA)]), facb, ALU.mult)\
                    .then_inc(S("ang_arg"), 1)

            def magnitudes(i, s):
                nc.gpsimd.tensor_tensor(mag[:, s % 2], bd(sw[:, 0, bass.ds(i * 32 + s * LA, LA)]), facb, ALU.mult)\
                    .then_inc(S("mag_arg"), 1)

            def chunks(i, last=False):
                for s in range(2):
                    n = i * 2 + s
                    ds = bass.ds(i * 32 + s * LA, LA)
                    pool.wait_ge(S("mag_ready"), n + 1)
                    pool.wait_ge(S("sin_ready"), n + 3)
                    if not last:
                        phases(i, s + 2)
                    nc.gpsimd.tensor_tensor(T2[:, :, :], T2[:, :, :], mag[:, s, :, 0:LA], ALU.mult).then_inc(S("t2_a"), 1)
                    pool.wait_ge(S("t2_a"), n + 1)
                    nc.gpsimd.tensor_tensor(T2[:, :, :], T2[:, :, :], bh(s4[:, 3, ds]), ALU.mult).then_inc(S("t2_b"), 1)
                    pool.wait_ge(S("t2_b"), n + 1)
                    pool.wait_ge(S("sv_mag"), n + 1)
                    pool.wait_ge(S("K_full"), n + 1)
                    nc.gpsimd.tensor_tensor(UV[:, s, :, 0:LA], SV[:, :, 0:LA], T2[:, :, :], ALU.subtract)\
                        .then_inc(S("uv_ready"), 1)
                    if not last:
                        magnitudes(i, s + 2)

            magnitudes(0, 0)
            magnitudes(0, 1)
            pool.wait_ge(S("q_lo_ready"), 2)
            phases(0, 0)
            phases(0, 1)
            with pool.Fori(0, 7) as i:
                chunks(i)
            chunks(7, True)
            pool.wait_ge(S("K_out"), 17 * 16)
            with pool.Fori(0, PAIRS) as p:
                for i in range(2 * SLOTS):
                    q, r = divmod(i, 4)
                    if r < 3:
                        pool.wait_ge(S("exp_done"), p * 32 + (i + 3))
                        b = i % BUFS
                        nc.gpsimd.tensor_tensor(prob_lo[:, b, :], prob[:, b, :], prob_hi[:, b, :].bitcast(F32),
                                                ALU.subtract).then_inc(S("low_pool"), 1)

            pool.wait_ge(S("aT"), 2)
            nc.gpsimd.memset(wraw[64:P, :, 5, :], 1.0).then_inc(S("wraw_set"), 1)
            pool.wait_ge(S("wraw_set"), 1)
            for n, (products, half, step) in enumerate(((score_products, 1, 1), (score_products, 3, 2),
                                                        (value_products, 1, 4), (value_products, 3, 5))):
                pool.wait_ge(S("attn_step"), step)
                nc.gpsimd.tensor_tensor(*products(half), ALU.mult).then_inc(S("attn_pool"), 1)
                pool.wait_ge(S("attn_pool"), n + 1)
            for n in range(2):
                pool.wait_ge(S("absmax_part"), n + 1)
                nc.gpsimd.partition_all_reduce(small[:, 36 + n:37 + n], small[:, 34 + n:35 + n], P, RMAX)\
                    .then_inc(S("absmax_all"), 1)
                pool.wait_ge(S("absmax_all"), n + 1)
            for n in range(6):
                t, h = divmod(n, 4)
                pool.wait_ge(S("E_scaled"), n + 1)
                if h > 0:
                    nc.gpsimd.tensor_tensor(AM[:, :], AM[:, :], EB[:, n % 2, :], ALU.add).then_inc(S("E_added"), 1)
                    pool.wait_ge(S("E_added"), 3 * t + h)
                if h == 3:
                    nc.gpsimd.sem_inc(S("AM_ready"), 1)

            def low_gu(n):
                arrived(pool, n)
                pool.wait_ge(S("gu_high"), n + 1)
                parts = gu_part[:, n % 3].rearrange("p a k (g i) -> p a k g i", g=2)
                nc.gpsimd.tensor_tensor(parts[:, 1], gu_of(n), parts[:, 0].bitcast(F32), ALU.subtract)\
                    .then_inc(S("gu_low"), 1)

            def low_down(n):
                arrived(pool, n)
                pool.wait_ge(S("down_high"), n + 1)
                nc.gpsimd.tensor_tensor(down_part[:, n % 3, 1], down_of(n), down_part[:, n % 3, 0].bitcast(F32),
                                        ALU.subtract).then_inc(S("down_low"), 1)

            low_gu(0)
            low_gu(1)
            low_down(0)
            for n in range(E + 4):
                if n + 2 < E + 4:
                    low_gu(n + 2)
                if n + 1 < E + 4:
                    low_down(n + 1)

        @block.vector
        def _(dve):
            link = chain(dve, "dve_chain")
            nc.vector.sem_inc(S("kv_low"), 4)
            nc.vector.sem_inc(S("s_free"), 2)
            nc.vector.sem_inc(S("exp_done"), 2)
            nc.vector.sem_inc(S("o_staged"), 2)
            nc.vector.sem_inc(S("pv_done"), BUFS)
            nc.vector.sem_inc(S("K_full"), 2)
            for name, n in (("uv_ready", 1), ("primed", 1), ("sin_ready", 2), ("K_staged", 1), ("K_out", 16), ("o_in", 48)):
                nc.vector.sem_inc(S(name), n)
            dve.wait_ge(S("x_in"), 16)
            ln_stats(dve, link, "ln0", x)
            tt = nc.vector.tensor_tensor
            stt = nc.vector.scalar_tensor_tensor
            ts = nc.vector.tensor_scalar
            Ar, Ai, Cr, Ci = (s4[:, n, :] for n in range(4))
            a, w1, th, s2, sn = (sw[:, n, :] for n in range(5))

            def reduce_angle(y, k):
                link(ts(k, y, 1 / (2 * pi), ROUND, ALU.mult, ALU.add))
                link(ts(k, k, ROUND, None, ALU.subtract))
                for part in TWO_PI:
                    link(stt(y, k, -part, y, ALU.mult, ALU.add))
                link(ts(y, y, SIN_MAX, -SIN_MAX, ALU.min, ALU.max))

            def low_keys(i):
                for u in range(4):
                    c, m = 2 * i + u // 2, u % 2
                    dve.wait_ge(S("kv_high"), 4 * i + u + 1)
                    nc.vector.tensor_tensor(k_lo[:, m, c * 512:(c + 1) * 512], bank(u),
                                            k_hi[:, m, c * 512:(c + 1) * 512].bitcast(F32),
                                            ALU.subtract).then_inc(S("kv_low"), 1)

            low_keys(0)
            dve.wait_ge(S("dt_ready"), 1)
            link(tt(sw[:, 0, :], dtb[:, :], Ar, ALU.mult))
            link(tt(dtb[:, :], dtb[:, :], Ai, ALU.mult))
            link(nc.vector.tensor_copy(sn, dtb[:, :]))
            reduce_angle(sn, w1)
            nc.vector.sem_inc(S("step_ready"), 1)
            low_keys(1)
            dve.wait_ge(S("step_funcs"), 1)
            link(ts(w1, th, -1.0, 1.0, ALU.mult, ALU.add))
            link(nc.vector.reciprocal(w1, w1))
            link(stt(th, th, 2.0, w1, ALU.mult, ALU.mult))
            link(tt(s2, s2, s2, ALU.mult))
            link(ts(s2, s2, 2.0, None, ALU.mult))
            link(stt(sn, th, 1.0, sn, ALU.add, ALU.mult))
            link(stt(w1, th, -1.0, s2, ALU.mult, ALU.mult))
            link(tt(w1, w1, th, ALU.add))
            link(tt(th, w1, s2, ALU.subtract))
            link(tt(w1, th, Ar, ALU.mult))
            link(tt(s2, sn, Ai, ALU.mult))
            link(tt(w1, w1, s2, ALU.add))
            low_keys(2)
            link(tt(s2, sn, Ar, ALU.mult))
            link(tt(th, th, Ai, ALU.mult))
            link(tt(s2, s2, th, ALU.subtract))
            link(tt(Ar, Ar, Ar, ALU.mult))
            link(tt(Ai, Ai, Ai, ALU.mult))
            link(tt(Ar, Ar, Ai, ALU.add))
            link(nc.vector.reciprocal(Ar, Ar))
            link(stt(w1, w1, 2.0, Ar, ALU.mult, ALU.mult))
            link(stt(s2, s2, 2.0, Ar, ALU.mult, ALU.mult))
            link(tt(Ar, Cr, w1, ALU.mult))
            link(tt(Ai, Ci, s2, ALU.mult))
            link(tt(th, Ar, Ai, ALU.subtract))
            link(tt(Ar, Cr, s2, ALU.mult))
            link(tt(Ai, Ci, w1, ALU.mult))
            link(tt(Ci, Ar, Ai, ALU.add))
            link(nc.vector.tensor_copy(Cr, th))
            nc.vector.sem_inc(S("dC_ready"), 1)
            low_keys(3)
            for m in range(2):
                dve.wait_ge(S("q_hi_ready"), 2)
                nc.vector.tensor_tensor(q_lo[:, m, :], bank(5)[:, m * T:(m + 1) * T], q_hi[:, m, :].bitcast(F32),
                                        ALU.subtract).then_inc(S("q_lo_ready"), 1)

            def low_values(i, m):
                dve.wait_ge(S("kv_high"), i * 8 + (16 + m + 1))
                v = bank(m % 4).rearrange("p (u h d) -> p u h d", u=2, d=HD)
                for u in range(2):
                    kt = i * 16 + (2 * m + u)
                    last = tt(vst[:, kt, :, HD + 1:2 * HD + 1], v[:, u], vst[:, kt, :, 0:HD].bitcast(F32), ALU.subtract)
                last.then_inc(S("kv_low"), 1)

            bd = lambda v: v.unsqueeze(2).broadcast_to([P, LA, 2 * LA])
            facb = fac[:, :].unsqueeze(1).broadcast_to([P, LA, 2 * LA])
            f = lambda v: v.rearrange("p d j -> p (d j)")

            def angles(i, j):
                n, an, kn = i * 4 + j, phases_of[j % 2], kk[:, j % 2]
                step = [0]

                def then(ins):
                    step[0] += 1
                    ins.then_inc(S("angle_step"), 1)
                    dve.wait_ge(S("angle_step"), n * 6 + step[0])
                dve.wait_ge(S("ang_arg"), n + 1)
                dve.wait_ge(S("sin_ready"), n + 1)
                then(ts(kn, an, 1 / (2 * pi), ROUND, ALU.mult, ALU.add))
                then(ts(kn, kn, ROUND, None, ALU.subtract))
                for part in TWO_PI:
                    then(stt(f(an), f(kn), -part, f(an), ALU.mult, ALU.add))
                then(ts(f(an), f(an), SIN_MAX, -SIN_MAX, ALU.min, ALU.max))
                then(stt(f(kn), f(an), phs[:, 0:1], f(an), ALU.mult, ALU.max))
                stt(an[:, :, 0:LA], an[:, :, 0:LA], phs[:, 1:2], an[:, :, 0:LA], ALU.mult, ALU.max)\
                    .then_inc(S("ang_ready"), 1)

            def products(i, j):
                ds = bass.ds(i * 64 + j * LA, LA)
                n, s = i * 4 + j, j % 2
                dve.wait_ge(S("mag_ready"), n + 1)
                dve.wait_ge(S("sin_ready"), n + 3)
                dve.wait_ge(S("K_full"), n + 1)
                tt(UV[:, s, :, LA:2 * LA], SV[:, :, LA:2 * LA], mag[:, s, :, LA:2 * LA], ALU.mult).then_inc(S("sv_1"), 1)
                tt(SV[:, :, 0:LA], SV[:, :, 0:LA], mag[:, s, :, 0:LA], ALU.mult).then_inc(S("sv_1"), 1)
                dve.wait_ge(S("sv_1"), n * 2 + 2)
                tt(SV[:, :, 0:LA], SV[:, :, 0:LA], bd(s4[:, 2, ds])[:, :, 0:LA], ALU.mult).then_inc(S("sv_mag"), 1)

            angles(0, 0)
            with dve.Fori(0, 2) as i:
                for j in range(4):
                    for m in (2 * j, 2 * j + 1):
                        low_values(i, m)
                    angles(i, j + 1)
                    products(i, j)
            for i in range(2, 4):
                for j in range(4):
                    if (i, j) != (3, 3):
                        angles(i, j + 1)
                    products(i, j)

            def take_max(s, n):
                nc.vector.reduce_max(mxp[:, n, s:s + 1], PS[:, 2 * (s % 2):2 * (s % 2) + 2, :].rearrange("p a b -> p (a b)"),
                                     AX).then_inc(S("s_free"), 1)

            def keep_max(n, h):
                dve.wait_ge(S("s_free"), 8 * h + 8 + 2)
                nc.vector.tensor_reduce(mx[:, n, :], mxp[:, n, :].rearrange("p (t s) -> p t s", t=TT), AX, ALU.max,
                                        negate=True).then_inc(S("m_ready"), 1)

            def split_row(h):
                dve.wait_ge(S("mrow_full"), h + 1)
                dve.wait_ge(S("m_in"), 16 * h)
                nc.vector.tensor_copy(mrow[96:97, 0, :], bank(7)[96:97, 0:T]).then_inc(S("mrow_high"), 1)
                dve.wait_ge(S("mrow_high"), h + 1)
                tt(mrow[96:97, 1, :], bank(7)[96:97, 0:T], mrow[96:97, 0, :].bitcast(F32), ALU.subtract)\
                    .then_inc(S("mrow_ready"), 1)

            def slots(p, first, after, last_pair=False):
                for i in range(first, after):
                    par, j = divmod(i, SLOTS)
                    if (i + DVE_EARLY) % 4 == 3:
                        k = i + DVE_EARLY
                        q = k // 4
                        dve.wait_ge(S("exp_done"), p * 32 + (k + 3))
                        b = k % BUFS
                        nc.vector.tensor_copy(prob_hi[:, b, :], prob[:, b, :]).then_inc(S("high_dve"), 1)
                        dve.wait_ge(S("high_dve"), p * 8 + (q + 1))
                        tt(prob_lo[:, b, :], prob[:, b, :], prob_hi[:, b, :].bitcast(F32), ALU.subtract)\
                            .then_inc(S("low_dve"), 1)
                    if j in S_NEXT and not (last_pair and par == 1):
                        s = S_NEXT[j]
                        dve.wait_ge(S("s_full"), p * 16 + (8 * (par + 1) + s + 1))
                        take_max(s, (par + 1) % 2)
                        if s == 7:
                            keep_max((par + 1) % 2, p * 2 + (par + 1))
                    if j in S_AFTER and not last_pair:
                        s = S_AFTER[j]
                        dve.wait_ge(S("s_full"), p * 16 + (8 * (par + 2) + s + 1))
                        take_max(s, par)
                    if j == M_AT + 1 and not (last_pair and par == 1):
                        split_row(p * 2 + (par + 1))
                    if i == SLOTS + LATE - 1:
                        keep_head(p * 2, 0)

            def keep_head(h, k):
                dve.wait_ge(S("pv_done"), h * SLOTS + (SLOTS + BUFS))
                dve.wait_ge(S("o_in"), h * 48 + 48)
                nc.vector.tensor_copy(ostage[:, k, :], bank(6 + k)[0:2 * HD + 1, 0:T]).then_inc(S("o_staged"), 1)

            for h, n in ((0, 8), (1, 5)):
                for s in range(n):
                    dve.wait_ge(S("s_full"), 8 * h + s + 1)
                    take_max(s, h)
                if h == 0:
                    keep_max(0, 0)
                    dve.wait_ge(S("K_out"), 17 * 16)
                    split_row(0)
            LATE = 3
            slots(0, 0, LATE)
            with dve.Fori(0, PAIRS - 1) as p:
                slots(p, LATE, 2 * SLOTS)
                slots(p + 1, 0, LATE)
                keep_head(p * 2 + 1, 1)
            slots(PAIRS - 1, LATE, 2 * SLOTS, True)

            def finish(m):
                dve.wait_ge(S("o_in"), 48 * (8 * m + 8) + 48)
                link(tt(oh[:, m, :], oh[:, m, :], ol[:, m, :], ALU.add))
                link(nc.vector.reciprocal(osum[:, m, :], osum[:, m, :]))
                tt(zT[:, m, :], oh[:, m, :], osum[:, m, :], ALU.mult).then_inc(S("aT"), 1)

            finish(0)
            keep_head(H - 1, 1)
            finish(1)
            dve.wait_ge(S("x_in"), 32)
            for t in range(TT):
                dve.wait_ge(S("projected"), t + 1)
                tt(x[:, t, :], x[:, t, :], bank(t)[:, 0:D], ALU.add).then_inc(S("x_new"), 1)
            dve.wait_ge(S("x_new"), 2)

            def add_tokens(b, nth, done):
                dve.wait_ge(S("tokens_full"), nth)
                v = bank(b).rearrange("p (t d) -> p t d", t=TT)
                link(tt(x[:, :, :], x[:, :, :], v, ALU.add))
                nc.vector.sem_inc(S(done), 2)

            ln_stats(dve, link, "ln1", x)
            dve.wait_ge(S("qkv_full"), 1)
            dve.wait_ge(S("self_in"), 16 * 5)
            for t in range(TT):
                for c in range(2):
                    last = tt(qkv[:, t, c * 384:(c + 1) * 384], bank(2 * t + c)[:, 0:384], bqkv[:, c * 384:(c + 1) * 384], ALU.add)
            link(last)
            nc.vector.sem_inc(S("attn_step"), 1)

            def scores_sum(n):
                t, half = divmod(n, 2)
                link(nc.vector.tensor_reduce(sc[:, t, half * 128:half * 128 + 128],
                                             prod[:, n % 2, :].rearrange("p (a d) -> p a d", d=HD), AX, ALU.add))

            for n in (0, 2):
                link(tt(*score_products(n), ALU.mult))
                scores_sum(n)
                dve.wait_ge(S("attn_pool"), n // 2 + 1)
                scores_sum(n + 1)
                nc.vector.sem_inc(S("attn_step"), 1)
            s3 = sc[:, :, :].rearrange("p t (h g) -> p (t h) g", g=H)
            st_ = small[:, 96:128]
            bg = st_.unsqueeze(2).broadcast_to([P, 2 * H, H])
            link(nc.vector.tensor_reduce(st_, s3, AX, ALU.max))
            tt(s3, s3, bg, ALU.subtract).then_inc(S("sc_ready"), 1)
            absmax = lambda o, i: nc.vector.tensor_reduce(o, i, AX, ALU.max, apply_absolute_value=True)
            dve.wait_ge(S("wffn_in"), 16 * 7)
            dve.wait_ge(S("wraw_set"), 1)
            nc.vector.tensor_copy(identb[:, :], ident[:, :])
            absmax(small[:, 0:6], wraw[:, 0])
            absmax(small[:, 6:12], wraw[:, 1])
            link(absmax(small[:, 12:14], wdraw[:, :, :]))
            link(ts(small[:, 0:14], small[:, 0:14], 1 / QMAX, None, ALU.mult))
            link(nc.vector.reciprocal(small[:, 16:30], small[:, 0:14]))
            rows_of = [(w[:, i, :], 6 * n + i) for n, w in ((0, wraw[:, 0]), (1, wraw[:, 1])) for i in range(6)]
            rows_of += [(wdraw[:, m, :], 12 + m) for m in range(2)]
            for w, a in rows_of:
                last = ts(w, w, small[:, 16 + a:17 + a], QMAX, ALU.mult, ALU.min)
            link(last)
            flat_w = wraw[:, :, :, :].rearrange("p n i k -> p (n i k)")
            ts(flat_w, flat_w, -QMAX - 1, ROUND, ALU.max, ALU.add)
            link(ts(wdraw[:, :, :], wdraw[:, :, :], -QMAX - 1, ROUND, ALU.max, ALU.add))
            ts(wint[:, :, :, :].rearrange("p n i k -> p (n i k)"), flat_w, ROUND, None, ALU.subtract)
            ts(wdint[:, :, :], wdraw[:, :, :], ROUND, None, ALU.subtract).then_inc(S("wints"), 1)
            dve.wait_ge(S("sc_exp"), 1)
            link(nc.vector.tensor_reduce(st_, s3, AX, ALU.add))
            link(nc.vector.reciprocal(st_, st_))
            link(tt(s3, s3, bg, ALU.mult))
            nc.vector.sem_inc(S("attn_step"), 1)

            def values_sum(n):
                t, half = divmod(n, 2)
                link(nc.vector.tensor_reduce(z[:, t, half * 128:half * 128 + 128],
                                             prod[:, n % 2, :].rearrange("p (a g) -> p a g", g=H), AX, ALU.add))

            for n in (0, 2):
                link(tt(*value_products(n), ALU.mult))
                values_sum(n)
                dve.wait_ge(S("attn_pool"), n // 2 + 3)
                values_sum(n + 1)
                nc.vector.sem_inc(S("attn_step"), 1)
            nc.vector.sem_inc(S("z_ready"), 1)
            dve.wait_ge(S("self_in"), 16 * 5)
            link(tt(x[:, :, :], x[:, :, :], bout[:, :].unsqueeze(1).broadcast_to([P, TT, D]), ALU.add))
            for t in range(TT):
                dve.wait_ge(S("projected"), TT + t + 1)
                tt(x[:, t, :], x[:, t, :], bank(t)[:, 0:D], ALU.add).then_inc(S("x_new"), 1)
            dve.wait_ge(S("x_new"), 4)

            dve.wait_ge(S("clip_exp"), 1)
            link(ts(small[:, 32:34], small[:, 32:34], 1.0, None, ALU.add))
            link(nc.vector.reciprocal(small[:, 32:34], small[:, 32:34]))
            link(ts(small[:, 32:34], small[:, 32:34], 1 / QMAX, None, ALU.mult))
            ln_stats(dve, link, "ln2", x)
            absmax(small[:, 34:35], z[:, :, :].rearrange("p t d -> p (t d)")).then_inc(S("absmax_part"), 1)
            dve.wait_ge(S("absmax_all"), 1)
            link(tt(small[:, 38:39], small[:, 36:37], small[:, 32:33], ALU.mult))
            link(nc.vector.reciprocal(small[:, 54:55], small[:, 38:39]))

            def quantise(to, v, inv, done):
                link(ts(v, v, inv, QMAX, ALU.mult, ALU.min))
                link(ts(v, v, -QMAX - 1, ROUND, ALU.max, ALU.add))
                ts(to, v, ROUND, None, ALU.subtract).then_inc(S(done), 1)

            quantise(z[:, :, :], z[:, :, :], small[:, 54:55], "z_ready")
            link(ts(small[:, 40:52], small[:, 0:12], small[:, 38:39], None, ALU.mult))
            nc.vector.sem_inc(S("comb_ready"), 1)
            link(nc.vector.memset(hf[64:P, 5, :], 0.0))
            for i, r in enumerate(FR):
                dve.wait_ge(S("sg_ready"), i + 1)
                stt(hf[0:r, i, :], bank(i)[0:r, T:2 * T], small[0:r, 46 + i:47 + i], sg[0:r, i, :], ALU.mult, ALU.mult)\
                    .then_inc(S("hf_ready"), 1)
            dve.wait_ge(S("hf_ready"), 6)
            absmax(small[:, 35:36], hf[:, :, :].rearrange("p i t -> p (i t)")).then_inc(S("absmax_part"), 1)
            dve.wait_ge(S("absmax_all"), 2)
            link(tt(small[:, 39:40], small[:, 37:38], small[:, 33:34], ALU.mult))
            link(nc.vector.reciprocal(small[:, 55:56], small[:, 39:40]))
            link(ts(small[:, 56:58], small[:, 12:14], small[:, 39:40], None, ALU.mult))
            quantise(hq[:, :, :], hf[:, :, :], small[:, 55:56], "hq_ready")
            add_tokens(7, 1, "x_new")

            ln_stats(dve, link, "ln3", x)
            link(nc.vector.tensor_copy(xt[:, :, :], z[:, :, :]))
            dve.wait_ge(S("film_in"), 16 * 18)
            link(nc.vector.tensor_copy(tmask[:, :], tmask_u[:, :]))
            link(nc.vector.memset(small[:, 104:112], 1.0))
            link(nc.vector.memset(small[:, 111:112], 2.0 * TOP))
            link(nc.vector.memset(small[:, 114:115], 1.0))
            dve.wait_ge(S("mask8_in"), 4 * 16)
            for h in range(4):
                last = nc.vector.tensor_copy(mask8b[h], mask8[h])
            last.then_inc(S("mask8_ready"), 1)
            in_full = chain(dve, "in_full_chain")
            IN_FULL = 10

            def find(n):
                a, k8 = Asc[:, n % 3, :], m8[:, n % 2, :]
                dve.wait_ge(S("A_copied"), CH * (n + 1))
                for c in range(M // PART):
                    last = nc.vector.max(cand[:, 8 * c:8 * c + 8], a[:, PART * c:PART * (c + 1)])
                link(last)
                for rnd in range(TOP // 8):
                    src, top = cand if rnd == 0 else cand_left, k8[:, 8 * rnd:8 * rnd + 8]
                    link(nc.vector.max(top, src))
                    if rnd < TOP // 8 - 1:
                        link(nc.vector.match_replace(cand_left, top, src, TAKEN))
                parts = lambda v: v.rearrange("p (c k) -> p c k", k=8)
                stt(parts(cand_left), parts(cand), k8[:, TOP - 1:TOP],
                    small[:, 104:112].unsqueeze(1).broadcast_to([P, M // PART, 8]), ALU.is_ge, ALU.mult,
                    accum_out=small[:, 112 + n % 2:113 + n % 2]).then_inc(S("counted"), 1)
                dve.wait_ge(S("counted"), n + 1)

            def search_in_full(n):
                a, b, k8 = Asc[:, n % 3, :], EB[:, n % 2, :], m8[:, n % 2, :]
                for rnd in range(TOP // 8):
                    src, top = a if rnd == 0 else b, k8[:, 8 * rnd:8 * rnd + 8]
                    in_full(nc.vector.max(top, src))
                    in_full(nc.vector.match_replace(b, top, src, TAKEN))
                in_full(ts(b, b, 0.99 * TAKEN, LOW, ALU.is_ge, ALU.mult))
                in_full(tt(a, a, b, ALU.add))

            def settle(n):
                if n >= 2:
                    dve.wait_ge(S("E_scaled"), n - 1)
                    dve.wait_ge(S("E_added"), (n - 2) // 4 * 3 + (n - 2) % 4)
                dve.wait_ge(S("count_full"), n + 1)
                link(nc.vector.tensor_copy(small[96:97, 116:117], bank(7)[96:97, 0:1]))
                total = nc.values_load(small[96:97, 116:117].bitcast(mybir.dt.int32), engines=(mybir.EngineType.DVE,))
                with dve.If(total != ALL_FOUND):
                    search_in_full(n)
                with dve.Else():
                    nc.vector.sem_inc(S("in_full_chain"), IN_FULL)
                ts(small[:, 64 + n % 2:65 + n % 2], m8[:, n % 2, 0:1], -1.0, None, ALU.mult).then_inc(S("top_found"), 1)

            def weigh_top(n):
                t, s = n // 4, n % 2
                dve.wait_ge(S("E_ready"), n + 1)
                link(stt(EB[:, s, :], Asc[:, n % 3, :], m8[:, s, TOP - 1:TOP], EB[:, s, :], ALU.is_ge, ALU.mult,
                         accum_out=small[:, 68 + s:69 + s]))
                nc.vector.sem_inc(S("top_weighed"), 1)
                link(nc.vector.reciprocal(small[:, 68 + s:69 + s], small[:, 68 + s:69 + s]))
                ts(small[:, 66 + s:67 + s], small[:, 68 + s:69 + s], 0.25, tmask[:, t:t + 1], ALU.mult, ALU.mult)\
                    .then_inc(S("r_ready"), 1)

            for n in range(8):
                find(n)
                if n >= 1:
                    weigh_top(n - 1)
                settle(n)
            dve.wait_ge(S("r_ready"), 7)
            dve.wait_ge(S("E_added"), 4)
            link(stt(AM[:, :], EB[:, 0, :], small[:, 66:67], AM[:, :], ALU.mult, ALU.add))
            weigh_top(7)
            dve.wait_ge(S("r_ready"), 8)
            for g in range(8):
                ks = slice(g * 512, (g + 1) * 512)
                stt(AM[:, ks], EB[:, 1, ks], small[:, 67:68], AM[:, ks], ALU.mult, ALU.add).then_inc(S("AM_ready"), 1)

            dve.wait_ge(S("film_in"), 16 * 18)
            for bias in (bfi, bfo):
                link(ts(bias[:, :], bias[:, :], gate[:, 0:1], None, ALU.mult))
                link(ts(bias[:, 0:D], bias[:, 0:D], 1.0, None, ALU.add))
            ln_stats(dve, link, "xin", xt, 0)
            both = lambda v: v.unsqueeze(1).broadcast_to([P, TT, v.shape[-1]])

            def modulation(n, b, bias, full):
                fm = Gh[:, 4 * n:4 * n + 4, :].rearrange("p (t a) d -> p t (a d)", t=TT)
                for t in range(TT):
                    dve.wait_ge(S(full), t + 1)
                    last = stt(fm[:, t, :], bank(b + t), gate[:, 0:1], bias, ALU.mult, ALU.add)
                link(last)
                return fm

            def modulate(v, fm):
                link(tt(v, fm[:, :, 0:D], v, ALU.mult))
                link(tt(v, v, fm[:, :, D:2 * D], ALU.add))

            dve.wait_ge(S("zc_ready"), 2)
            modulate(z[:, :, :], modulation(0, 1, bfi[:, :], "film_in_full"))
            nc.vector.sem_inc(S("conv_ready"), 1)
            link(tt(y[:, :, :], z[:, :, :], both(dskip[:, :]), ALU.mult))
            dve.wait_ge(S("conv_full"), 1)
            re, im = bank(6), bank(7)
            kre, kim = (Kf[:, 2 * n:2 * n + 2, :].rearrange("p a d -> p (a d)") for n in range(2))
            yre, yim = (Yf[:, 2 * n:2 * n + 2, :].rearrange("p a d -> p (a d)") for n in range(2))
            tmp = Gh[:, 0:2, :].rearrange("p a d -> p (a d)")
            link(tt(yre, re, kre, ALU.mult))
            link(tt(tmp, im, kim, ALU.mult))
            link(tt(yre, yre, tmp, ALU.subtract))
            link(tt(yim, re, kim, ALU.mult))
            link(tt(tmp, im, kre, ALU.mult))
            tt(yim, yim, tmp, ALU.add).then_inc(S("conv_ready"), 1)
            fm_out = modulation(1, 3, bfo[:, :], "film_out_full")
            dve.wait_ge(S("conv_full"), 2)
            link(tt(y[:, :, :], y[:, :, :], bank(5).rearrange("p (t d) -> p t d", t=TT), ALU.add))
            modulate(y[:, :, :], fm_out)
            link(tt(xt[:, :, :], xt[:, :, :], y[:, :, :], ALU.add))
            ln_stats(dve, link, "ln4", xt, 2)
            link(tt(xt[:, :, :], xt[:, :, :], both(b2[:, :]), ALU.add))
            dve.wait_ge(S("conv_full"), 3)
            for t in range(TT):
                last = tt(xt[:, t, :], xt[:, t, :], bank(4 + t)[:, 0:D], ALU.add)
            link(last)
            ln_stats(dve, link, "nout", xt, 4)
            link(tt(x[:, :, :], x[:, :, :], z[:, :, :], ALU.add))
            nc.vector.sem_inc(S("x_new"), 2)

            ln_stats(dve, link, "ln5", x)
            dve.wait_ge(S("gru_act"), 2)
            for m in range(2):
                last = nc.vector.tensor_tensor_scan(cT[:, m, :], gt[:, m, :], cd[:, m, :], 0.0, ALU.mult, ALU.add)
            last.then_inc(S("gru_done"), 1)
            add_tokens(2, 2, "x_new")

            ln_stats(dve, link, "ln6", x)
            dve.wait_ge(S("rest_in"), 16 * 6)
            dve.wait_ge(S("z_high"), 1)
            tt(z_part[:, 1], zT[:, :, :], z_part[:, 0].bitcast(F32), ALU.subtract).then_inc(S("z_low"), 1)
            dve.wait_ge(S("rscores"), 1)
            link(tt(rt[:, 1, :, :], rt[:, 0, :, :], both(rbias[:, :]), ALU.add))
            for t in range(TT):
                k8 = small[:, 72 + 8 * t:80 + 8 * t]
                link(nc.vector.max(k8, rt[:, 1, t, :]))
                link(nc.vector.match_replace(rt[:, 2, t, :], k8, rt[:, 1, t, :], -3e38))
            link(tt(rt[:, 2, :, :], rt[:, 2, :, :], rt[:, 1, :, :], ALU.not_equal))
            link(tt(rt[:, 2, :, :], rt[:, 2, :, :], rt[:, 0, :, :], ALU.mult))
            link(nc.vector.tensor_reduce(small[:, 88:90], rt[:, 2, :, :], AX, ALU.add))
            link(ts(small[:, 88:90], small[:, 88:90], 1e-20, None, ALU.add))
            link(nc.vector.reciprocal(small[:, 88:90], small[:, 88:90]))
            for t in range(TT):
                last = ts(wtok[:, t, 0:E], rt[:, 2, t, :], small[:, 88 + t:89 + t], 2.5, ALU.mult, ALU.mult)
            link(last)
            link(nc.vector.tensor_copy(wtok[:, :, E:2 * E], wtok[:, :, 0:E]))
            tt(pick[:, :], ident[0:2 * E, 0:E], ident[0:2 * E, E:2 * E], ALU.add).then_inc(S("wtok"), 1)
            def low_h(n):
                dve.wait_ge(S("h_high"), n + 1)
                tt(h_part[:, n % 3, 1], hw[:, n % 2, :], h_part[:, n % 3, 0].bitcast(F32), ALU.subtract)\
                    .then_inc(S("h_low"), 1)

            for n in range(E + 4):
                b, up = n % 2, bank(n % 3)[:, T:2 * T]
                if n >= 1:
                    low_h(n - 1)
                if n == 2:
                    dve.wait_ge(S("wT_ready"), 1)
                    tt(wT[E:2 * E, :], bank(7)[E:2 * E, 0:T], wT[E:2 * E, :].bitcast(F32), ALU.subtract)\
                        .then_inc(S("wT_ready"), 1)
                dve.wait_ge(S("unit_silu"), n + 1)
                if n < 4:
                    tt(hw[:, b, :], up, esg[:, b, :], ALU.mult).then_inc(S("unit_ready"), 1)
                else:
                    link(ts(euc[:, b, :], up, 7.0, -7.0, ALU.min, ALU.max))
                    link(stt(euc[:, b, :], esg[:, b, :], SILU7, euc[:, b, :], ALU.min, ALU.mult))
                    tt(hw[:, b, :], euc[:, b, :], bank(WEIGHT_BANK[n % 3])[:, 0:T], ALU.mult).then_inc(S("unit_ready"), 1)
                dve.wait_ge(S("unit_ready"), n + 1)
                nc.vector.sem_inc(S("unit_read"), 1)
            low_h(E + 3)
            dve.wait_ge(S("unit_done"), E + 4)
            for t in range(TT):
                tt(x[:, t, :], x[:, t, :], bank(4 + t)[:, 0:D], ALU.add).then_inc(S("x_new"), 1)


def laid_out(inputs):
    import numpy as np

    i = {name: np.asarray(a) for name, a in inputs.items()}
    turned = lambda a: np.ascontiguousarray(a.T)
    flags = lambda a: np.ascontiguousarray(a).view(np.uint8)
    a = {name: i[name] for name in (
        "L0_xattn_Wq", "L0_xattn_Wk", "L0_xattn_Wv", "L0_xattn_Wo", "L0_attn_W_qkv", "L0_attn_b_qkv", "L0_attn_W_out",
        "L0_attn_b_out", "L0_ffn_clip_x", "L0_ffn_clip_down", "L0_ffn_w_gate", "L0_ffn_w_up", "L0_ffn_w_down",
        "L1_xattn_Wq", "L1_xattn_Wk", "L1_xattn_Wv", "L1_xattn_W_film_in", "L1_xattn_b_film_in", "L1_xattn_W_film_out",
        "L1_xattn_b_film_out", "L1_xattn_g_norm_in", "L1_xattn_b_norm_in", "L1_xattn_g_norm_out", "L1_xattn_b_norm_out",
        "L1_xattn_g_ffn", "L1_xattn_b_ffn", "L1_xattn_W1", "L1_xattn_W2", "L1_xattn_b2", "L1_xattn_log_dt",
        "L1_xattn_D_skip", "L1_ffn_e_score_correction_bias")}
    a["L1_xattn_mod_gate"] = i["L1_xattn_mod_gate"].reshape(1)
    a["x"] = i["x"][0]
    a["ctx"] = i["ctx_768"][0]
    a["ctxT"] = turned(i["ctx_768"][0])
    a["ctx_mask"] = flags(i["mask_BxS2_bf1"][0])
    a["text_mask"] = turned(flags(i["mask_BxS_bf1"][0]).reshape(TT, P))
    for name in ("A_re", "A_im", "C_re", "C_im"):
        a[name + "T"] = turned(i["L1_xattn_" + name])
    a["b1T"] = turned(i["L1_xattn_b1"].reshape(8, P))
    for name in ("g", "c"):
        a[f"W{name}T"] = turned(i["L1_attn_W" + name])
        a[f"b{name}T"] = turned(i["L1_attn_b" + name].reshape(2, P))
    a["routerT"] = turned(i["L1_ffn_router_weight"])
    a["gupT"] = np.ascontiguousarray(i["L1_ffn_gate_up_proj"].reshape(E, 2 * I, 2, P).transpose(3, 0, 2, 1))
    a["downT"] = np.ascontiguousarray(i["L1_ffn_down_proj"].transpose(2, 0, 1))
    both = np.stack([i["L1_ffn_shared_gate"], i["L1_ffn_shared_up"]])
    a["sguT"] = np.ascontiguousarray(both.reshape(2, 512, 2, P).transpose(3, 2, 0, 1).reshape(P, -1))
    a["sdnT"] = np.ascontiguousarray(i["L1_ffn_shared_down"].reshape(D, 4, P).transpose(2, 1, 0).reshape(P, -1))

    a["ident"] = np.eye(P, dtype=np.float32)
    j = np.arange(LA, dtype=np.float32)
    a["lfac"] = np.tile(np.concatenate([LA * j, j]), (P, 1))
    phase = np.zeros((P, 8), np.float32)
    phase[:NS, 0], phase[NS:, 0] = -1, 1
    phase[:NS, 1], phase[NS:, 1] = 1, -1
    phase[:NS, 3] = phase[NS:, 4] = np.pi / 2
    a["phase"] = phase
    angle = np.outer(np.arange(T), (np.arange(T) + 0.5) * (np.pi / T))
    table = np.concatenate([np.cos(angle), -np.sin(angle)], 1)
    a["dft"] = table.astype(np.float32)
    a["dftT"] = turned((table / T).astype(np.float32))
    return a


def kernel(**inputs):
    import numpy as np
    import concourse.bacc as bacc
    from concourse import mybir
    from concourse.bass_utils import run_bass_kernel_spmd

    nc = bacc.Bacc("TRN2", target_bir_lowering=False, num_devices=1)
    arrays, A = {}, {}
    for name, a in laid_out(inputs).items():
        a = np.ascontiguousarray(a)
        arrays[f"in_{name}_dram"] = a
        A[name] = nc.dram_tensor(f"in_{name}_dram", a.shape, mybir.dt.from_np(a.dtype), kind="ExternalInput").ap()
    out = nc.dram_tensor("out_0_dram", (1, T, D), F32, kind="ExternalOutput").ap()
    perceiver_kernel(nc, A, out[0])
    r = run_bass_kernel_spmd(nc, [arrays], core_ids=[0])
    return r.results[0]["out_0_dram"]
```
